# Optimizing a Trainium2 kernel written in Bass

```python
import numpy as np
import jax
import jax.numpy as jnp

def _softmax(x, axis=-1):
    return jax.nn.softmax(x, axis=axis)

def _gelu(x):
    return jax.nn.gelu(x, approximate=True)

def _silu(x):
    return jax.nn.silu(x)

def _sigmoid(x):
    return jax.nn.sigmoid(x)

def _layernorm(x, axis=-1, eps=1e-05):
    m = jnp.mean(x, axis=axis, keepdims=True)
    v = jnp.var(x, axis=axis, keepdims=True)
    return (x - m) / jnp.sqrt(v + eps)

def _scatter_add(tgt, idx, src, axis=0):
    return tgt.at[idx].add(src)

def _segment_sum(src, seg, n):
    return jax.ops.segment_sum(src, seg, n)
kernel_name = 'mk_perceiver_d2_seqx_r2_98d705'

def setup_inputs(seed: int=0):
    np.random.seed(seed)
    _w = jnp.asarray

    def _rec_inputs():
        import jax
        import jax.numpy as jnp
        _rk = jax.random.key(seed)
        x = -0.0002928 + 1 * jax.random.normal(jax.random.fold_in(_rk, 1), (4, 128, 512), jnp.float32)
        _lenS = 128 - jax.random.randint(jax.random.fold_in(_rk, 7), (4,), 0, max(1, 128 // 4) + 1, jnp.int32)
        _lenS2 = 2048 - jax.random.randint(jax.random.fold_in(_rk, 8), (4,), 0, max(1, 2048 // 4) + 1, jnp.int32)
        _ctx_1024P = jax.random.normal(jax.random.fold_in(_rk, 11), (4, 16, 512), jnp.float32)
        _ctx_1024c = jax.random.dirichlet(jax.random.fold_in(_rk, 511), 0.3 * jnp.ones((16,), jnp.float32), (4, 2048))
        _ctx_1024t = jnp.einsum('bsk,bkd->bsd', _ctx_1024c, _ctx_1024P)
        _ctx_1024t = _ctx_1024t * jax.lax.rsqrt(jnp.mean(jnp.square(_ctx_1024t)) + 1e-12) * 0.953939
        ctx_1024 = -1.39393e-06 + 0.999914 * (_ctx_1024t + 0.3 * jax.random.normal(jax.random.fold_in(_rk, 611), (4, 2048, 512), jnp.float32))
        _validS = jnp.arange(128)[None, :] < _lenS[:, None]
        _validS2 = jnp.arange(2048)[None, :] < _lenS2[:, None]
        _causal = jnp.tril(jnp.ones((128, 128), dtype=bool))
        mask_1x1xSxS2_bk0 = jnp.logical_not(jnp.broadcast_to(_validS2[0:1, None, None, :], (1, 1, 128, 2048)))
        return (x, ctx_1024, mask_1x1xSxS2_bk0)
    x, ctx_1024, mask_1x1xSxS2_bk0 = _rec_inputs()

    def _L0_xattn_setup():
        import jax, jax.numpy as jnp
        import numpy as np
        D_MODEL = 512
        NUM_HEADS = 16
        D_K = D_MODEL // NUM_HEADS
        B, L = (2, 1024)
        NEG = -1000000000.0

        def _split_heads(x):
            b, l, _ = x.shape
            return x.reshape(b, l, NUM_HEADS, D_K).transpose(0, 2, 1, 3)
        key = jax.random.key(seed)
        ks = jax.random.split(key, 11)
        s = 1.0 / np.sqrt(D_MODEL)
        inp = {'Q': jax.random.normal(ks[0], (B, L, D_MODEL), jnp.float32), 'K': jax.random.normal(ks[1], (B, L, D_MODEL), jnp.float32), 'V': jax.random.normal(ks[2], (B, L, D_MODEL), jnp.float32), 'mask': jnp.tril(jnp.ones((L, L), bool))[None, None], 'Wq': jax.random.normal(ks[3], (D_MODEL, D_MODEL), jnp.float32) * s, 'bq': jnp.zeros((D_MODEL,), jnp.float32), 'Wk': jax.random.normal(ks[4], (D_MODEL, D_MODEL), jnp.float32) * s, 'bk': jnp.zeros((D_MODEL,), jnp.float32), 'Wv': jax.random.normal(ks[5], (D_MODEL, D_MODEL), jnp.float32) * s, 'bv': jnp.zeros((D_MODEL,), jnp.float32), 'Wo': jax.random.normal(ks[6], (D_MODEL, D_MODEL), jnp.float32) * s, 'bo': jnp.zeros((D_MODEL,), jnp.float32)}
        return inp
    _L0_xattn_all = _L0_xattn_setup()
    _L0_xattn_in = {k: v for k, v in _L0_xattn_all.items() if k in ('Wq', 'bq', 'Wk', 'bk', 'Wv', 'bv', 'Wo', 'bo')}
    del _L0_xattn_all

    def _L0_attn_setup():
        import jax, jax.numpy as jnp
        import numpy as np
        N_HEAD = 8
        HEAD = 64
        RATIO = 2
        DEG = 2
        N_EMBD = 512
        QKV = (RATIO + 2) * N_HEAD * HEAD

        def _rope(t):
            B, T, h, d = t.shape
            div = 2.0 * np.pi / float(T) ** (np.arange(0, d, 2, dtype=np.float32) / d)
            ang = jnp.arange(T, dtype=jnp.float32)[:, None] * jnp.asarray(div)[None, :]
            sin = jnp.repeat(jnp.sin(ang), 2, axis=-1)[None, :, None, :]
            cos = jnp.repeat(jnp.cos(ang), 2, axis=-1)[None, :, None, :]
            x1 = t[..., ::2]
            x2 = t[..., 1::2]
            rot = jnp.stack((-x2, x1), axis=-1).reshape(t.shape)
            return t * cos + rot * sin
        key = jax.random.key(seed)
        k1, k2, k3 = jax.random.split(key, 3)
        B, T = (1, 1024)
        x = jax.random.normal(k1, (B, T, N_EMBD), dtype=jnp.float32)
        w_attn = jax.random.normal(k2, (N_EMBD, QKV + N_HEAD), dtype=jnp.float32) * N_EMBD ** (-0.5)
        w_proj = jax.random.normal(k3, (RATIO * N_HEAD * HEAD, N_EMBD), dtype=jnp.float32) * (RATIO * N_HEAD * HEAD) ** (-0.5)
        ln_w = jnp.ones((HEAD,), dtype=jnp.float32)
        return {'x': x, 'w_attn': w_attn, 'w_proj': w_proj, 'ln_w': ln_w}
    _L0_attn_all = _L0_attn_setup()
    _L0_attn_in = {k: v for k, v in _L0_attn_all.items() if k in ('w_attn', 'w_proj', 'ln_w')}
    del _L0_attn_all

    def _L0_ffn_setup():
        import jax, jax.numpy as jnp
        import numpy as np
        EMB, HID, E, TOPK = (512, 2048, 8, 2)
        key = jax.random.key(seed)
        ks = jax.random.split(key, 10)
        s = 0.02
        return {'x': jax.random.normal(ks[0], (4, 1024, EMB), jnp.float32), 'rw1': s * jax.random.normal(ks[1], (EMB, HID), jnp.float32), 'rb1': jnp.zeros((HID,), jnp.float32), 'rw2': s * jax.random.normal(ks[2], (HID, E), jnp.float32), 'rb2': jnp.zeros((E,), jnp.float32), 'w1': s * jax.random.normal(ks[3], (E, EMB, HID), jnp.float32), 'b1': jnp.zeros((E, HID), jnp.float32), 'w2': s * jax.random.normal(ks[4], (E, HID, EMB), jnp.float32), 'b2': jnp.zeros((E, EMB), jnp.float32)}
    _L0_ffn_all = _L0_ffn_setup()
    _L0_ffn_in = {k: v for k, v in _L0_ffn_all.items() if k in ('rw1', 'rb1', 'rw2', 'rb2', 'w1', 'b1', 'w2', 'b2')}
    del _L0_ffn_all

    def _L1_xattn_setup():
        import jax, jax.numpy as jnp
        import numpy as np
        DIM = 512
        H = 16
        HD = DIM // H
        EPS = 1e-05
        key = jax.random.key(seed)
        ks = jax.random.split(key, 12)
        B, S = (4, 1024)
        s = 0.02
        return {'q': jax.random.normal(ks[0], (B, S, DIM), jnp.float32), 'k': jax.random.normal(ks[1], (B, S, DIM), jnp.float32), 'v': jax.random.normal(ks[2], (B, S, DIM), jnp.float32), 'Wq': jax.random.normal(ks[3], (DIM, DIM), jnp.float32) * s, 'bq': jnp.zeros((DIM,), jnp.float32), 'Wk': jax.random.normal(ks[4], (DIM, DIM), jnp.float32) * s, 'bk': jnp.zeros((DIM,), jnp.float32), 'Wv': jax.random.normal(ks[5], (DIM, DIM), jnp.float32) * s, 'bv': jnp.zeros((DIM,), jnp.float32), 'Wo': jax.random.normal(ks[6], (DIM, DIM), jnp.float32) * s, 'bo': jnp.zeros((DIM,), jnp.float32), 'gamma': jnp.ones((DIM,), jnp.float32), 'beta': jnp.zeros((DIM,), jnp.float32)}
    _L1_xattn_all = _L1_xattn_setup()
    _L1_xattn_in = {k: v for k, v in _L1_xattn_all.items() if k in ('Wq', 'bq', 'Wk', 'bk', 'Wv', 'bv', 'Wo', 'bo', 'gamma', 'beta')}
    del _L1_xattn_all

    def _L1_attn_setup():
        import jax, jax.numpy as jnp
        import numpy as np
        D_MODEL = 512
        BATCH = 8
        SEQ = 1024
        LN_EPS = 1e-05

        def _layernorm(z, w, b):
            m = jnp.mean(z, axis=-1, keepdims=True)
            v = jnp.mean(jnp.square(z - m), axis=-1, keepdims=True)
            return (z - m) * jax.lax.rsqrt(v + LN_EPS) * w + b

        def _reference_tuple_inner(x, ln_w, ln_b, tmk, tmv, tmr, decay_w, Wk, Wv, Wr, Wo):
            xn = _layernorm(x, ln_w, ln_b)
            prev = jnp.pad(xn[:, :-1, :], ((0, 0), (1, 0), (0, 0)))
            xk = xn * tmk + prev * (1.0 - tmk)
            xv = xn * tmv + prev * (1.0 - tmv)
            xr = xn * tmr + prev * (1.0 - tmr)
            k = jnp.einsum('btd,ed->bte', xk, Wk)
            v = jnp.einsum('btd,ed->bte', xv, Wv)
            r = jax.nn.sigmoid(jnp.einsum('btd,ed->bte', xr, Wr))
            decay = jax.nn.sigmoid(decay_w)
            kv = (k * v).swapaxes(0, 1)

            def step(S, kv_t):
                S_new = decay * S + kv_t
                return (S_new, S_new)
            S0 = jnp.zeros((x.shape[0], x.shape[2]), x.dtype)
            final_S, S_seq = jax.lax.scan(step, S0, kv)
            S_seq = S_seq.swapaxes(0, 1)
            out = x + r * jnp.einsum('btd,ed->bte', S_seq, Wo)
            return (out, final_S, S_seq)
        key = jax.random.key(seed)
        ks = jax.random.split(key, 8)
        scale = 0.1 / np.sqrt(D_MODEL)
        x = jax.random.normal(ks[0], (BATCH, SEQ, D_MODEL), dtype=jnp.float32)
        return {'x': x, 'ln_w': jnp.ones((D_MODEL,), jnp.float32), 'ln_b': jnp.zeros((D_MODEL,), jnp.float32), 'tmk': jnp.ones((D_MODEL,), jnp.float32) * 0.9, 'tmv': jnp.ones((D_MODEL,), jnp.float32) * 0.9, 'tmr': jnp.ones((D_MODEL,), jnp.float32) * 0.9, 'decay_w': jnp.full((D_MODEL,), -0.5, jnp.float32) + 0.1 * jax.random.normal(ks[1], (D_MODEL,), jnp.float32), 'Wk': scale * jax.random.normal(ks[2], (D_MODEL, D_MODEL), jnp.float32), 'Wv': scale * jax.random.normal(ks[3], (D_MODEL, D_MODEL), jnp.float32), 'Wr': scale * jax.random.normal(ks[4], (D_MODEL, D_MODEL), jnp.float32), 'Wo': scale * jax.random.normal(ks[5], (D_MODEL, D_MODEL), jnp.float32)}
    _L1_attn_all = _L1_attn_setup()
    _L1_attn_in = {k: v for k, v in _L1_attn_all.items() if k in ('ln_w', 'ln_b', 'tmk', 'tmv', 'tmr', 'decay_w', 'Wk', 'Wv', 'Wr', 'Wo')}
    del _L1_attn_all

    def _L1_ffn_setup():
        import jax, jax.numpy as jnp
        import numpy as np
        EMBED = 512
        NUM_EXPERTS = 8
        TOP_K = 2
        key = jax.random.key(seed)
        ks = jax.random.split(key, 6)
        scale = EMBED ** (-0.5)
        return {'x': jax.random.normal(ks[0], (4, 2048, EMBED), jnp.float32), 'router_w': jax.random.normal(ks[1], (EMBED, NUM_EXPERTS), jnp.float32) * scale, 'router_b': jnp.zeros((NUM_EXPERTS,), jnp.float32), 'we_gate': jax.random.normal(ks[2], (NUM_EXPERTS, EMBED, EMBED), jnp.float32) * scale, 'we_up': jax.random.normal(ks[3], (NUM_EXPERTS, EMBED, EMBED), jnp.float32) * scale, 'we_down': jax.random.normal(ks[4], (NUM_EXPERTS, EMBED, EMBED), jnp.float32) * scale}
    _L1_ffn_all = _L1_ffn_setup()
    _L1_ffn_in = {k: v for k, v in _L1_ffn_all.items() if k in ('router_w', 'router_b', 'we_gate', 'we_up', 'we_down')}
    del _L1_ffn_all
    return {'x': x, 'ctx_1024': ctx_1024, 'mask_1x1xSxS2_bk0': mask_1x1xSxS2_bk0, 'L0_xattn_Wq': _L0_xattn_in['Wq'], 'L0_xattn_bq': _L0_xattn_in['bq'], 'L0_xattn_Wk': _L0_xattn_in['Wk'], 'L0_xattn_bk': _L0_xattn_in['bk'], 'L0_xattn_Wv': _L0_xattn_in['Wv'], 'L0_xattn_bv': _L0_xattn_in['bv'], 'L0_xattn_Wo': _L0_xattn_in['Wo'], 'L0_xattn_bo': _L0_xattn_in['bo'], 'L0_attn_w_attn': _L0_attn_in['w_attn'], 'L0_attn_w_proj': _L0_attn_in['w_proj'], 'L0_attn_ln_w': _L0_attn_in['ln_w'], 'L0_ffn_rw1': _L0_ffn_in['rw1'], 'L0_ffn_rb1': _L0_ffn_in['rb1'], 'L0_ffn_rw2': _L0_ffn_in['rw2'], 'L0_ffn_rb2': _L0_ffn_in['rb2'], 'L0_ffn_w1': _L0_ffn_in['w1'], 'L0_ffn_b1': _L0_ffn_in['b1'], 'L0_ffn_w2': _L0_ffn_in['w2'], 'L0_ffn_b2': _L0_ffn_in['b2'], 'L1_xattn_Wq': _L1_xattn_in['Wq'], 'L1_xattn_bq': _L1_xattn_in['bq'], 'L1_xattn_Wk': _L1_xattn_in['Wk'], 'L1_xattn_bk': _L1_xattn_in['bk'], 'L1_xattn_Wv': _L1_xattn_in['Wv'], 'L1_xattn_bv': _L1_xattn_in['bv'], 'L1_xattn_Wo': _L1_xattn_in['Wo'], 'L1_xattn_bo': _L1_xattn_in['bo'], 'L1_xattn_gamma': _L1_xattn_in['gamma'], 'L1_xattn_beta': _L1_xattn_in['beta'], 'L1_attn_ln_w': _L1_attn_in['ln_w'], 'L1_attn_ln_b': _L1_attn_in['ln_b'], 'L1_attn_tmk': _L1_attn_in['tmk'], 'L1_attn_tmv': _L1_attn_in['tmv'], 'L1_attn_tmr': _L1_attn_in['tmr'], 'L1_attn_decay_w': _L1_attn_in['decay_w'], 'L1_attn_Wk': _L1_attn_in['Wk'], 'L1_attn_Wv': _L1_attn_in['Wv'], 'L1_attn_Wr': _L1_attn_in['Wr'], 'L1_attn_Wo': _L1_attn_in['Wo'], 'L1_ffn_router_w': _L1_ffn_in['router_w'], 'L1_ffn_router_b': _L1_ffn_in['router_b'], 'L1_ffn_we_gate': _L1_ffn_in['we_gate'], 'L1_ffn_we_up': _L1_ffn_in['we_up'], 'L1_ffn_we_down': _L1_ffn_in['we_down']}

def reference(x, ctx_1024, mask_1x1xSxS2_bk0, L0_xattn_Wq, L0_xattn_bq, L0_xattn_Wk, L0_xattn_bk, L0_xattn_Wv, L0_xattn_bv, L0_xattn_Wo, L0_xattn_bo, L0_attn_w_attn, L0_attn_w_proj, L0_attn_ln_w, L0_ffn_rw1, L0_ffn_rb1, L0_ffn_rw2, L0_ffn_rb2, L0_ffn_w1, L0_ffn_b1, L0_ffn_w2, L0_ffn_b2, L1_xattn_Wq, L1_xattn_bq, L1_xattn_Wk, L1_xattn_bk, L1_xattn_Wv, L1_xattn_bv, L1_xattn_Wo, L1_xattn_bo, L1_xattn_gamma, L1_xattn_beta, L1_attn_ln_w, L1_attn_ln_b, L1_attn_tmk, L1_attn_tmv, L1_attn_tmr, L1_attn_decay_w, L1_attn_Wk, L1_attn_Wv, L1_attn_Wr, L1_attn_Wo, L1_ffn_router_w, L1_ffn_router_b, L1_ffn_we_gate, L1_ffn_we_up, L1_ffn_we_down):
    import jax
    import jax.numpy as jnp

    def _L0_xattn_ref(Q, K, V, mask, Wq, bq, Wk, bk, Wv, bv, Wo, bo):
        import jax, jax.numpy as jnp
        import numpy as np
        D_MODEL = 512
        NUM_HEADS = 16
        D_K = D_MODEL // NUM_HEADS
        B, L = (2, 1024)
        NEG = -1000000000.0

        def _split_heads(x):
            b, l, _ = x.shape
            return x.reshape(b, l, NUM_HEADS, D_K).transpose(0, 2, 1, 3)
        q = _split_heads(Q @ Wq.T + bq)
        k = _split_heads(K @ Wk.T + bk)
        v = _split_heads(V @ Wv.T + bv)
        scores = jnp.einsum('bhqd,bhkd->bhqk', q, k) / jnp.sqrt(jnp.float32(D_K))
        scores = jnp.where(mask, scores, NEG)
        probs = jax.nn.softmax(scores, axis=-1)
        attn = jnp.einsum('bhqk,bhkd->bhqd', probs, v)
        b, h, l, dk = attn.shape
        o_in = attn.transpose(0, 2, 1, 3).reshape(b, l, D_MODEL)
        return o_in @ Wo.T + bo

    def _L0_attn_ref(x, w_attn, w_proj, ln_w):
        import jax, jax.numpy as jnp
        import numpy as np
        N_HEAD = 8
        HEAD = 64
        RATIO = 2
        DEG = 2
        N_EMBD = 512
        QKV = (RATIO + 2) * N_HEAD * HEAD

        def _rope(t):
            B, T, h, d = t.shape
            div = 2.0 * np.pi / float(T) ** (np.arange(0, d, 2, dtype=np.float32) / d)
            ang = jnp.arange(T, dtype=jnp.float32)[:, None] * jnp.asarray(div)[None, :]
            sin = jnp.repeat(jnp.sin(ang), 2, axis=-1)[None, :, None, :]
            cos = jnp.repeat(jnp.cos(ang), 2, axis=-1)[None, :, None, :]
            x1 = t[..., ::2]
            x2 = t[..., 1::2]
            rot = jnp.stack((-x2, x1), axis=-1).reshape(t.shape)
            return t * cos + rot * sin
        B, T, C = x.shape
        h, d, r = (N_HEAD, HEAD, RATIO)
        hq = r * h
        qkvg = x @ w_attn
        q = qkvg[..., :hq * d].reshape(B, T, hq, d)
        k = qkvg[..., hq * d:(hq + h) * d].reshape(B, T, h, d)
        v = qkvg[..., (hq + h) * d:QKV].reshape(B, T, h, d)
        log_g = jax.nn.log_sigmoid(6.906768 + qkvg[..., QKV:])
        q = _rope(q)
        k = _rope(k)
        k = jnp.repeat(k, r, axis=2)
        v = jnp.repeat(v, r, axis=2)
        log_G = jnp.repeat(jnp.cumsum(log_g, axis=1), r, axis=2).transpose(0, 2, 1)
        scale = 1.0 / d ** 0.5
        s = jnp.einsum('bthd,bshd->bhts', q, k) * scale
        logits = DEG * jnp.log(jnp.abs(s) + 1e-30) + log_G[:, :, :, None] - log_G[:, :, None, :]
        mask = jnp.tril(jnp.ones((T, T), dtype=bool))
        logits = jnp.where(mask, logits, -jnp.inf)
        m = jax.lax.stop_gradient(jnp.max(logits, axis=-1, keepdims=True))
        a = jnp.exp(logits - m)
        if DEG % 2 == 1:
            a = a * jnp.sign(s)
        a = jnp.where(mask, a, 0.0)
        num = jnp.einsum('bhts,bshd->bthd', a, v)
        den = jnp.sum(a, axis=-1).transpose(0, 2, 1)
        y = num / (den[..., None] + 1e-06)
        mu = jnp.mean(y, axis=-1, keepdims=True)
        var = jnp.mean((y - mu) ** 2, axis=-1, keepdims=True)
        y = (y - mu) / jnp.sqrt(var + 1e-09) * ln_w
        return y.reshape(B, T, hq * d) @ w_proj

    def _L0_ffn_ref(x, rw1, rb1, rw2, rb2, w1, b1, w2, b2):
        import jax, jax.numpy as jnp
        import numpy as np
        EMB, HID, E, TOPK = (512, 2048, 8, 2)
        B, S, D = x.shape
        logits = jax.nn.silu(jnp.einsum('bsd,dh->bsh', x, rw1) + rb1)
        logits = jnp.einsum('bsh,he->bse', logits, rw2) + rb2
        k_logits, k_index = jax.lax.top_k(logits, TOPK)
        k_prob = jax.nn.softmax(k_logits, axis=-1)
        xf = x.reshape(B * S, D)
        k_index_f = k_index.reshape(B * S, TOPK)
        k_prob_f = k_prob.reshape(B * S, TOPK)
        out = jnp.zeros_like(xf)
        for e in range(E):
            we = jnp.sum(jnp.where(k_index_f == e, k_prob_f, 0.0), axis=-1)
            h = jax.nn.silu(xf @ w1[e] + b1[e]) @ w2[e] + b2[e]
            out = out + we[:, None] * h
        return out.reshape(B, S, D)

    def _L1_xattn_ref(q, k, v, Wq, bq, Wk, bk, Wv, bv, Wo, bo, gamma, beta):
        import jax, jax.numpy as jnp
        import numpy as np
        DIM = 512
        H = 16
        HD = DIM // H
        EPS = 1e-05
        B, S, _ = q.shape
        scale = HD ** (-0.5)

        def proj(x, W, b):
            return (x @ W.T + b).reshape(B, -1, H, HD).transpose(0, 2, 1, 3)
        qh = proj(q, Wq, bq)
        kh = proj(k, Wk, bk)
        vh = proj(v, Wv, bv)
        scores = jnp.einsum('bhsd,bhtd->bhst', qh, kh) * scale
        attn = jax.nn.softmax(scores, axis=-1)
        out = jnp.einsum('bhst,bhtd->bhsd', attn, vh)
        out = out.transpose(0, 2, 1, 3).reshape(B, S, DIM)
        out = out @ Wo.T + bo
        mu = out.mean(-1, keepdims=True)
        var = out.var(-1, keepdims=True)
        return (out - mu) * jax.lax.rsqrt(var + EPS) * gamma + beta

    def _L1_attn_ref(x, ln_w, ln_b, tmk, tmv, tmr, decay_w, Wk, Wv, Wr, Wo):
        import jax, jax.numpy as jnp
        import numpy as np
        D_MODEL = 512
        BATCH = 8
        SEQ = 1024
        LN_EPS = 1e-05

        def _layernorm(z, w, b):
            m = jnp.mean(z, axis=-1, keepdims=True)
            v = jnp.mean(jnp.square(z - m), axis=-1, keepdims=True)
            return (z - m) * jax.lax.rsqrt(v + LN_EPS) * w + b

        def _reference_tuple_inner(x, ln_w, ln_b, tmk, tmv, tmr, decay_w, Wk, Wv, Wr, Wo):
            xn = _layernorm(x, ln_w, ln_b)
            prev = jnp.pad(xn[:, :-1, :], ((0, 0), (1, 0), (0, 0)))
            xk = xn * tmk + prev * (1.0 - tmk)
            xv = xn * tmv + prev * (1.0 - tmv)
            xr = xn * tmr + prev * (1.0 - tmr)
            k = jnp.einsum('btd,ed->bte', xk, Wk)
            v = jnp.einsum('btd,ed->bte', xv, Wv)
            r = jax.nn.sigmoid(jnp.einsum('btd,ed->bte', xr, Wr))
            decay = jax.nn.sigmoid(decay_w)
            kv = (k * v).swapaxes(0, 1)

            def step(S, kv_t):
                S_new = decay * S + kv_t
                return (S_new, S_new)
            S0 = jnp.zeros((x.shape[0], x.shape[2]), x.dtype)
            final_S, S_seq = jax.lax.scan(step, S0, kv)
            S_seq = S_seq.swapaxes(0, 1)
            out = x + r * jnp.einsum('btd,ed->bte', S_seq, Wo)
            return (out, final_S, S_seq)
        return _reference_tuple_inner(x, ln_w, ln_b, tmk, tmv, tmr, decay_w, Wk, Wv, Wr, Wo)[0]

    def _L1_ffn_ref(x, router_w, router_b, we_gate, we_up, we_down):
        import jax, jax.numpy as jnp
        import numpy as np
        EMBED = 512
        NUM_EXPERTS = 8
        TOP_K = 2
        x_shape = x.shape
        x_flat = x.reshape(-1, x_shape[-1])
        num_tokens = x_flat.shape[0]
        router_logits = x_flat @ router_w + router_b
        topk_weights, topk_indices = jax.lax.top_k(router_logits, k=TOP_K)
        topk_weights = jax.nn.softmax(topk_weights, axis=-1)
        token_idx_mesh = jnp.repeat(jnp.arange(num_tokens), TOP_K)
        expert_idx_mesh = topk_indices.reshape(-1)
        sort_permutation = jnp.argsort(expert_idx_mesh)
        sorted_expert_idx = expert_idx_mesh[sort_permutation]
        sorted_token_idx = token_idx_mesh[sort_permutation]
        group_sizes = jnp.bincount(sorted_expert_idx, length=NUM_EXPERTS)
        sorted_tokens = x_flat[sorted_token_idx]
        ff_gate = jax.lax.ragged_dot(sorted_tokens, we_gate, group_sizes)
        ff_up = jax.lax.ragged_dot(sorted_tokens, we_up, group_sizes)
        activated = jax.nn.silu(ff_gate) * ff_up
        ff_out = jax.lax.ragged_dot(activated, we_down, group_sizes)
        sorted_weights = topk_weights.reshape(-1)[sort_permutation]
        ff_out = ff_out * sorted_weights[:, None]
        output_flat = jnp.zeros_like(x_flat).at[sorted_token_idx].add(ff_out)
        return output_flat.reshape(x_shape)
    x = x + _L0_xattn_ref(_layernorm(x, axis=-1), ctx_1024, ctx_1024, mask_1x1xSxS2_bk0, L0_xattn_Wq, L0_xattn_bq, L0_xattn_Wk, L0_xattn_bk, L0_xattn_Wv, L0_xattn_bv, L0_xattn_Wo, L0_xattn_bo)
    x = x + _L0_attn_ref(_layernorm(x, axis=-1), L0_attn_w_attn, L0_attn_w_proj, L0_attn_ln_w)
    x = x + _L0_ffn_ref(_layernorm(x, axis=-1), L0_ffn_rw1, L0_ffn_rb1, L0_ffn_rw2, L0_ffn_rb2, L0_ffn_w1, L0_ffn_b1, L0_ffn_w2, L0_ffn_b2)
    x = x + _L1_xattn_ref(_layernorm(x, axis=-1), ctx_1024, ctx_1024, L1_xattn_Wq, L1_xattn_bq, L1_xattn_Wk, L1_xattn_bk, L1_xattn_Wv, L1_xattn_bv, L1_xattn_Wo, L1_xattn_bo, L1_xattn_gamma, L1_xattn_beta)
    x = x + _L1_attn_ref(_layernorm(x, axis=-1), L1_attn_ln_w, L1_attn_ln_b, L1_attn_tmk, L1_attn_tmv, L1_attn_tmr, L1_attn_decay_w, L1_attn_Wk, L1_attn_Wv, L1_attn_Wr, L1_attn_Wo)
    x = x + _L1_ffn_ref(_layernorm(x, axis=-1), L1_ffn_router_w, L1_ffn_router_b, L1_ffn_we_gate, L1_ffn_we_up, L1_ffn_we_down)
    return x

_drawn_inputs = setup_inputs


def setup_inputs(seed=0):
    import zlib

    import numpy as np

    out = dict(_drawn_inputs(seed))
    spreads = {'L0_xattn_bq': (0.0, 0.1),
     'L0_xattn_bk': (0.0, 2.0),
     'L0_xattn_bv': (0.0, 0.1),
     'L0_xattn_bo': (0.0, 0.1),
     'L0_attn_ln_w': (1.0, 0.2),
     'L0_ffn_rb1': (0.0, 0.1),
     'L0_ffn_rb2': (0.0, 0.1),
     'L0_ffn_b1': (0.0, 0.359),
     'L0_ffn_b2': (0.0, 0.1),
     'L1_xattn_bq': (0.0, 0.8),
     'L1_xattn_bk': (0.0, 2.0),
     'L1_xattn_bv': (0.0, 0.1),
     'L1_xattn_bo': (0.0, 0.1),
     'L1_xattn_gamma': (1.0, 0.2),
     'L1_xattn_beta': (0.0, 0.1),
     'L1_attn_ln_w': (1.0, 0.6),
     'L1_attn_ln_b': (0.0, 0.8),
     'L1_attn_tmk': (0.8999999761581421, 0.6),
     'L1_attn_tmv': (0.8999999761581421, 0.6),
     'L1_attn_tmr': (0.8999999761581421, 0.6),
     'L1_ffn_router_b': (0.0, 0.1)}
    factors = {'L1_attn_decay_w': 200.0,
     'L1_attn_Wk': 8.0,
     'L1_attn_Wv': 8.0,
     'L1_attn_Wr': 8.0,
     'L1_attn_Wo': 8.0}
    for name, (base, spread) in spreads.items():
        noise = np.random.default_rng([zlib.crc32(name.encode()), seed]).standard_normal(out[name].shape)
        drawn = base * np.exp(spread * noise) if base else spread * noise
        out[name] = jnp.asarray(drawn.astype(out[name].dtype))
    for name, factor in factors.items():
        out[name] = (out[name] * factor).astype(out[name].dtype)
    return out
```

```python
from contextlib import ExitStack

import numpy as np

import concourse.bass as bass
from concourse import mybir
from concourse.alu_op_type import AluOpType as ALU

ACT = mybir.ActivationFunctionType
AX = mybir.AxisListType
F32 = mybir.dt.float32
F32R = mybir.dt.float32r
BF16 = mybir.dt.bfloat16
U8 = mybir.dt.uint8
U32 = mybir.dt.uint32

P = 128
D = 512
C = D // P
NB = 4
TOK = NB * P
KEYS = 2048
HEADS = 16
HD = D // HEADS
HPT = P // HD
CH = 512
NCH = KEYS // CH
KT = KEYS // P
QH, KVH, RD = 16, 8, 64
NE = 8
HID = 2048
LN_EPS = 1e-5
NEG = -1e9


class Mem:

    def __init__(self, nc, ctx, stage):
        self.nc, self.ctx, self.stage = nc, ctx, stage
        self.sems = []
        ctx.callback(self.clear)

    def sb(self, name, shape, dt=F32):
        return self.ctx.enter_context(self.nc.sbuf_tensor(f"{self.stage}_{name}", shape, dt))

    def sem(self, name):
        self.sems.append(self.nc.alloc_semaphore(f"{self.stage}_{name}"))
        return self.sems[-1]

    def clear(self):
        if self.sems:
            self.nc.clear_and_free_semaphores(self.sems)
            self.nc.all_engine_barrier()


class Steps:

    def __init__(self, engine, sem, turn=0, per_turn=0):
        self.engine, self.sem, self.base, self.n = engine, sem, turn * per_turn, 0

    def then(self, ins):
        self.mark(ins)
        self.engine.wait_ge(self.sem, self.base + self.n)

    def mark(self, ins):
        ins.then_inc(self.sem, 1)
        self.n += 1

    def wait(self):
        self.engine.wait_ge(self.sem, self.base + self.n)


def f32(ap):
    return ap.bitcast(F32)


def three_products(pe, out, w_hi, w_lo, m_hi, m_lo, start, stop, check=True):
    pe.matmul(out, w_hi, m_hi, start=start, stop=False, skip_group_check=not check)
    pe.matmul(out, w_hi, m_lo, start=False, stop=False, skip_group_check=not check)
    return pe.matmul(out, w_lo, m_hi, start=False, stop=stop, skip_group_check=not check)


def stage_constants(nc, k):
    with ExitStack() as ctx:
        m = Mem(nc, ctx, "const")
        filled, cut = m.sem("filled"), m.sem("cut")
        with nc.Block() as block:
            @block.gpsimd
            def _(pool):
                nc.gpsimd.memset(k["ident"][:], 0.0).then_inc(filled, 1)
                nc.gpsimd.memset(k["ones"][:], 1.0).then_inc(filled, 1)
                pool.wait_ge(filled, 2)
                nc.gpsimd.affine_select(out=k["ident"][:], in_=k["ident"][:], compare_op=ALU.not_equal, fill=1.0,
                                        base=0, pattern=[[-1, P]], channel_multiplier=1).then_inc(cut, 1)


def stage_project_q(nc, k, name, x_in, wq, bq, wk, wv, weights, q_hi_out, q_lo_out, mask):
    with ExitStack() as ctx:
        m = Mem(nc, ctx, name)
        x = m.sb("x", [P, NB, D])
        xn = m.sb("xn", [P, NB, D])
        xT = m.sb("xT", [P, C, TOK])
        wqT = m.sb("wqT", [P, C, D])
        wraw = m.sb("wraw", [P, 2, C * D])
        bcol = m.sb("bcol", [P, C])
        qf = m.sb("qf", [P, C, TOK])
        qhi = m.sb("qhi", [P, C, TOK], F32R)
        qlo = m.sb("qlo", [P, C, TOK], F32R)
        stats = m.sb("stats", [P, NB, 6])
        mv = m.sb("mv", [P, NB, 2])
        ve = m.sb("ve", [P, NB])
        std = m.sb("std", [P, NB])
        rstd = m.sb("rstd", [P, NB])
        x_in_sem, w_in, wq_in, b_in = m.sem("x_in"), m.sem("w_in"), m.sem("wq_in"), m.sem("b_in")
        dstep, var_ready, std_ready, xn_ready = m.sem("dstep"), m.sem("var"), m.sem("std"), m.sem("xn")
        turned, xT_ready, q_made = m.sem("turned"), m.sem("xT"), m.sem("q_made")
        lo_ready, whi_ready, wlo_ready, q_out = (m.sem(s) for s in ("lo", "whi", "wlo", "q_out"))
        if mask is not None:
            mraw = m.sb("mraw", [P, KEYS], U8)
            many = m.sb("many", [P, 1])
            manyr = m.sb("manyr", [P, P])
            manyT = m.sb("manyT", [P, P])
            m_in, any_ready, any_turned = m.sem("m_in"), m.sem("any_ready"), m.sem("any_turned")
        ps = k["ps"]
        with nc.Block() as block:
            @block.sync
            def _(sp):
                sp.dma_start(x[:], x_in.rearrange("b p d -> p b d")).then_inc(x_in_sem, 16)
                sp.dma_start(wqT[:], wq).then_inc(wq_in, 16)
                sp.dma_start(bcol[:], bq).then_inc(b_in, 16)
                if mask is not None:
                    sp.dma_start(mraw[:], mask).then_inc(m_in, 16)
                sp.dma_start(wraw[:, 0, :], wk).then_inc(w_in, 16)
                sp.dma_start(wraw[:, 1, :], wv).then_inc(w_in, 16)
                sp.wait_ge(lo_ready, C)
                for b in range(NB):
                    sp.dma_start(q_hi_out[b], f32(qhi[:, :, b * P:(b + 1) * P])).then_inc(q_out, 16)
                    sp.dma_start(q_lo_out[b], f32(qlo[:, :, b * P:(b + 1) * P])).then_inc(q_out, 16)
                sp.wait_ge(q_out, 32 * NB)

            @block.vector
            def _(dve):
                s = Steps(dve, dstep)
                dve.wait_ge(x_in_sem, 16)
                for b in range(NB):
                    s.mark(nc.vector.bn_stats(stats[:, b, :], x[:, b, :]))
                s.wait()
                for b in range(NB):
                    s.mark(nc.vector.bn_aggr(mv[:, b, :], stats[:, b, :]))
                s.wait()
                nc.vector.tensor_scalar_add(ve[:], mv[:, :, 1], LN_EPS).then_inc(var_ready, 1)
                dve.wait_ge(std_ready, 1)
                s.then(nc.vector.reciprocal(rstd[:], std[:]))
                for b in range(NB):
                    nc.vector.tensor_scalar(xn[:, b, :], x[:, b, :], mv[:, b, 0:1], rstd[:, b:b + 1],
                                            ALU.subtract, ALU.mult).then_inc(xn_ready, 1)
                if mask is not None:
                    dve.wait_ge(m_in, 16)
                    nc.vector.tensor_scalar(k["bias"][:], mraw[:], -NEG, NEG, ALU.mult, ALU.add).then_inc(any_ready, 1)
                    s.then(nc.vector.reduce_max(many[:], mraw[:], AX.X))
                    nc.vector.tensor_scalar(manyr[:], k["ones"][:], many[:, 0:1], None, ALU.mult).then_inc(any_ready, 1)
                    dve.wait_ge(any_turned, 1)
                    s.mark(nc.vector.tensor_copy(manyT[:], ps[7][:, 0:P]))
                for c in range(C):
                    dve.wait_ge(turned, c + 1)
                    nc.vector.tensor_copy(xT[:, c, :], ps[c % 2][:]).then_inc(xT_ready, 1)
                if mask is not None:
                    s.wait()
                dve.wait_ge(b_in, 16)
                for c in range(C):
                    dve.wait_ge(q_made, c + 1)
                    s.then(nc.vector.tensor_scalar(qf[:, c, :], ps[2 + c][:], bcol[:, c:c + 1], float(HD) ** -0.5,
                                                   ALU.add, ALU.mult))
                    if mask is not None:
                        for b in range(NB):
                            s.mark(nc.vector.tensor_tensor(qf[:, c, b * P:(b + 1) * P], qf[:, c, b * P:(b + 1) * P],
                                                           manyT[:], ALU.mult))
                        s.wait()
                    s.then(nc.vector.tensor_copy(qhi[:, c, :], qf[:, c, :]))
                    nc.vector.tensor_tensor(qlo[:, c, :], qf[:, c, :], f32(qhi[:, c, :]), ALU.subtract).then_inc(lo_ready, 1)
                dve.wait_ge(w_in, 32)
                for i, (hi, lo) in enumerate(weights):
                    dve.wait_ge(whi_ready, i + 1)
                    nc.vector.tensor_tensor(lo[:], wraw[:, i, :], f32(hi[:]), ALU.subtract).then_inc(wlo_ready, 1)

            @block.scalar
            def _(act):
                act.wait_ge(var_ready, 1)
                nc.scalar.sqrt(std[:], ve[:]).then_inc(std_ready, 1)
                act.wait_ge(w_in, 32)
                for i, (hi, lo) in enumerate(weights):
                    nc.scalar.copy(hi[:], wraw[:, i, :]).then_inc(whi_ready, 1)

            @block.tensor
            def _(pe):
                if mask is not None:
                    pe.wait_ge(any_ready, 2)
                    pe.transpose(ps[7][:, 0:P], manyr[:], k["ident"][:]).then_inc(any_turned, 1)
                for c in range(C):
                    pe.wait_ge(xn_ready, NB)
                    if c >= 2:
                        pe.wait_ge(xT_ready, c - 1)
                    for b in range(NB):
                        last = pe.transpose(ps[c % 2][:, b * P:(b + 1) * P], xn[:, b, c * P:(c + 1) * P], k["ident"][:])
                    last.then_inc(turned, 1)
                pe.wait_ge(xT_ready, C)
                pe.wait_ge(wq_in, 16)
                for o in range(C):
                    for c in range(C):
                        last = pe.matmul(ps[2 + o][:], wqT[:, c, o * P:(o + 1) * P], xT[:, c, :],
                                         start=(c == 0), stop=(c == C - 1))
                    last.then_inc(q_made, 1)


def stage_attention(nc, k, name, ctxT, weights, bk, q_hi_in, q_lo_in, attn_out, masked):
    (wk_hi, wk_lo), (wv_hi, wv_lo) = weights
    with ExitStack() as ctx:
        m = Mem(nc, ctx, name)
        raw = m.sb("raw", [P, C * CH])
        chi = m.sb("chi", [P, 2, C * CH], F32R)
        clo = m.sb("clo", [P, 2, C * CH], F32R)
        khi = m.sb("khi", [P, C, KEYS], F32R)
        klo = m.sb("klo", [P, C, KEYS], F32R)
        v = m.sb("v", [P, KT, D])
        q_hi = m.sb("q_hi", [P, C, P], F32R)
        q_lo = m.sb("q_lo", [P, C, P], F32R)
        prob = m.sb("prob", [P, 2, KEYS])
        probT = m.sb("probT", [P, KEYS])
        attn = m.sb("attn", [P, D])
        bkcol = m.sb("bkcol", [P, C])
        mx = m.sb("mx", [P, 2, 2])
        nmx = m.sb("nmx", [P, 2])
        den = m.sb("den", [P, 4, 2])
        dsum = m.sb("dsum", [P, 2])
        rden = m.sb("rden", [P, 2])
        pad = m.sb("pad", [P, 2])
        sem = m.sem
        bk_in, raw_in, chi_ready, clo_ready, chunk_used = (sem(s) for s in ("bk_in", "raw_in", "chi", "clo", "chunk_used"))
        k_made, k_done, khi_done, v_made, v_done = (sem(s) for s in ("k_made", "k_done", "khi_done", "v_made", "v_done"))
        q_in, scores_made, max_ready, nmax_ready, exp_done = (sem(s) for s in ("q_in", "scores", "max", "nmax", "exp"))
        turned, turned_dve, turned_act, pv_made, pv_done = (sem(s) for s in ("turned", "t_dve", "t_act", "pv", "pv_done"))
        dsum_done, rden_done, stored = sem("dsum_done"), sem("rden_done"), sem("stored")
        ps, ps2 = k["ps"], k["ps2"]
        S = [ps2[0], ps2[1]]
        T = [ps[4], ps[5]]
        O = [ps[6], ps[7]]
        HALF = KEYS // 2
        GRP = 4
        NG = KT // GRP
        KG, VG = C * NCH, KT

        with nc.Block() as block:
            @block.sync
            def _(sp):
                sp.dma_start(bkcol[:], bk).then_inc(bk_in, 16)
                with sp.Fori(0, NB) as b:
                    for ch in range(NCH):
                        if ch:
                            sp.wait_ge(clo_ready, b * NCH + ch)
                        else:
                            sp.wait_ge(clo_ready, b * NCH)
                        sp.dma_start(raw[:], ctxT[bass.ds(b * NCH + ch, 1)].rearrange("o p n -> (o p) n")) \
                            .then_inc(raw_in, 16)
                        if ch == 0:
                            sp.wait_ge(scores_made, b * 2 * HEADS)
                            sp.dma_start(f32(q_hi[:]), q_hi_in[bass.ds(b, 1)].rearrange("o p c t -> (o p) c t")).then_inc(q_in, 16)
                            sp.dma_start(f32(q_lo[:]), q_lo_in[bass.ds(b, 1)].rearrange("o p c t -> (o p) c t")).then_inc(q_in, 16)
                    sp.wait_ge(pv_done, b * HEADS + HEADS)
                    sp.dma_start(attn_out[bass.ds(b, 1)].rearrange("o p d -> (o p) d"), attn[:]).then_inc(stored, 16)
                sp.wait_ge(stored, 16 * NB)

            @block.tensor
            def _(pe):
                with pe.Fori(0, NB) as b:
                    for ch in range(NCH):
                        n = b * NCH + ch
                        pe.wait_ge(clo_ready, n + 1)
                        hi = chi[:, ch % 2].rearrange("p (c t) -> p c t", c=C)
                        lo = clo[:, ch % 2].rearrange("p (c t) -> p c t", c=C)
                        for o in range(C):
                            g = ch * C + o
                            if g == 0:
                                pe.wait_ge(turned_dve, b * 2 * HEADS)
                            pe.wait_ge(k_done, b * KG + g)
                            for c in range(C):
                                last = three_products(pe, T[0][:], wk_hi[:, c * D + o * P:c * D + (o + 1) * P],
                                                      wk_lo[:, c * D + o * P:c * D + (o + 1) * P],
                                                      hi[:, c, :], lo[:, c, :], c == 0, c == C - 1)
                            last.then_inc(k_made, 1)
                            if g == 0:
                                pe.wait_ge(turned_act, b * 2 * HEADS)
                            pe.wait_ge(v_done, b * VG + g)
                            for c in range(C):
                                last = three_products(pe, T[1][:], hi[:, c, o * P:(o + 1) * P], lo[:, c, o * P:(o + 1) * P],
                                                      wv_hi[:, c * D:(c + 1) * D], wv_lo[:, c * D:(c + 1) * D],
                                                      c == 0, c == C - 1)
                            last.then_inc(v_made, 1)
                    pe.wait_ge(k_done, b * KG + KG)
                    pe.wait_ge(v_done, b * VG + VG)
                    pe.wait_ge(q_in, 32 * b + 32)

                    def scores(h):
                        o, r = h // HPT, (h % HPT) * HD
                        for half in range(2):
                            pe.wait_ge(exp_done, b * 2 * HEADS + 2 * max(h - 1, 0) + (half + 1 if h else 0))
                            for j in range(2):
                                at = half * HALF + j * CH
                                last = three_products(pe, S[half][:, j * CH:(j + 1) * CH],
                                                      q_hi[r:r + HD, o, :], q_lo[r:r + HD, o, :],
                                                      khi[r:r + HD, o, at:at + CH], klo[r:r + HD, o, at:at + CH], True, True)
                            last.then_inc(scores_made, 1)

                    def outputs(h):
                        pe.wait_ge(turned_dve, b * 2 * HEADS + 2 * h + 2)
                        pe.wait_ge(turned_act, b * 2 * HEADS + 2 * h + 2)
                        if h >= 2:
                            pe.wait_ge(pv_done, b * HEADS + h - 1)
                        else:
                            pe.wait_ge(pv_done, b * HEADS)
                        for t in range(KT):
                            last = pe.matmul(O[h % 2][:, 0:HD], probT[:, t * P:(t + 1) * P], v[:, t, h * HD:(h + 1) * HD],
                                             start=(t == 0), stop=(t == KT - 1))
                        last.then_inc(pv_made, 1)

                    def turn(h):
                        for g in range(NG):
                            pe.wait_ge(exp_done, b * 2 * HEADS + 2 * h + (1 if g < NG // 2 else 2))
                            done = turned_dve if g % 2 == 0 else turned_act
                            pe.wait_ge(done, b * 2 * HEADS + 2 * h + g // 2)
                            for i in range(GRP):
                                t = g * GRP + i
                                last = pe.transpose(T[g % 2][:, i * P:(i + 1) * P], prob[:, h % 2, t * P:(t + 1) * P], k["ident"][:])
                            last.then_inc(turned, 1)

                    scores(0)
                    for h in range(HEADS):
                        if h + 1 < HEADS:
                            scores(h + 1)
                        if h:
                            outputs(h - 1)
                        turn(h)
                    outputs(HEADS - 1)

            @block.vector
            def _(dve):
                with dve.Fori(0, NB) as b:
                    for ch in range(NCH):
                        n = b * NCH + ch
                        dve.wait_ge(chi_ready, n + 1)
                        nc.vector.tensor_tensor(clo[:, ch % 2, :], raw[:], f32(chi[:, ch % 2, :]), ALU.subtract) \
                            .then_inc(clo_ready, 1)
                        for o in range(C):
                            g = ch * C + o
                            dve.wait_ge(khi_done, b * KG + g + 1)
                            nc.vector.scalar_tensor_tensor(out=klo[:, o, ch * CH:(ch + 1) * CH], in0=T[0][:],
                                                           scalar=bkcol[:, o:o + 1],
                                                           in1=f32(khi[:, o, ch * CH:(ch + 1) * CH]),
                                                           op0=ALU.add, op1=ALU.subtract).then_inc(k_done, 1)

                    def head_max(h):
                        for half in range(2):
                            dve.wait_ge(scores_made, b * 2 * HEADS + 2 * h + half + 1)
                            if masked:
                                nc.vector.memset(pad[:, half:half + 1], 0.0)
                                nc.vector.tensor_tensor_reduce(S[half][:], S[half][:], k["bias"][:, half * HALF:(half + 1) * HALF],
                                                               1.0, -3e38, ALU.add, ALU.max,
                                                               mx[:, h % 2, half:half + 1]).then_inc(max_ready, 1)
                            else:
                                nc.vector.reduce_max(mx[:, h % 2, half:half + 1], S[half][:], AX.X).then_inc(max_ready, 1)
                        dve.wait_ge(max_ready, b * 2 * HEADS + 2 * h + 2)
                        nc.vector.tensor_reduce(nmx[:, h % 2:h % 2 + 1], mx[:, h % 2, :], AX.X, ALU.max, negate=True) \
                            .then_inc(nmax_ready, 1)

                    def copy_turned(h):
                        for g in range(0, NG, 2):
                            dve.wait_ge(turned, b * NG * HEADS + NG * h + g + 1)
                            if g == 0:
                                dve.wait_ge(pv_made, b * HEADS + h)
                            nc.vector.tensor_copy(probT[:, g * GRP * P:(g + 1) * GRP * P], T[0][:]).then_inc(turned_dve, 1)

                    def finish(h):
                        e = b * HEADS + h
                        dve.wait_ge(exp_done, 2 * e + 2)
                        nc.vector.reduce_sum(dsum[:, h % 2:h % 2 + 1], den[:, h % 4, :], AX.X).then_inc(dsum_done, 1)
                        dve.wait_ge(dsum_done, e + 1)
                        nc.vector.reciprocal(rden[:, h % 2:h % 2 + 1], dsum[:, h % 2:h % 2 + 1]).then_inc(rden_done, 1)
                        dve.wait_ge(rden_done, e + 1)
                        dve.wait_ge(pv_made, e + 1)
                        if h == 0:
                            dve.wait_ge(stored, 16 * b)
                        nc.vector.tensor_scalar(attn[:, h * HD:(h + 1) * HD], O[h % 2][:, 0:HD], rden[:, h % 2:h % 2 + 1],
                                                None, ALU.mult).then_inc(pv_done, 1)

                    head_max(0)
                    for h in range(HEADS):
                        if h + 1 < HEADS:
                            head_max(h + 1)
                        if h:
                            finish(h - 1)
                        copy_turned(h)
                    finish(HEADS - 1)

            @block.scalar
            def _(act):
                act.wait_ge(bk_in, 16)
                with act.Fori(0, NB) as b:
                    for ch in range(NCH):
                        n = b * NCH + ch
                        act.wait_ge(raw_in, 16 * n + 16)
                        if ch >= 2:
                            act.wait_ge(v_made, b * VG + (ch - 1) * C)
                        else:
                            act.wait_ge(v_made, b * VG)
                        nc.scalar.copy(chi[:, ch % 2, :], raw[:]).then_inc(chi_ready, 1)
                        for o in range(C):
                            g = ch * C + o
                            act.wait_ge(k_made, b * KG + g + 1)
                            nc.scalar.activation(khi[:, o, ch * CH:(ch + 1) * CH], T[0][:], ACT.Identity,
                                                 bias=bkcol[:, o:o + 1]).then_inc(khi_done, 1)
                            act.wait_ge(v_made, b * VG + g + 1)
                            nc.scalar.copy(v[:, ch * C + o, :], T[1][:]).then_inc(v_done, 1)

                    def exponent(h):
                        act.wait_ge(nmax_ready, b * HEADS + h + 1)
                        if h >= 2:
                            act.wait_ge(turned, b * NG * HEADS + NG * (h - 1))
                        else:
                            act.wait_ge(turned, b * NG * HEADS)
                        for half in range(2):
                            nc.scalar.activation(prob[:, h % 2, half * HALF:(half + 1) * HALF], S[half][:], ACT.Exp,
                                                 bias=nmx[:, h % 2:h % 2 + 1],
                                                 accum_out=den[:, h % 4, half:half + 1]).then_inc(exp_done, 1)

                    def copy_turned(h):
                        for g in range(1, NG, 2):
                            act.wait_ge(turned, b * NG * HEADS + NG * h + g + 1)
                            if g == 1:
                                act.wait_ge(pv_made, b * HEADS + h)
                            nc.scalar.copy(probT[:, g * GRP * P:(g + 1) * GRP * P], T[1][:]).then_inc(turned_act, 1)

                    exponent(0)
                    for h in range(HEADS):
                        if h + 1 < HEADS:
                            exponent(h + 1)
                        copy_turned(h)


def stage_attention_output(nc, k, name, attn_in, bv, wo, bo, gamma, beta, x_in, x_out):
    with ExitStack() as ctx:
        m = Mem(nc, ctx, name)
        a = m.sb("a", [P, NB, D])
        ab = m.sb("ab", [P, NB, D])
        x = m.sb("x", [P, NB, D])
        y = m.sb("y", [P, NB, D])
        y2 = m.sb("y2", [P, NB, D])
        aT = m.sb("aT", [P, C, TOK])
        woT = m.sb("woT", [P, C, D])
        rows = m.sb("rows", [P, 4, D])
        stats, mv = m.sb("stats", [P, NB, 6]), m.sb("mv", [P, NB, 2])
        ve, std, rstd = m.sb("ve", [P, NB]), m.sb("std", [P, NB]), m.sb("rstd", [P, NB])
        a_in, w_in, x_sem, r_in = m.sem("a_in"), m.sem("w_in"), m.sem("x_in"), m.sem("r_in")
        dstep, ab_ready, turned, aT_ready, made = (m.sem(s) for s in ("dstep", "ab", "turned", "aT", "made"))
        var_ready, std_ready, done, stored = (m.sem(s) for s in ("var", "std", "done", "stored"))
        ps = k["ps"]
        row_list = [bv, bo] + ([gamma, beta] if gamma is not None else [])
        with nc.Block() as block:
            @block.sync
            def _(sp):
                sp.dma_start(a[:], attn_in.rearrange("b p d -> p b d")).then_inc(a_in, 16)
                for i, r in enumerate(row_list):
                    sp.dma_start(rows[:, i, :], r.partition_broadcast(P)).then_inc(r_in, 16)
                sp.dma_start(woT[:], wo).then_inc(w_in, 16)
                sp.dma_start(x[:], x_in.rearrange("b p d -> p b d")).then_inc(x_sem, 16)
                sp.wait_ge(done, NB)
                sp.dma_start(x_out.rearrange("b p d -> p b d"), x[:]).then_inc(stored, 16)
                sp.wait_ge(stored, 16)

            @block.tensor
            def _(pe):
                pe.wait_ge(ab_ready, NB)
                for c in range(C):
                    if c >= 2:
                        pe.wait_ge(aT_ready, c - 1)
                    for b in range(NB):
                        last = pe.transpose(ps[c % 2][:, b * P:(b + 1) * P], ab[:, b, c * P:(c + 1) * P], k["ident"][:])
                    last.then_inc(turned, 1)
                pe.wait_ge(aT_ready, C)
                pe.wait_ge(w_in, 16)
                for b in range(NB):
                    for c in range(C):
                        last = pe.matmul(ps[2 + b][:], aT[:, c, b * P:(b + 1) * P], woT[:, c, :],
                                         start=(c == 0), stop=(c == C - 1))
                    last.then_inc(made, 1)

            @block.scalar
            def _(act):
                for c in range(C):
                    act.wait_ge(turned, c + 1)
                    nc.scalar.copy(aT[:, c, :], ps[c % 2][:]).then_inc(aT_ready, 1)
                if gamma is not None:
                    act.wait_ge(var_ready, 1)
                    nc.scalar.sqrt(std[:], ve[:]).then_inc(std_ready, 1)

            @block.vector
            def _(dve):
                s = Steps(dve, dstep)
                dve.wait_ge(a_in, 16)
                dve.wait_ge(r_in, 16 * len(row_list))
                for b in range(NB):
                    nc.vector.tensor_tensor(ab[:, b, :], a[:, b, :], rows[:, 0, :], ALU.add).then_inc(ab_ready, 1)
                dve.wait_ge(x_sem, 16)
                for b in range(NB):
                    dve.wait_ge(made, b + 1)
                    s.mark(nc.vector.tensor_tensor(y[:, b, :], ps[2 + b][:], rows[:, 1, :], ALU.add))
                s.wait()
                last_y = y
                if gamma is not None:
                    for b in range(NB):
                        s.mark(nc.vector.bn_stats(stats[:, b, :], y[:, b, :]))
                    s.wait()
                    for b in range(NB):
                        s.mark(nc.vector.bn_aggr(mv[:, b, :], stats[:, b, :]))
                    s.wait()
                    nc.vector.tensor_scalar_add(ve[:], mv[:, :, 1], LN_EPS).then_inc(var_ready, 1)
                    dve.wait_ge(std_ready, 1)
                    s.then(nc.vector.reciprocal(rstd[:], std[:]))
                    for b in range(NB):
                        s.mark(nc.vector.tensor_scalar(y2[:, b, :], y[:, b, :], mv[:, b, 0:1], rstd[:, b:b + 1],
                                                       ALU.subtract, ALU.mult))
                    s.wait()
                    for b in range(NB):
                        s.mark(nc.vector.tensor_tensor(y[:, b, :], y2[:, b, :], rows[:, 2, :], ALU.mult))
                    s.wait()
                    for b in range(NB):
                        s.mark(nc.vector.tensor_tensor(y2[:, b, :], y[:, b, :], rows[:, 3, :], ALU.add))
                    s.wait()
                    last_y = y2
                for b in range(NB):
                    nc.vector.tensor_tensor(x[:, b, :], x[:, b, :], last_y[:, b, :], ALU.add).then_inc(done, 1)


def stage_retention(nc, k, t, x_in, x_out):
    QD, KD = QH * RD, KVH * RD
    WIDE = QD + 2 * KD + KVH
    ROT = QH + KVH
    with ExitStack() as ctx:
        m = Mem(nc, ctx, "ret")
        w = m.sb("w", [P, C, WIDE])
        wp = m.sb("wp", [P, 2 * C, D])
        rot = m.sb("rot", [P, 2, RD])
        lnw = m.sb("lnw", [P, RD])
        causal = m.sb("causal", [P, P])
        upto = m.sb("upto", [P, P])
        after = m.sb("after", [P, P])
        x, xn = m.sb("x", [P, D]), m.sb("xn", [P, D])
        xT = m.sb("xT", [P, C, P])
        qk = m.sb("qk", [P, ROT, RD])
        qkr = m.sb("qkr", [P, ROT, RD])
        qks = m.sb("qks", [P, ROT, RD])
        qr = m.sb("qr", [P, QH, RD])
        kr = m.sb("kr", [P, KVH, 2, RD])
        vx = m.sb("vx", [P, KVH, RD + 1])
        gate = m.sb("gate", [P, 6, KVH])
        cut = m.sb("cut", [P, KVH, P])
        decay = m.sb("decay", [P, KVH, P])
        qT, kT = m.sb("qT", [P, KVH, P]), m.sb("kT", [P, KVH, P])
        s_abs, u = m.sb("s_abs", [P, QH, P]), m.sb("u", [P, QH, P])
        um, ru = m.sb("um", [P, QH]), m.sb("ru", [P, QH])
        aT = m.sb("aT", [P, QH, P])
        y, yc, y2 = m.sb("y", [P, QH, RD]), m.sb("yc", [P, QH, RD]), m.sb("y2", [P, QH, RD])
        col = m.sb("col", [P, 6, QH])
        yT = m.sb("yT", [P, 2 * C, P])
        res = m.sb("res", [P, D])
        stats, mv, rs = m.sb("stats", [P, 6]), m.sb("mv", [P, 2]), m.sb("rs", [P, 3])
        pad = m.sb("pad", [P, 1])
        S = {}
        for n in ("const_in", "filled", "x_sem", "dstep", "astep", "pstep", "var", "std", "xn", "xturned", "xT", "proj", "proj_read",
                  "gate_in", "e_gate", "gate_1", "l_gate", "cut", "decay_made", "decay_exp", "rotated", "qk_turned", "qk_copied",
                  "scores", "abs", "r_ready", "squared", "a_turned", "a_copied", "num", "y_sum", "yvar", "ystd", "y_ready",
                  "y_turned", "y_copied", "out_made", "res", "stored"):
            S[n] = m.sem(n)
        ps, ps2 = k["ps"], k["ps2"]
        NPJ = WIDE // D + 1
        with nc.Block() as block:
            @block.sync
            def _(sp):
                sp.dma_start(rot[:], t["rotary"]).then_inc(S["const_in"], 16)
                sp.dma_start(lnw[:], t["L0_attn_ln_w"].partition_broadcast(P)).then_inc(S["const_in"], 16)
                sp.dma_start(w[:], t["L0_attn_w_attn"]).then_inc(S["const_in"], 16)
                sp.dma_start(wp[:], t["L0_attn_w_proj"]).then_inc(S["const_in"], 16)
                with sp.Fori(0, NB) as b:
                    sp.wait_ge(S["res"], b)
                    sp.dma_start(x[:], x_in[bass.ds(b, 1)].rearrange("o p d -> (o p) d")).then_inc(S["x_sem"], 16)
                    sp.wait_ge(S["res"], b + 1)
                    sp.dma_start(x_out[bass.ds(b, 1)].rearrange("o p d -> (o p) d"), res[:]).then_inc(S["stored"], 16)
                sp.wait_ge(S["stored"], 16 * NB)

            @block.gpsimd
            def _(pool):
                nc.gpsimd.memset(vx[:, :, RD:RD + 1], 1.0).then_inc(S["filled"], 1)
                nc.gpsimd.affine_select(out=causal[:], in_=k["ones"][:], compare_op=ALU.is_ge, fill=0.0, base=0,
                                        pattern=[[-1, P]], channel_multiplier=1).then_inc(S["filled"], 1)
                nc.gpsimd.affine_select(out=upto[:], in_=k["ones"][:], compare_op=ALU.is_ge, fill=0.0, base=0,
                                        pattern=[[1, P]], channel_multiplier=-1).then_inc(S["filled"], 1)
                nc.gpsimd.affine_select(out=after[:], in_=k["ones"][:], compare_op=ALU.is_gt, fill=0.0, base=0,
                                        pattern=[[-1, P]], channel_multiplier=1).then_inc(S["filled"], 1)

            @block.tensor
            def _(pe):
                pe.wait_ge(S["filled"], 4)
                pe.wait_ge(S["const_in"], 64)
                with pe.Fori(0, NB) as b:
                    pe.wait_ge(S["xn"], b + 1)
                    pe.wait_ge(S["out_made"], b)
                    for c in range(C):
                        last = pe.transpose(ps[4][:, c * P:(c + 1) * P], xn[:, c * P:(c + 1) * P], k["ident"][:])
                    last.then_inc(S["xturned"], 1)
                    pe.wait_ge(S["xT"], b + 1)
                    for g in range(NPJ):
                        n = min(D, WIDE - g * D)
                        if g >= 2:
                            pe.wait_ge(S["proj_read"], b * NPJ + g - 1)
                        for c in range(C):
                            last = pe.matmul(ps[5 + g % 2][:, 0:n], xT[:, c, :], w[:, c, g * D:g * D + n],
                                             start=(c == 0), stop=(c == C - 1))
                        last.then_inc(S["proj"], 1)
                    pe.wait_ge(S["cut"], b + 1)
                    for i in range(2):
                        last = pe.matmul(ps2[0][:, i * D:(i + 1) * D], upto[:],
                                         cut[:, i * 4:(i + 1) * 4, :].rearrange("p h s -> p (h s)"), start=True, stop=True)
                    last.then_inc(S["decay_made"], 1)
                    for i in range(4):
                        src = qr if i < 2 else kr
                        flat = src[:].rearrange("p h d -> p (h d)") if i < 2 else src[:].rearrange("p h r d -> p (h r d)")
                        if i == 0:
                            pe.wait_ge(S["rotated"], 2 * b + 1)
                        if i == 2:
                            pe.wait_ge(S["rotated"], 2 * b + 2)
                        if i >= 2:
                            pe.wait_ge(S["qk_copied"], 4 * b + i - 1)
                        for j in range(4):
                            at = ((i % 2) * 4 + j) * P
                            last = pe.transpose(ps[6 + i % 2][:, j * P:(j + 1) * P], flat[:, at:at + P], k["ident"][:])
                        last.then_inc(S["qk_turned"], 1)
                    pe.wait_ge(S["qk_copied"], 4 * b + 4)
                    pe.wait_ge(S["decay_exp"], b + 1)
                    for r in range(2):
                        for h in range(KVH):
                            last = pe.matmul(ps2[r][:, h * P:(h + 1) * P], qT[r * RD:(r + 1) * RD, h, :],
                                             kT[r * RD:(r + 1) * RD, h, :], start=True, stop=True)
                        last.then_inc(S["scores"], 1)
                    pe.wait_ge(S["squared"], b + 1)
                    for i in range(4):
                        if i >= 2:
                            pe.wait_ge(S["a_copied"], 4 * b + i - 1)
                        for j in range(4):
                            last = pe.transpose(ps[4 + i % 2][:, j * P:(j + 1) * P], s_abs[:, i * 4 + j, :], k["ident"][:])
                        last.then_inc(S["a_turned"], 1)
                    pe.wait_ge(S["a_copied"], 4 * b + 4)
                    for h in range(QH):
                        last = pe.matmul(ps[h // 4][:, (h % 4) * (RD + 1):(h % 4 + 1) * (RD + 1)], aT[:, h, :],
                                         vx[:, h // 2, :], start=True, stop=True)
                    last.then_inc(S["num"], 1)
                    pe.wait_ge(S["y_ready"], b + 1)
                    flat = y2[:].rearrange("p h d -> p (h d)")
                    for i in range(2):
                        for j in range(4):
                            last = pe.transpose(ps[4 + i][:, j * P:(j + 1) * P], flat[:, (i * 4 + j) * P:(i * 4 + j + 1) * P], k["ident"][:])
                        last.then_inc(S["y_turned"], 1)
                    pe.wait_ge(S["y_copied"], 2 * b + 2)
                    for c in range(2 * C):
                        last = pe.matmul(ps[6][:], yT[:, c, :], wp[:, c, :], start=(c == 0), stop=(c == 2 * C - 1))
                    last.then_inc(S["out_made"], 1)

            @block.scalar
            def _(act):
                with act.Fori(0, NB) as b:
                    act.wait_ge(S["var"], b + 1)
                    nc.scalar.sqrt(rs[:, 1:2], rs[:, 0:1]).then_inc(S["std"], 1)
                    act.wait_ge(S["xturned"], b + 1)
                    nc.scalar.copy(xT[:].rearrange("p c t -> p (c t)"), ps[4][:]).then_inc(S["xT"], 1)
                    for g in range(NPJ):
                        act.wait_ge(S["proj"], b * NPJ + g + 1)
                        src = ps[5 + g % 2]
                        if g < 3:
                            ins = nc.scalar.copy(qk[:, g * 8:(g + 1) * 8, :], src[:].rearrange("p (h d) -> p h d", d=RD))
                        elif g == 3:
                            ins = nc.scalar.copy(vx[:, :, 0:RD], src[:].rearrange("p (h d) -> p h d", d=RD))
                        else:
                            ins = nc.scalar.copy(gate[:, 0, :], src[:, 0:KVH])
                        ins.then_inc(S["proj_read"], 1)
                    act.wait_ge(S["gate_in"], b + 1)
                    nc.scalar.activation(gate[:, 2, :], gate[:, 1, :], ACT.Exp, scale=-1.0).then_inc(S["e_gate"], 1)
                    act.wait_ge(S["gate_1"], b + 1)
                    nc.scalar.activation(gate[:, 4, :], gate[:, 3, :], ACT.Ln).then_inc(S["l_gate"], 1)
                    act.wait_ge(S["decay_made"], b + 1)
                    nc.scalar.activation(decay[:].rearrange("p h s -> p (h s)"), ps2[0][:], ACT.Exp, scale=0.5) \
                        .then_inc(S["decay_exp"], 1)
                    for i in range(4):
                        act.wait_ge(S["qk_turned"], 4 * b + i + 1)
                        dst = (qT if i < 2 else kT)[:, (i % 2) * 4:(i % 2 + 1) * 4, :].rearrange("p h t -> p (h t)")
                        nc.scalar.copy(dst, ps[6 + i % 2][:]).then_inc(S["qk_copied"], 1)
                    for r in range(2):
                        act.wait_ge(S["scores"], 2 * b + r + 1)
                        nc.scalar.activation(s_abs[:, r:QH:2, :], ps2[r][:].rearrange("p (h s) -> p h s", s=P), ACT.Abs,
                                             scale=float(RD) ** -0.5).then_inc(S["abs"], 1)
                    act.wait_ge(S["r_ready"], b + 1)
                    nc.scalar.square(s_abs[:], u[:]).then_inc(S["squared"], 1)
                    for i in range(4):
                        act.wait_ge(S["a_turned"], 4 * b + i + 1)
                        nc.scalar.copy(aT[:, i * 4:(i + 1) * 4, :].rearrange("p h t -> p (h t)"), ps[4 + i % 2][:]) \
                            .then_inc(S["a_copied"], 1)
                    act.wait_ge(S["yvar"], b + 1)
                    nc.scalar.sqrt(col[:, 3, :], col[:, 2, :]).then_inc(S["ystd"], 1)
                    for i in range(2):
                        act.wait_ge(S["y_turned"], 2 * b + i + 1)
                        nc.scalar.copy(yT[:, i * 4:(i + 1) * 4, :].rearrange("p c t -> p (c t)"), ps[4 + i][:]) \
                            .then_inc(S["y_copied"], 1)

            @block.vector
            def _(dve):
                dve.wait_ge(S["filled"], 4)
                dve.wait_ge(S["const_in"], 64)
                with dve.Fori(0, NB) as b:
                    s = Steps(dve, S["dstep"], b, RET_STEPS)
                    dve.wait_ge(S["x_sem"], 16 * b + 16)
                    s.then(nc.vector.bn_stats(stats[:], x[:]))
                    nc.vector.memset(pad[:], 0.0)
                    s.then(nc.vector.bn_aggr(mv[:], stats[:]))
                    nc.vector.tensor_scalar_add(rs[:, 0:1], mv[:, 1:2], LN_EPS).then_inc(S["var"], 1)
                    dve.wait_ge(S["std"], b + 1)
                    s.then(nc.vector.reciprocal(rs[:, 2:3], rs[:, 1:2]))
                    nc.vector.tensor_scalar(xn[:], x[:], mv[:, 0:1], rs[:, 2:3], ALU.subtract, ALU.mult).then_inc(S["xn"], 1)
                    dve.wait_ge(S["proj_read"], b * NPJ + 3)
                    cos = rot[:, 0:1, :].to_broadcast([P, ROT, RD])
                    pairs = qk[:].rearrange("p h (i e) -> p h i e", e=2)
                    spairs = qks[:].rearrange("p h (i e) -> p h i e", e=2)
                    sinp = rot[:, 1, :].rearrange("p (i e) -> p i e", e=2)
                    s.mark(nc.vector.tensor_tensor(qkr[:], qk[:], cos, ALU.mult))
                    for e in range(2):
                        sin_e = sinp[:, :, e].unsqueeze(1).to_broadcast([P, ROT, RD // 2])
                        s.mark(nc.vector.tensor_tensor(spairs[:, :, :, e], pairs[:, :, :, 1 - e], sin_e, ALU.mult))
                    s.wait()
                    nc.vector.tensor_tensor(qr[:], qkr[:, 0:QH], qks[:, 0:QH], ALU.add).then_inc(S["rotated"], 1)
                    s.mark(nc.vector.tensor_tensor(kr[:, :, 0, :], qkr[:, QH:ROT], qks[:, QH:ROT], ALU.add))
                    nc.vector.tensor_tensor(kr[:, :, 1, :], qkr[:, QH:ROT], qks[:, QH:ROT], ALU.add).then_inc(S["rotated"], 1)
                    dve.wait_ge(S["proj_read"], b * NPJ + NPJ)
                    s.then(nc.vector.tensor_scalar_add(gate[:, 0, :], gate[:, 0, :], 6.906768))
                    nc.vector.scalar_tensor_tensor(out=gate[:, 1, :], in0=gate[:, 0, :], scalar=-1.0, in1=gate[:, 0, :],
                                                   op0=ALU.mult, op1=ALU.max).then_inc(S["gate_in"], 1)
                    dve.wait_ge(S["e_gate"], b + 1)
                    nc.vector.tensor_scalar_add(gate[:, 3, :], gate[:, 2, :], 1.0).then_inc(S["gate_1"], 1)
                    dve.wait_ge(S["l_gate"], b + 1)
                    s.then(nc.vector.scalar_tensor_tensor(out=gate[:, 5, :], in0=gate[:, 0, :], scalar=0.0, in1=gate[:, 4, :],
                                                          op0=ALU.min, op1=ALU.subtract))
                    nc.vector.tensor_tensor(cut[:], after[:].unsqueeze(1).to_broadcast([P, KVH, P]),
                                            gate[:, 5, :].unsqueeze(2).to_broadcast([P, KVH, P]), ALU.mult).then_inc(S["cut"], 1)
                    dve.wait_ge(S["decay_exp"], b + 1)
                    s.then(nc.vector.tensor_tensor(decay[:], decay[:], causal[:].unsqueeze(1).to_broadcast([P, KVH, P]), ALU.mult))
                    dve.wait_ge(S["abs"], 2 * b + 2)
                    for r in range(2):
                        s.mark(nc.vector.scalar_tensor_tensor(out=u[:, r:QH:2, :], in0=s_abs[:, r:QH:2, :], scalar=1e-30,
                                                              in1=decay[:], op0=ALU.add, op1=ALU.mult))
                    s.wait()
                    s.then(nc.vector.tensor_reduce(um[:], u[:], AX.X, ALU.max))
                    s.then(nc.vector.reciprocal(ru[:], um[:]))
                    nc.vector.tensor_tensor(u[:], u[:], ru[:].unsqueeze(2).to_broadcast([P, QH, P]), ALU.mult) \
                        .then_inc(S["r_ready"], 1)
                    dve.wait_ge(S["num"], b + 1)
                    for i in range(4):
                        at = ps[i][:, 0:4 * (RD + 1)].rearrange("p (h d) -> p h d", h=4)
                        s.then(nc.vector.tensor_scalar_add(col[:, 0, i * 4:(i + 1) * 4], at[:, :, RD], 1e-6))
                        s.then(nc.vector.reciprocal(col[:, 1, i * 4:(i + 1) * 4], col[:, 0, i * 4:(i + 1) * 4]))
                        s.mark(nc.vector.tensor_tensor(y[:, i * 4:(i + 1) * 4, :], at[:, :, 0:RD],
                                                       col[:, 1, i * 4:(i + 1) * 4].unsqueeze(2).to_broadcast([P, 4, RD]), ALU.mult))
                    s.wait()
                    s.then(nc.vector.reduce_sum(col[:, 4, :], y[:], AX.X))
                    s.then(nc.vector.tensor_scalar(col[:, 5, :], col[:, 4, :], 1.0 / RD, None, ALU.mult))
                    s.then(nc.vector.tensor_tensor(yc[:], y[:], col[:, 5, :].unsqueeze(2).to_broadcast([P, QH, RD]), ALU.subtract))
                    s.then(nc.vector.tensor_tensor(y[:], yc[:], yc[:], ALU.mult))
                    s.then(nc.vector.reduce_sum(col[:, 4, :], y[:], AX.X))
                    nc.vector.tensor_scalar(col[:, 2, :], col[:, 4, :], 1.0 / RD, 1e-9, ALU.mult, ALU.add).then_inc(S["yvar"], 1)
                    dve.wait_ge(S["ystd"], b + 1)
                    s.then(nc.vector.reciprocal(col[:, 5, :], col[:, 3, :]))
                    s.then(nc.vector.tensor_tensor(y[:], yc[:], col[:, 5, :].unsqueeze(2).to_broadcast([P, QH, RD]), ALU.mult))
                    nc.vector.tensor_tensor(y2[:], y[:], lnw[:].unsqueeze(1).to_broadcast([P, QH, RD]), ALU.mult) \
                        .then_inc(S["y_ready"], 1)
                    dve.wait_ge(S["out_made"], b + 1)
                    dve.wait_ge(S["stored"], 16 * b)
                    nc.vector.tensor_tensor(res[:], x[:], ps[6][:], ALU.add).then_inc(S["res"], 1)
                    assert s.n == RET_STEPS, s.n


RET_STEPS = 33


def stage_experts(nc, k, name, t, x_in, x_out, layer):
    HT = HID // P if layer == 0 else C
    GR = HT // C
    with ExitStack() as ctx:
        m = Mem(nc, ctx, name)
        x = m.sb("x", [P, NB, D])
        xhi, xlo = m.sb("xhi", [P, C, TOK], F32R), m.sb("xlo", [P, C, TOK], F32R)
        weT = m.sb("weT", [NE, TOK])
        weB = m.sb("weB", [P, NE, TOK])
        b2 = m.sb("b2", [NE, D])
        b1 = m.sb("b1", [P, NE * HT]) if layer == 0 else None
        prep_done = {n: m.sem(n) for n in ("x_in", "b_in", "xlo_ready", "weB_ready")}
        ps = k["ps"]
        Y = ps[0:4]
        with ExitStack() as prep:
            p = Mem(nc, prep, name + "p")
            xn = p.sb("xn", [P, NB, D])
            xT = p.sb("xT", [P, C, TOK])
            stats, mv = p.sb("stats", [P, NB, 6]), p.sb("mv", [P, NB, 2])
            ve, std, rstd = p.sb("ve", [P, NB]), p.sb("std", [P, NB]), p.sb("rstd", [P, NB])
            if layer == 0:
                rw1, rw2 = p.sb("rw1", [P, C, HID]), p.sb("rw2", [P, HT, NE])
                rb1, hr = p.sb("rb1", [P, HT]), p.sb("hr", [P, HT, TOK])
            else:
                rw2 = p.sb("rw2", [P, C, NE])
            rb2 = p.sb("rb2", [1, NE])
            logit = p.sb("logit", [P, NB, NE])
            best, bidx, bidf = p.sb("best", [P, NB, 8]), p.sb("bidx", [P, NB, 8], U32), p.sb("bidf", [P, NB, 8])
            gap, e2, e1 = p.sb("gap", [P, NB]), p.sb("e2", [P, NB]), p.sb("e1", [P, NB])
            prob = p.sb("prob", [P, NB, 2])
            number = p.sb("number", [P, NE])
            we, we2 = p.sb("we", [P, NB, NE]), p.sb("we2", [P, NB, NE])
            sel = p.sb("sel", [NE, NE, P])
            s_ = {n: p.sem(n) for n in ("w_in", "dstep", "var", "std", "xn", "turned", "xT", "xhi", "h_made", "h_read", "logits",
                                        "gap", "e2", "we", "we_turned", "weT", "weB_made", "filled", "selected")}
            with nc.Block() as block:
                @block.sync
                def _(sp):
                    sp.dma_start(x[:], x_in.rearrange("b p d -> p b d")).then_inc(prep_done["x_in"], 16)
                    if layer == 0:
                        sp.dma_start(rb1[:], t["L0_ffn_rb1"]).then_inc(s_["w_in"], 16)
                        sp.dma_start(rw1[:], t["L0_ffn_rw1"]).then_inc(s_["w_in"], 16)
                        sp.dma_start(rw2[:], t["L0_ffn_rw2"]).then_inc(s_["w_in"], 16)
                        sp.dma_start(rb2[:], t["L0_ffn_rb2"].rearrange("(o e) -> o e", o=1)).then_inc(s_["w_in"], 16)
                        sp.dma_start(b1[:], t["L0_ffn_b1"]).then_inc(prep_done["b_in"], 16)
                        sp.dma_start(b2[:], t["L0_ffn_b2"]).then_inc(prep_done["b_in"], 16)
                    else:
                        sp.dma_start(rw2[:], t["L1_ffn_router_w"]).then_inc(s_["w_in"], 16)
                        sp.dma_start(rb2[:], t["L1_ffn_router_b"].rearrange("(o e) -> o e", o=1)).then_inc(s_["w_in"], 16)

                @block.gpsimd
                def _(pool):
                    nc.gpsimd.memset(sel[:], 1.0).then_inc(s_["filled"], 1)
                    nc.gpsimd.iota(number[:], pattern=[[1, NE]], base=0, channel_multiplier=0,
                                   allow_small_or_imprecise_dtypes=True).then_inc(s_["filled"], 1)
                    pool.wait_ge(s_["filled"], 2)
                    nc.gpsimd.affine_select(out=sel[:], in_=sel[:], compare_op=ALU.is_equal, fill=0.0, base=0,
                                            pattern=[[-1, NE], [0, P]], channel_multiplier=1).then_inc(s_["selected"], 1)
                    if layer == 1:
                        nc.gpsimd.memset(b2[:], 0.0).then_inc(prep_done["b_in"], 16)

                @block.tensor
                def _(pe):
                    for c in range(C):
                        pe.wait_ge(s_["xn"], NB)
                        if c >= 2:
                            pe.wait_ge(s_["xT"], c - 1)
                        for b in range(NB):
                            last = pe.transpose(ps[4 + c % 2][:, b * P:(b + 1) * P], xn[:, b, c * P:(c + 1) * P], k["ident"][:])
                        last.then_inc(s_["turned"], 1)
                    pe.wait_ge(s_["xT"], C)
                    pe.wait_ge(s_["w_in"], 64 if layer == 0 else 32)
                    if layer == 0:
                        for j in range(HT):
                            if j >= 2:
                                pe.wait_ge(s_["h_read"], j - 1)
                            for c in range(C):
                                last = pe.matmul(ps[4 + j % 2][:], rw1[:, c, j * P:(j + 1) * P], xT[:, c, :],
                                                 start=(c == 0), stop=(c == C - 1))
                            last.then_inc(s_["h_made"], 1)
                        pe.wait_ge(s_["h_read"], HT)
                    rows, n = (hr, HT) if layer == 0 else (xT, C)
                    for b in range(NB):
                        pe.matmul(ps[6][:, b * NE:(b + 1) * NE], k["ones"][0:1, :], rb2[:], start=True, stop=False)
                        for j in range(n):
                            last = pe.matmul(ps[6][:, b * NE:(b + 1) * NE], rows[:, j, b * P:(b + 1) * P], rw2[:, j, :],
                                             start=False, stop=(j == n - 1))
                    last.then_inc(s_["logits"], 1)
                    pe.wait_ge(s_["we"], NB)
                    for b in range(NB):
                        last = pe.transpose(ps[7][0:NE, b * P:(b + 1) * P], we[:, b, :], k["ident"][:])
                    last.then_inc(s_["we_turned"], 1)
                    pe.wait_ge(s_["weT"], 1)
                    pe.wait_ge(s_["selected"], 1)
                    for e in range(NE):
                        if e >= 2:
                            pe.wait_ge(prep_done["weB_ready"], e - 1)
                        pe.matmul(ps[4 + e % 2][:], sel[:, e, :], weT[:], start=True, stop=True).then_inc(s_["weB_made"], 1)

                @block.scalar
                def _(act):
                    act.wait_ge(s_["var"], 1)
                    nc.scalar.sqrt(std[:], ve[:]).then_inc(s_["std"], 1)
                    for c in range(C):
                        act.wait_ge(s_["xT"], c + 1)
                        nc.scalar.copy(xhi[:, c, :], xT[:, c, :]).then_inc(s_["xhi"], 1)
                    if layer == 0:
                        act.wait_ge(s_["w_in"], 64)
                        for j in range(HT):
                            act.wait_ge(s_["h_made"], j + 1)
                            nc.scalar.activation(hr[:, j, :], ps[4 + j % 2][:], ACT.Silu, bias=rb1[:, j:j + 1]) \
                                .then_inc(s_["h_read"], 1)
                    act.wait_ge(s_["gap"], 1)
                    nc.scalar.activation(e2[:], gap[:], ACT.Exp).then_inc(s_["e2"], 1)
                    for e in range(NE):
                        act.wait_ge(s_["weB_made"], e + 1)
                        nc.scalar.copy(weB[:, e, :], ps[4 + e % 2][:]).then_inc(prep_done["weB_ready"], 1)

                @block.vector
                def _(dve):
                    s = Steps(dve, s_["dstep"])
                    dve.wait_ge(prep_done["x_in"], 16)
                    for b in range(NB):
                        s.mark(nc.vector.bn_stats(stats[:, b, :], x[:, b, :]))
                    s.wait()
                    for b in range(NB):
                        s.mark(nc.vector.bn_aggr(mv[:, b, :], stats[:, b, :]))
                    s.wait()
                    nc.vector.tensor_scalar_add(ve[:], mv[:, :, 1], LN_EPS).then_inc(s_["var"], 1)
                    dve.wait_ge(s_["std"], 1)
                    s.then(nc.vector.reciprocal(rstd[:], std[:]))
                    for b in range(NB):
                        nc.vector.tensor_scalar(xn[:, b, :], x[:, b, :], mv[:, b, 0:1], rstd[:, b:b + 1],
                                                ALU.subtract, ALU.mult).then_inc(s_["xn"], 1)
                    for c in range(C):
                        dve.wait_ge(s_["turned"], c + 1)
                        nc.vector.tensor_copy(xT[:, c, :], ps[4 + c % 2][:]).then_inc(s_["xT"], 1)
                    for c in range(C):
                        dve.wait_ge(s_["xhi"], c + 1)
                        nc.vector.tensor_tensor(xlo[:, c, :], xT[:, c, :], f32(xhi[:, c, :]), ALU.subtract) \
                            .then_inc(prep_done["xlo_ready"], 1)
                    dve.wait_ge(s_["logits"], 1)
                    s.then(nc.vector.tensor_copy(logit[:].rearrange("p b e -> p (b e)"), ps[6][:, 0:NB * NE]))
                    for b in range(NB):
                        s.mark(nc.vector.max(best[:, b, :], logit[:, b, :]))
                    s.wait()
                    for b in range(NB):
                        s.mark(nc.vector.max_index(bidx[:, b, :], best[:, b, :], logit[:, b, :]))
                    s.wait()
                    s.mark(nc.vector.tensor_copy(bidf[:], bidx[:]))
                    nc.vector.tensor_tensor(gap[:], best[:, :, 1], best[:, :, 0], ALU.subtract).then_inc(s_["gap"], 1)
                    dve.wait_ge(s_["e2"], 1)
                    s.then(nc.vector.tensor_scalar_add(e1[:], e2[:], 1.0))
                    s.then(nc.vector.reciprocal(prob[:, :, 0], e1[:]))
                    s.then(nc.vector.tensor_tensor(prob[:, :, 1], e2[:], prob[:, :, 0], ALU.mult))
                    dve.wait_ge(s_["filled"], 2)
                    for b in range(NB):
                        s.mark(nc.vector.tensor_scalar(we2[:, b, :], number[:], bidf[:, b, 1:2], prob[:, b, 1:2], ALU.is_equal, ALU.mult))
                        s.mark(nc.vector.tensor_scalar(we[:, b, :], number[:], bidf[:, b, 0:1], prob[:, b, 0:1], ALU.is_equal, ALU.mult))
                    s.wait()
                    for b in range(NB):
                        nc.vector.tensor_tensor(we[:, b, :], we[:, b, :], we2[:, b, :], ALU.add).then_inc(s_["we"], 1)
                    dve.wait_ge(s_["we_turned"], 1)
                    nc.vector.tensor_copy(weT[:], ps[7][0:NE, :]).then_inc(s_["weT"], 1)
        NW = 2 if layer == 0 else 3
        wraw = [m.sb(f"wraw{i}", [P, C * D]) for i in range(NW)]
        whi = [m.sb(f"whi{i}", [P, 2, C * D], F32R) for i in range(NW)]
        wlo = [m.sb(f"wlo{i}", [P, 2, C * D], F32R) for i in range(NW)]
        act_h, wh = m.sb("act_h", [P, 2, TOK]), m.sb("wh", [P, 2, TOK])
        hhi, hlo = m.sb("hhi", [P, 2, TOK], F32R), m.sb("hlo", [P, 2, TOK], F32R)
        names = ("L0_ffn_w1", "L0_ffn_w2") if layer == 0 else ("L1_ffn_we_gate", "L1_ffn_we_up", "L1_ffn_we_down")
        s_ = {n: m.sem("x" + n) for n in ("w_in", "whi", "wlo", "primed", "h_made", "h_read", "silu", "dstep", "wh", "hhi", "hlo",
                                          "y_tile", "y_made", "out", "stored")}
        up = 1 if layer == 1 else 0
        with nc.Block() as block:
            @block.sync
            def _(sp):
                with sp.Fori(0, NE) as e:
                    for g in range(GR):
                        if g:
                            sp.wait_ge(s_["wlo"], NW * (e * GR + g))
                        else:
                            sp.wait_ge(s_["wlo"], e * (NW * GR))
                        for i in range(NW):
                            sp.dma_start(wraw[i][:], t[names[i]][bass.ds(e * GR + g, 1)].rearrange("o p n -> (o p) n")) \
                                .then_inc(s_["w_in"], 16)
                sp.wait_ge(s_["out"], NB)
                sp.dma_start(x_out.rearrange("b p d -> p b d"), x[:]).then_inc(s_["stored"], 16)
                sp.wait_ge(s_["stored"], 16)

            PAR = 2 if GR > 1 else 1

            @block.gpsimd
            def _(pool):
                with pool.Fori(0, NE) as e:
                    for g in range(GR):
                        for i in range(NW):
                            pool.wait_ge(s_["whi"], e * (NW * GR) + NW * g + i + 1)
                            nc.gpsimd.tensor_tensor(wlo[i][:, g % PAR, :], wraw[i][:], f32(whi[i][:, g % PAR, :]), ALU.subtract) \
                                .then_inc(s_["wlo"], 1)

            @block.tensor
            def _(pe):
                pe.wait_ge(prep_done["b_in"], 32 if layer == 0 else 16)
                for b in range(NB):
                    pe.matmul(Y[b][:], weT[:, b * P:(b + 1) * P], b2[:], start=True, stop=False, skip_group_check=True)
                with pe.Fori(0, NE) as e:
                    def hidden(j):
                        g, r = j // C, j % C
                        if r == 0:
                            pe.wait_ge(s_["wlo"], e * (NW * GR) + NW * (g + 1))
                        pe.wait_ge(s_["h_read"] if up else s_["silu"], e * HT + max(j - 1, 0))
                        for i in range(1 + up):
                            bank = ps[4 + (j % 2) * (1 + up) + i]
                            for c in range(C):
                                at = c * D + r * P
                                last = three_products(pe, bank[:], whi[i][:, g % PAR, at:at + P], wlo[i][:, g % PAR, at:at + P],
                                                      xhi[:, c, :], xlo[:, c, :], c == 0, c == C - 1)
                        last.then_inc(s_["h_made"], 1)

                    def output(j):
                        g, r = j // C, j % C
                        pe.wait_ge(s_["hlo"], e * HT + j + 1)
                        for b in range(NB):
                            last = three_products(pe, Y[b][:], hhi[:, j % 2, b * P:(b + 1) * P], hlo[:, j % 2, b * P:(b + 1) * P],
                                                  whi[-1][:, g % PAR, r * D:(r + 1) * D], wlo[-1][:, g % PAR, r * D:(r + 1) * D],
                                                  False, j == HT - 1, check=False)
                        last.then_inc(s_["y_tile"], 1)

                    hidden(0)
                    for j in range(HT):
                        if j + 1 < HT:
                            hidden(j + 1)
                        output(j)

            @block.scalar
            def _(act):
                with act.Fori(0, NE) as e:
                    def split(g):
                        act.wait_ge(s_["w_in"], e * (16 * NW * GR) + 16 * NW * (g + 1))
                        act.wait_ge(s_["y_tile"], e * HT + max(0, g - PAR + 1) * C)
                        for i in range(NW):
                            nc.scalar.copy(whi[i][:, g % PAR, :], wraw[i][:]).then_inc(s_["whi"], 1)

                    split(0)
                    for j in range(HT):
                        if j % C == 1 and j // C + 1 < GR:
                            split(j // C + 1)
                        act.wait_ge(s_["h_made"], e * HT + j + 1)
                        if j >= 2:
                            act.wait_ge(s_["wh"], e * HT + j - 1)
                        else:
                            act.wait_ge(s_["wh"], e * HT)
                        bank = ps[4 + (j % 2) * (1 + up)]
                        if layer == 0:
                            nc.scalar.activation(act_h[:, j % 2, :], bank[:], ACT.Silu, bias=b1[:, bass.ds(e * HT + j, 1)]) \
                                .then_inc(s_["silu"], 1)
                        else:
                            nc.scalar.activation(act_h[:, j % 2, :], bank[:], ACT.Silu).then_inc(s_["silu"], 1)
                        act.wait_ge(s_["wh"], e * HT + j + 1)
                        if j >= 2:
                            act.wait_ge(s_["y_tile"], e * HT + j - 1)
                        else:
                            act.wait_ge(s_["y_tile"], e * HT)
                        nc.scalar.copy(hhi[:, j % 2, :], wh[:, j % 2, :]).then_inc(s_["hhi"], 1)

            @block.vector
            def _(dve):
                with dve.Fori(0, NE) as e:
                    for j in range(HT):
                        weight = weB[:, bass.ds(e, 1), :].rearrange("p o t -> p (o t)")
                        dve.wait_ge(s_["silu"], e * HT + j + 1)
                        bank = ps[4 + (j % 2) * (1 + up)]
                        if layer == 0:
                            nc.vector.tensor_tensor(wh[:, j % 2, :], act_h[:, j % 2, :], weight, ALU.mult).then_inc(s_["wh"], 1)
                        else:
                            nc.vector.tensor_tensor(act_h[:, j % 2, :], act_h[:, j % 2, :], ps[4 + (j % 2) * 2 + 1][:], ALU.mult) \
                                .then_inc(s_["h_read"], 1)
                            dve.wait_ge(s_["h_read"], e * HT + j + 1)
                            nc.vector.tensor_tensor(wh[:, j % 2, :], act_h[:, j % 2, :], weight, ALU.mult).then_inc(s_["wh"], 1)
                        dve.wait_ge(s_["hhi"], e * HT + j + 1)
                        nc.vector.tensor_tensor(hlo[:, j % 2, :], wh[:, j % 2, :], f32(hhi[:, j % 2, :]), ALU.subtract) \
                            .then_inc(s_["hlo"], 1)
                dve.wait_ge(s_["y_tile"], NE * HT)
                for b in range(NB):
                    nc.vector.tensor_tensor(x[:, b, :], x[:, b, :], Y[b][:], ALU.add).then_inc(s_["out"], 1)


def stage_rwkv(nc, k, t, x_in, x_out):
    with ExitStack() as ctx:
        m = Mem(nc, ctx, "rwkv")
        x, z, zn = m.sb("x", [P, NB, D]), m.sb("z", [P, NB, D]), m.sb("zn", [P, NB, D])
        zT = m.sb("zT", [P, C, NB, P])
        prev = m.sb("prev", [P, C, NB, P])
        mixed = [m.sb(f"mixed{i}", [P, C, NB, P]) for i in range(3)]
        w = [m.sb(f"w{i}", [P, C, D]) for i in range(4)]
        cols = m.sb("cols", [P, 6, C])
        one_minus = m.sb("one_minus", [P, 3, C])
        decay = m.sb("decay", [P, C])
        vT = m.sb("vT", [P, C, TOK])
        kv = m.sb("kv", [P, C, NB, P])
        state = m.sb("state", [P, C, NB, P])
        rate = m.sb("rate", [P, C, P])
        r = m.sb("r", [P, NB, D])
        stats, mv = m.sb("stats", [P, NB, 6]), m.sb("mv", [P, NB, 2])
        ve, std, rstd = m.sb("ve", [P, 2, NB]), m.sb("std", [P, 2, NB]), m.sb("rstd", [P, 2, NB])
        names = ("ln_w", "ln_b", "tmk", "tmv", "tmr", "decay_w")
        s_ = {n: m.sem(n) for n in ("x_in", "c_in", "w_in", "dstep", "var", "std", "zn", "turned", "zT", "decay", "mixed", "v_made",
                                    "vT", "k_made", "kv", "state", "r_made", "r", "o_made", "rate", "done", "stored")}
        ps = k["ps"]
        with nc.Block() as block:
            @block.sync
            def _(sp):
                sp.dma_start(x[:], x_in.rearrange("b p d -> p b d")).then_inc(s_["x_in"], 16)
                for i, n in enumerate(names):
                    sp.dma_start(cols[:, i, :], t["L1_attn_" + n]).then_inc(s_["c_in"], 16)
                for i, n in enumerate(("Wv", "Wk", "Wr", "Wo")):
                    sp.dma_start(w[i][:], t["L1_attn_" + n]).then_inc(s_["w_in"], 16)
                sp.wait_ge(s_["done"], NB)
                sp.dma_start(x_out.rearrange("b p d -> p b d"), x[:]).then_inc(s_["stored"], 16)
                sp.wait_ge(s_["stored"], 16)

            @block.tensor
            def _(pe):
                for c in range(C):
                    pe.wait_ge(s_["zn"], NB)
                    if c >= 2:
                        pe.wait_ge(s_["zT"], c - 1)
                    for b in range(NB):
                        last = pe.transpose(ps[c % 2][:, b * P:(b + 1) * P], zn[:, b, c * P:(c + 1) * P], k["ident"][:])
                    last.then_inc(s_["turned"], 1)
                pe.wait_ge(s_["w_in"], 64)
                flat = [x_[:].rearrange("p c b t -> p c (b t)") for x_ in mixed]
                pe.wait_ge(s_["zT"], C)
                for i, (src, made, banks) in enumerate(((1, "v_made", (2, 3, 4, 5)), (0, "k_made", (6, 7, 0, 1)))):
                    pe.wait_ge(s_["mixed"], C * (i + 1))
                    for o in range(C):
                        for c in range(C):
                            last = pe.matmul(ps[banks[o]][:], w[i][:, c, o * P:(o + 1) * P], flat[src][:, c, :],
                                             start=(c == 0), stop=(c == C - 1))
                        last.then_inc(s_[made], 1)
                pe.wait_ge(s_["vT"], C)
                pe.wait_ge(s_["mixed"], 3 * C)
                for b in range(NB):
                    for c in range(C):
                        last = pe.matmul(ps[2 + b][:], mixed[2][:, c, b, :], w[2][:, c, :], start=(c == 0), stop=(c == C - 1))
                    last.then_inc(s_["r_made"], 1)
                pe.wait_ge(s_["state"], C * NB)
                for b in range(NB):
                    for c in range(C):
                        last = pe.matmul(ps[(6 + b) % 8][:], state[:, c, b, :], w[3][:, c, :], start=(c == 0), stop=(c == C - 1))
                    last.then_inc(s_["o_made"], 1)

            @block.scalar
            def _(act):
                for i in range(2):
                    act.wait_ge(s_["var"], i + 1)
                    nc.scalar.sqrt(std[:, i, :], ve[:, i, :]).then_inc(s_["std"], 1)
                act.wait_ge(s_["c_in"], 16 * len(names))
                nc.scalar.activation(decay[:], cols[:, 5, :], ACT.Sigmoid).then_inc(s_["decay"], 1)
                for o in range(C):
                    act.wait_ge(s_["v_made"], o + 1)
                    nc.scalar.copy(vT[:, o, :], ps[2 + o][:]).then_inc(s_["vT"], 1)
                for b in range(NB):
                    act.wait_ge(s_["r_made"], b + 1)
                    nc.scalar.activation(r[:, b, :], ps[2 + b][:], ACT.Sigmoid).then_inc(s_["r"], 1)

            @block.gpsimd
            def _(pool):
                nc.gpsimd.memset(prev[:, :, :, 0:1], 0.0).then_inc(s_["rate"], 1)
                pool.wait_ge(s_["decay"], 1)
                nc.gpsimd.tensor_copy(rate[:], decay[:].unsqueeze(2).to_broadcast([P, C, P])).then_inc(s_["rate"], 1)

            @block.vector
            def _(dve):
                s = Steps(dve, s_["dstep"])
                dve.wait_ge(s_["x_in"], 16)
                for i, (src, dst) in enumerate(((x, z), (z, zn))):
                    for b in range(NB):
                        s.mark(nc.vector.bn_stats(stats[:, b, :], src[:, b, :]))
                    s.wait()
                    for b in range(NB):
                        s.mark(nc.vector.bn_aggr(mv[:, b, :], stats[:, b, :]))
                    s.wait()
                    nc.vector.tensor_scalar_add(ve[:, i, :], mv[:, :, 1], LN_EPS).then_inc(s_["var"], 1)
                    dve.wait_ge(s_["std"], i + 1)
                    s.then(nc.vector.reciprocal(rstd[:, i, :], std[:, i, :]))
                    for b in range(NB):
                        ins = nc.vector.tensor_scalar(dst[:, b, :], src[:, b, :], mv[:, b, 0:1], rstd[:, i, b:b + 1],
                                                      ALU.subtract, ALU.mult)
                        if i:
                            ins.then_inc(s_["zn"], 1)
                        else:
                            s.mark(ins)
                    if not i:
                        s.wait()
                dve.wait_ge(s_["c_in"], 16 * len(names))
                s.mark(nc.vector.tensor_scalar(one_minus[:], cols[:, 2:5, :], -1.0, 1.0, ALU.mult, ALU.add))
                for c in range(C):
                    dve.wait_ge(s_["turned"], c + 1)
                    nc.vector.tensor_scalar(zT[:, c].rearrange("p b t -> p (b t)"), ps[c % 2][:], cols[:, 0, c:c + 1],
                                            cols[:, 1, c:c + 1], ALU.mult, ALU.add).then_inc(s_["zT"], 1)
                dve.wait_ge(s_["zT"], C)
                dve.wait_ge(s_["rate"], 1)
                for i in (1, 0, 2):
                    for c in range(C):
                        s.mark(nc.vector.tensor_scalar(prev[:, c, :, 1:P], zT[:, c, :, 0:P - 1], one_minus[:, i, c:c + 1],
                                                       None, ALU.mult))
                    s.wait()
                    for c in range(C):
                        nc.vector.scalar_tensor_tensor(out=mixed[i][:, c], in0=zT[:, c], scalar=cols[:, 2 + i, c:c + 1],
                                                       in1=prev[:, c], op0=ALU.mult, op1=ALU.add).then_inc(s_["mixed"], 1)
                    dve.wait_ge(s_["mixed"], C * {1: 1, 0: 2, 2: 3}[i])
                for o in range(C):
                    dve.wait_ge(s_["k_made"], o + 1)
                    dve.wait_ge(s_["vT"], o + 1)
                    nc.vector.tensor_tensor(kv[:, o].rearrange("p b t -> p (b t)"), vT[:, o, :], ps[(6 + o) % 8][:], ALU.mult) \
                        .then_inc(s_["kv"], 1)
                dve.wait_ge(s_["rate"], 2)
                dve.wait_ge(s_["kv"], C)
                for o in range(C):
                    for b in range(NB):
                        nc.vector.tensor_tensor_scan(state[:, o, b, :], rate[:, o, :], kv[:, o, b, :], 0.0, ALU.mult, ALU.add) \
                            .then_inc(s_["state"], 1)
                for b in range(NB):
                    s.mark(nc.vector.tensor_tensor(x[:, b, :], x[:, b, :], z[:, b, :], ALU.add))
                for b in range(NB):
                    dve.wait_ge(s_["o_made"], b + 1)
                    dve.wait_ge(s_["r"], b + 1)
                    s.mark(nc.vector.tensor_tensor(r[:, b, :], r[:, b, :], ps[(6 + b) % 8][:], ALU.mult))
                s.wait()
                for b in range(NB):
                    nc.vector.tensor_tensor(x[:, b, :], x[:, b, :], r[:, b, :], ALU.add).then_inc(s_["done"], 1)




def build(nc, t, out, stages=99):
    def dram(name, shape, dt=F32):
        return nc.dram_tensor(name, shape, dt, kind="Internal").ap()

    xs = [t["x"]] + [dram(f"x_{i}", (NB, P, D)) for i in range(1, 6)] + [out]
    q_hi, q_lo = dram("q_hi", (NB, P, C, P)), dram("q_lo", (NB, P, C, P))
    attn = dram("attn", (NB, P, D))
    with ExitStack() as ctx:
        k = {
            "ident": ctx.enter_context(nc.sbuf_tensor("ident", [P, P], F32)),
            "ones": ctx.enter_context(nc.sbuf_tensor("ones", [P, P], F32)),
        }
        k["ps2"] = [ctx.enter_context(nc.psum_tensor(f"wide{i}", [P, 2 * 512], F32)) for i in range(2)]
        one = [ctx.enter_context(nc.psum_tensor(f"bank{i}", [P, 512], F32)) for i in range(4, 8)]
        k["ps"] = [k["ps2"][0][:, 0:512], k["ps2"][0][:, 512:1024], k["ps2"][1][:, 0:512], k["ps2"][1][:, 512:1024]] \
            + [x[:, :] for x in one]
        stage_constants(nc, k)

        def cross(layer, x_in, x_out, mask):
            L = f"L{layer}_xattn_"
            with ExitStack() as inner:
                weights = [tuple(inner.enter_context(nc.sbuf_tensor(f"{L}{w}_{p}", [P, C * D], F32R)) for p in ("hi", "lo"))
                           for w in ("wk", "wv")]
                if mask is not None:
                    k["bias"] = inner.enter_context(nc.sbuf_tensor("mask_bias", [P, KEYS], BF16))
                stage_project_q(nc, k, f"q{layer}", x_in, t[L + "Wq"], t[L + "bq"], t[L + "Wk"], t[L + "Wv"], weights,
                                q_hi, q_lo, mask)
                stage_attention(nc, k, f"a{layer}", t["ctx_1024"], weights, t[L + "bk"], q_hi, q_lo, attn, mask is not None)
            norm = layer == 1
            stage_attention_output(nc, k, f"o{layer}", attn, t[L + "bv"], t[L + "Wo"], t[L + "bo"],
                                   t[L + "gamma"] if norm else None, t[L + "beta"] if norm else None, x_in, x_out)

        def last(i):
            return out if stages == i else xs[i]

        cross(0, xs[0], last(1), t["mask_1x1xSxS2_bk0"])
        if stages >= 2:
            stage_retention(nc, k, t, xs[1], last(2))
        if stages >= 3:
            stage_experts(nc, k, "moe0", t, xs[2], last(3), 0)
        if stages >= 4:
            cross(1, xs[3], last(4), None)
        if stages >= 5:
            stage_rwkv(nc, k, t, xs[4], last(5))
        if stages >= 6:
            stage_experts(nc, k, "moe1", t, xs[5], out, 1)


def _tiles(a):
    return a.reshape(-1, P, a.shape[-1]).transpose(1, 0, 2)


def _columns(a):
    return a.reshape(-1, P).T


def _layout(name, a):
    if name == "ctx_1024":
        return a.reshape(NB, NCH, CH, C, P).transpose(0, 1, 4, 3, 2).reshape(NB * NCH, P, C * CH)
    if name == "mask_1x1xSxS2_bk0":
        return a.reshape(P, KEYS)
    if "_xattn_W" in name or name in ("L1_attn_Wk", "L1_attn_Wv", "L1_attn_Wr", "L1_attn_Wo"):
        w = _tiles(a.T)
        return w.reshape(P, C * D) if name.endswith(("_Wk", "_Wv")) and "xattn" in name else w
    if name in ("L0_attn_w_attn", "L0_attn_w_proj", "L0_ffn_rw1", "L0_ffn_rw2", "L1_ffn_router_w"):
        return _tiles(a)
    if name == "L0_ffn_w1":
        return a.reshape(NE, C, P, C, D).transpose(0, 3, 2, 1, 4).reshape(NE * C, P, C * D)
    if name == "L0_ffn_w2":
        return a.reshape(NE, C, C, P, D).transpose(0, 1, 3, 2, 4).reshape(NE * C, P, C * D)
    if name in ("L1_ffn_we_gate", "L1_ffn_we_up", "L1_ffn_we_down"):
        return a.reshape(NE, C, P, D).transpose(0, 2, 1, 3).reshape(NE, P, C * D)
    if name == "L0_ffn_b1":
        return a.reshape(NE, HID // P, P).transpose(2, 0, 1).reshape(P, NE * HID // P)
    if name in ("L0_xattn_bq", "L0_xattn_bk", "L1_xattn_bq", "L1_xattn_bk", "L0_ffn_rb1", "L1_attn_ln_w", "L1_attn_ln_b",
                "L1_attn_tmk", "L1_attn_tmv", "L1_attn_tmr", "L1_attn_decay_w"):
        return _columns(a)
    return a


def _rotary():
    div = (2.0 * np.pi / float(P) ** (np.arange(0, RD, 2, dtype=np.float32) / RD)).astype(np.float32)
    ang = (np.arange(P, dtype=np.float32)[:, None] * div[None, :]).astype(np.float32)
    cos = np.repeat(np.cos(ang), 2, axis=-1)
    sin = np.repeat(np.sin(ang), 2, axis=-1)
    sin[:, 0::2] *= -1.0
    return np.stack([cos, sin], 1).astype(np.float32)


def kernel(**inputs):
    import concourse.bacc as _bacc
    from concourse import mybir as _mybir
    from concourse.bass_utils import run_bass_kernel_spmd as _run

    nc = _bacc.Bacc("TRN2", target_bir_lowering=False, num_devices=1)
    arrays, t = {}, {}
    inputs = dict(inputs, rotary=_rotary())
    for name, a in inputs.items():
        a = np.ascontiguousarray(_layout(name, np.asarray(a)))
        arrays[f"in_{name}"] = a
        t[name] = nc.dram_tensor(f"in_{name}", a.shape, _mybir.dt.from_np(a.dtype), kind="ExternalInput").ap()
    out = nc.dram_tensor("out_x", (NB, P, D), _mybir.dt.float32, kind="ExternalOutput").ap()
    build(nc, t, out, STAGES)
    r = _run(nc, [arrays], core_ids=[0])
    return r.results[0]["out_x"]


STAGES = 99
```

```python
from contextlib import ExitStack

import numpy as np

import concourse.bass as bass
from concourse import mybir
from concourse.alu_op_type import AluOpType as ALU

ACT = mybir.ActivationFunctionType
AX = mybir.AxisListType
F32 = mybir.dt.float32
F32R = mybir.dt.float32r
BF16 = mybir.dt.bfloat16
U8 = mybir.dt.uint8
U32 = mybir.dt.uint32

P = 128
D = 512
C = D // P
NB = 4
TOK = NB * P
KEYS = 2048
HEADS = 16
HD = D // HEADS
HPT = P // HD
CH = 256
KT = KEYS // P
QH, KVH, RD = 16, 8, 64
NE = 8
HID = 2048
LN_EPS = 1e-5
NEG = -1e9


class Mem:

    def __init__(self, nc, ctx, stage):
        self.nc, self.ctx, self.stage = nc, ctx, stage
        self.sems = []
        ctx.callback(self.clear)

    def sb(self, name, shape, dt=F32):
        return self.ctx.enter_context(self.nc.sbuf_tensor(f"{self.stage}_{name}", shape, dt))

    def sem(self, name):
        self.sems.append(self.nc.alloc_semaphore(f"{self.stage}_{name}"))
        return self.sems[-1]

    def clear(self):
        if self.sems:
            self.nc.clear_and_free_semaphores(self.sems)
            self.nc.all_engine_barrier()


class Steps:

    def __init__(self, engine, sem, turn=0, per_turn=0):
        self.engine, self.sem, self.base, self.n = engine, sem, turn * per_turn, 0

    def then(self, ins):
        self.mark(ins)
        self.engine.wait_ge(self.sem, self.base + self.n)

    def mark(self, ins):
        ins.then_inc(self.sem, 1)
        self.n += 1

    def wait(self):
        self.engine.wait_ge(self.sem, self.base + self.n)


def f32(ap):
    return ap.bitcast(F32)


def three_products(pe, out, w_hi, w_lo, m_hi, m_lo, start, stop, check=True):
    pe.matmul(out, w_hi, m_hi, start=start, stop=False, skip_group_check=not check)
    pe.matmul(out, w_hi, m_lo, start=False, stop=False, skip_group_check=not check)
    return pe.matmul(out, w_lo, m_hi, start=False, stop=stop, skip_group_check=not check)


def stage_constants(nc, k):
    with ExitStack() as ctx:
        m = Mem(nc, ctx, "const")
        filled, cut = m.sem("filled"), m.sem("cut")
        with nc.Block() as block:
            @block.gpsimd
            def _(pool):
                nc.gpsimd.memset(k["ident"][:], 0.0).then_inc(filled, 1)
                nc.gpsimd.memset(k["ones"][:], 1.0).then_inc(filled, 1)
                pool.wait_ge(filled, 2)
                nc.gpsimd.affine_select(out=k["ident"][:], in_=k["ident"][:], compare_op=ALU.not_equal, fill=1.0,
                                        base=0, pattern=[[-1, P]], channel_multiplier=1).then_inc(cut, 1)


def stage_project_q(nc, k, name, x_in, wq, bq, wk, wv, weights, q_hi_out, q_lo_out, mask):
    with ExitStack() as ctx:
        m = Mem(nc, ctx, name)
        x = m.sb("x", [P, NB, D])
        xn = m.sb("xn", [P, NB, D])
        xT = m.sb("xT", [P, C, TOK])
        wqT = m.sb("wqT", [P, C, D])
        wraw = m.sb("wraw", [P, 2, C * D])
        bcol = m.sb("bcol", [P, C])
        qf = m.sb("qf", [P, C, TOK])
        qhi = m.sb("qhi", [P, C, TOK], F32R)
        qlo = m.sb("qlo", [P, C, TOK], F32R)
        stats = m.sb("stats", [P, NB, 6])
        mv = m.sb("mv", [P, NB, 2])
        ve = m.sb("ve", [P, NB])
        std = m.sb("std", [P, NB])
        rstd = m.sb("rstd", [P, NB])
        x_in_sem, w_in, wq_in, b_in = m.sem("x_in"), m.sem("w_in"), m.sem("wq_in"), m.sem("b_in")
        dstep, var_ready, std_ready, xn_ready = m.sem("dstep"), m.sem("var"), m.sem("std"), m.sem("xn")
        turned, xT_ready, q_made = m.sem("turned"), m.sem("xT"), m.sem("q_made")
        lo_ready, whi_ready, wlo_ready, q_out = (m.sem(s) for s in ("lo", "whi", "wlo", "q_out"))
        if mask is not None:
            mraw = m.sb("mraw", [P, KEYS], U8)
            many = m.sb("many", [P, 1])
            manyr = m.sb("manyr", [P, P])
            manyT = m.sb("manyT", [P, P])
            m_in, any_ready, any_turned = m.sem("m_in"), m.sem("any_ready"), m.sem("any_turned")
        ps = k["ps"]
        with nc.Block() as block:
            @block.sync
            def _(sp):
                sp.dma_start(x[:], x_in.rearrange("b p d -> p b d")).then_inc(x_in_sem, 16)
                sp.dma_start(wqT[:], wq).then_inc(wq_in, 16)
                sp.dma_start(bcol[:], bq).then_inc(b_in, 16)
                if mask is not None:
                    sp.dma_start(mraw[:], mask).then_inc(m_in, 16)
                sp.dma_start(wraw[:, 0, :], wk).then_inc(w_in, 16)
                sp.dma_start(wraw[:, 1, :], wv).then_inc(w_in, 16)
                sp.wait_ge(lo_ready, C)
                for b in range(NB):
                    sp.dma_start(q_hi_out[b], f32(qhi[:, :, b * P:(b + 1) * P])).then_inc(q_out, 16)
                    sp.dma_start(q_lo_out[b], f32(qlo[:, :, b * P:(b + 1) * P])).then_inc(q_out, 16)
                sp.wait_ge(q_out, 32 * NB)

            @block.vector
            def _(dve):
                s = Steps(dve, dstep)
                dve.wait_ge(x_in_sem, 16)
                for b in range(NB):
                    s.mark(nc.vector.bn_stats(stats[:, b, :], x[:, b, :]))
                s.wait()
                for b in range(NB):
                    s.mark(nc.vector.bn_aggr(mv[:, b, :], stats[:, b, :]))
                s.wait()
                nc.vector.tensor_scalar_add(ve[:], mv[:, :, 1], LN_EPS).then_inc(var_ready, 1)
                dve.wait_ge(std_ready, 1)
                s.then(nc.vector.reciprocal(rstd[:], std[:]))
                for b in range(NB):
                    nc.vector.tensor_scalar(xn[:, b, :], x[:, b, :], mv[:, b, 0:1], rstd[:, b:b + 1],
                                            ALU.subtract, ALU.mult).then_inc(xn_ready, 1)
                if mask is not None:
                    dve.wait_ge(m_in, 16)
                    s.then(nc.vector.reduce_max(many[:], mraw[:], AX.X))
                    nc.vector.tensor_scalar(manyr[:], k["ones"][:], many[:, 0:1], None, ALU.mult).then_inc(any_ready, 1)
                    dve.wait_ge(any_turned, 1)
                    s.mark(nc.vector.tensor_copy(manyT[:], ps[7][:, 0:P]))
                for c in range(C):
                    dve.wait_ge(turned, c + 1)
                    nc.vector.tensor_copy(xT[:, c, :], ps[c % 2][:]).then_inc(xT_ready, 1)
                if mask is not None:
                    s.wait()
                dve.wait_ge(b_in, 16)
                for c in range(C):
                    dve.wait_ge(q_made, c + 1)
                    s.then(nc.vector.tensor_scalar(qf[:, c, :], ps[2 + c][:], bcol[:, c:c + 1], float(HD) ** -0.5,
                                                   ALU.add, ALU.mult))
                    if mask is not None:
                        for b in range(NB):
                            s.mark(nc.vector.tensor_tensor(qf[:, c, b * P:(b + 1) * P], qf[:, c, b * P:(b + 1) * P],
                                                           manyT[:], ALU.mult))
                        s.wait()
                    s.then(nc.vector.tensor_copy(qhi[:, c, :], qf[:, c, :]))
                    nc.vector.tensor_tensor(qlo[:, c, :], qf[:, c, :], f32(qhi[:, c, :]), ALU.subtract).then_inc(lo_ready, 1)
                dve.wait_ge(w_in, 32)
                for i, (hi, lo) in enumerate(weights):
                    dve.wait_ge(whi_ready, i + 1)
                    nc.vector.tensor_tensor(lo[:], wraw[:, i, :], f32(hi[:]), ALU.subtract).then_inc(wlo_ready, 1)

            @block.scalar
            def _(act):
                act.wait_ge(var_ready, 1)
                nc.scalar.sqrt(std[:], ve[:]).then_inc(std_ready, 1)
                act.wait_ge(w_in, 32)
                for i, (hi, lo) in enumerate(weights):
                    nc.scalar.copy(hi[:], wraw[:, i, :]).then_inc(whi_ready, 1)

            @block.tensor
            def _(pe):
                if mask is not None:
                    pe.wait_ge(any_ready, 1)
                    pe.transpose(ps[7][:, 0:P], manyr[:], k["ident"][:]).then_inc(any_turned, 1)
                for c in range(C):
                    pe.wait_ge(xn_ready, NB)
                    if c >= 2:
                        pe.wait_ge(xT_ready, c - 1)
                    for b in range(NB):
                        last = pe.transpose(ps[c % 2][:, b * P:(b + 1) * P], xn[:, b, c * P:(c + 1) * P], k["ident"][:])
                    last.then_inc(turned, 1)
                pe.wait_ge(xT_ready, C)
                pe.wait_ge(wq_in, 16)
                for o in range(C):
                    for c in range(C):
                        last = pe.matmul(ps[2 + o][:], wqT[:, c, o * P:(o + 1) * P], xT[:, c, :],
                                         start=(c == 0), stop=(c == C - 1))
                    last.then_inc(q_made, 1)


def prime(engine, *sems):
    for s in sems:
        engine.sem_inc(s, 1)


def stage_attention(nc, k, name, ctxT, weights, bk, q_hi_in, q_lo_in, attn, mask):
    (wk_hi, wk_lo), (wv_hi, wv_lo) = weights
    masked = mask is not None
    KC = CH
    NKC = KEYS // KC
    KG, VG = NKC * C, KT
    PAIR = 2 * P
    U = HEADS // 2
    AG = 2
    NA = KT // AG
    NG, GT = 4, KT // 4
    VW = HD + 1
    ODD = 64
    pool_groups = (0, 1, 2, 3) if masked else (1, 3)
    dve_groups = tuple(g for g in range(NG) if g not in pool_groups)
    with ExitStack() as ctx:
        m = Mem(nc, ctx, name)
        raw = m.sb("raw", [P, C, KC])
        chi, clo = m.sb("chi", [P, 2, C, KC], F32R), m.sb("clo", [P, 2, C, KC], F32R)
        khi, klo = m.sb("khi", [P, C, KEYS], F32R), m.sb("klo", [P, C, KEYS], F32R)
        v = m.sb("v", [P, KT, HEADS, VW])
        q_hi, q_lo = m.sb("q_hi", [P, 2, PAIR], F32R), m.sb("q_lo", [P, 2, PAIR], F32R)
        st = m.sb("st", [P, 2, KT, PAIR])
        mxh = m.sb("mxh", [P, 2, PAIR])
        nmax = m.sb("nmax", [P, 2])
        diag = m.sb("diag", [P, 2, P])
        nmB = m.sb("nmB", [P, 2, PAIR])
        oT = m.sb("oT", [P, 2, P])
        rden = m.sb("rden", [P, 2, 2])
        bkcol = m.sb("bkcol", [P, C])
        sem = m.sem
        bk_in, raw_in, chi_ready, clo_ready, cleared = (sem(s) for s in ("bk_in", "raw_in", "chi", "clo", "cleared"))
        k_made, khi_done, k_done, v_made, v_done = (sem(s) for s in ("k_made", "khi_done", "k_done", "v_made", "v_done"))
        q_in = [sem(f"q_in_{i}") for i in range(2)]
        scored, kept, half_max, max_turned = (sem(s) for s in ("scored", "kept", "half_max", "max_turned"))
        max_row, diag_made, max_spread, nmB_ready = (sem(s) for s in ("max_row", "diag", "max_spread", "nmB"))
        sub_pool, sub_dve, exp_done, pv_done = (sem(s) for s in ("sub_pool", "sub_dve", "exp", "pv"))
        o_kept, o_turned, rden_done, o_done = (sem(s) for s in ("o_kept", "o_turned", "rden", "o_done"))
        ps = k["ps"]
        A = ps[0:3]
        MT, MB = ps[3], ps[4]
        O = ps[5:7]
        OT = ps[7]
        KB, VB = ps[0:2], ps[3:5]
        if masked:
            hidden = m.sb("hidden", [P, KT, P], U8)
            mraw = st[:, 0].rearrange("p t q -> p (t q)").bitcast(U8)[:, 0:KEYS]
            m_in, hidden_ready = sem("m_in"), sem("hidden")

        with nc.Block() as block:
            @block.sync
            def _(sp):
                sp.dma_start(bkcol[:], bk).then_inc(bk_in, 16)
                if masked:
                    sp.dma_start(mraw, mask).then_inc(m_in, 16)
                sp.wait_ge(cleared, 4)
                with sp.Fori(0, NB) as b:
                    for ch in range(NKC):
                        sp.wait_ge(clo_ready, b * NKC + ch + 1)
                        sp.dma_start(raw[:].rearrange("p c n -> p (c n)"),
                                     ctxT[bass.ds(b * NKC + ch, 1)].rearrange("o p n -> (o p) n")).then_inc(raw_in, 16)
                    for u in range(U):
                        sp.wait_ge(scored, b * U * NA + max(u - 1, 0) * NA + 1)
                        for part, src in ((q_hi, q_hi_in), (q_lo, q_lo_in)):
                            for i in range(2):
                                r = ((2 * u + i) % HPT) * HD
                                sp.dma_start(f32(part[r:r + HD, u % 2, i * P:(i + 1) * P]),
                                             src[bass.ds(b, 1), r:r + HD, u // 2, :].rearrange("o p t -> (o p) t")) \
                                    .then_inc(q_in[u % 2], 16)

            @block.gpsimd
            def _(pool):
                nc.gpsimd.memset(f32(q_hi[:]), 0.0).then_inc(cleared, 1)
                nc.gpsimd.memset(f32(q_lo[:]), 0.0).then_inc(cleared, 1)
                nc.gpsimd.memset(oT[:], 0.0).then_inc(cleared, 1)
                nc.gpsimd.memset(v[:, :, :, HD:VW], 1.0).then_inc(cleared, 1)
                prime(pool, sub_pool)
                with pool.Fori(0, NB) as b:
                    for u in range(U):
                        for i, g in enumerate(pool_groups):
                            pool.wait_ge(nmB_ready, b * U + u + 2)
                            nc.gpsimd.tensor_tensor(st[:, u % 2, g * GT:(g + 1) * GT, :], st[:, u % 2, g * GT:(g + 1) * GT, :],
                                                    nmB[:, u % 2, :].unsqueeze(1).to_broadcast([P, GT, PAIR]), ALU.add) \
                                .then_inc(sub_pool, 1)

            @block.tensor
            def _(pe):
                prime(pe, scored, pv_done, o_turned, max_spread)
                with pe.Fori(0, NB) as b:
                    for ch in range(NKC):
                        pe.wait_ge(clo_ready, b * NKC + ch + 2)
                        for i in range(C + KC // P):
                            if i % 3 == 2:
                                t = i // 3
                                g = ch * 2 + t
                                if g == 0:
                                    pe.wait_ge(max_row, b * U + 1)
                                if g == 1:
                                    pe.wait_ge(nmB_ready, b * U + 1)
                                pe.wait_ge(v_done, b * VG + max(g - 1, 0) + 1)
                                for c in range(C):
                                    last = three_products(pe, VB[t][:], chi[:, ch % 2, c, t * P:(t + 1) * P],
                                                          clo[:, ch % 2, c, t * P:(t + 1) * P],
                                                          wv_hi[:, c * D:(c + 1) * D], wv_lo[:, c * D:(c + 1) * D],
                                                          c == 0, c == C - 1)
                                last.then_inc(v_made, 1)
                            else:
                                o = i - i // 3
                                g = ch * C + o
                                if g < 2:
                                    pe.wait_ge(kept, b * U * NA + 1)
                                pe.wait_ge(k_done, b * KG + max(g - 1, 0) + 1)
                                for c in range(C):
                                    at = c * D + o * P
                                    last = three_products(pe, KB[o % 2][:, 0:KC], wk_hi[:, at:at + P], wk_lo[:, at:at + P],
                                                          chi[:, ch % 2, c, :], clo[:, ch % 2, c, :], c == 0, c == C - 1)
                                last.then_inc(k_made, 1)
                    pe.wait_ge(k_done, b * KG + KG + 1)
                    pe.wait_ge(v_done, b * VG + VG + 1)

                    def scores(u, j):
                        n = u * NA + j
                        if j == 0:
                            pe.wait_ge(q_in[u % 2], 64 * (b * (U // 2) + u // 2) + 64)
                        pe.wait_ge(kept, b * U * NA + max(n - 2, 0) + 1)
                        for i in range(AG):
                            t = j * AG + i
                            last = three_products(pe, A[n % 3][:, i * PAIR:(i + 1) * PAIR], khi[:, u // 2, t * P:(t + 1) * P],
                                                  klo[:, u // 2, t * P:(t + 1) * P], q_hi[:, u % 2, :], q_lo[:, u % 2, :],
                                                  True, True)
                        last.then_inc(scored, 1)

                    def turn_max(u):
                        pe.wait_ge(half_max, 2 * (b * U + u) + 3)
                        for half in range(2):
                            for i in range(2):
                                last = pe.transpose(MT[:, (2 * half + i) * P:(2 * half + i + 1) * P],
                                                    mxh[:, half, i * P:(i + 1) * P], k["ident"][:])
                        last.then_inc(max_turned, 1)

                    def spread_max(u):
                        pe.wait_ge(diag_made, b * U + u + 2)
                        pe.wait_ge(nmB_ready, b * U + u + 1)
                        pe.matmul(MB[:, 0:PAIR], k["ones"][:], diag[:].rearrange("p h q -> p (h q)"),
                                  start=True, stop=True).then_inc(max_spread, 1)

                    def outputs(u, g):
                        pe.wait_ge(exp_done, NG * (b * U + u) + g + 1)
                        if g == 0:
                            pe.wait_ge(o_kept, b * U + max(u - 1, 0) + 1)
                        for t in range(g * GT, (g + 1) * GT):
                            for i in range(2):
                                last = pe.matmul(O[u % 2][i * ODD:i * ODD + VW, 0:P], v[:, t, 2 * u + i, :],
                                                 st[:, u % 2, t, i * P:(i + 1) * P], start=(t == 0), stop=(t == KT - 1))
                        last.then_inc(pv_done, 1)

                    def turn_output(u):
                        pe.wait_ge(o_kept, b * U + u + 2)
                        pe.wait_ge(o_done, b * U + u + 1)
                        pe.transpose(OT[:, 0:ODD + VW], oT[0:ODD + VW, u % 2, :], k["ident"][0:ODD + VW, 0:ODD + VW]) \
                            .then_inc(o_turned, 1)

                    for j in range(NA):
                        scores(0, j)
                    for u in range(U + 1):
                        for g in range(NG):
                            if u >= 1:
                                outputs(u - 1, g)
                            if u + 1 < U:
                                scores(u + 1, 2 * g)
                                scores(u + 1, 2 * g + 1)
                            if g == 0:
                                if u < U:
                                    turn_max(u)
                                if u >= 2:
                                    turn_output(u - 2)
                            if g == 1 and u < U:
                                spread_max(u)
                    turn_output(U - 1)

            @block.vector
            def _(dve):
                prime(dve, clo_ready, k_done, half_max, max_row, diag_made, sub_dve, rden_done, o_done)
                if masked:
                    prime(dve, kept)
                    dve.wait_ge(m_in, 16)
                    nc.vector.tensor_scalar(hidden[:].rearrange("p t q -> p (t q)"), mraw, -1.0, 1.0, ALU.mult, ALU.add) \
                        .then_inc(hidden_ready, 1)
                    dve.wait_ge(hidden_ready, 1)
                dve.wait_ge(bk_in, 16)
                with dve.Fori(0, NB) as b:
                    for ch in range(NKC):
                        dve.wait_ge(chi_ready, b * NKC + ch + 1)
                        nc.vector.tensor_tensor(clo[:, ch % 2], raw[:], f32(chi[:, ch % 2]), ALU.subtract).then_inc(clo_ready, 1)
                        for o in range(C):
                            g = ch * C + o
                            dve.wait_ge(khi_done, b * KG + g + 1)
                            at = slice(ch * KC, (ch + 1) * KC)
                            nc.vector.scalar_tensor_tensor(out=klo[:, o, at], in0=KB[o % 2][:, 0:KC], scalar=bkcol[:, o:o + 1],
                                                           in1=f32(khi[:, o, at]), op0=ALU.add, op1=ALU.subtract) \
                                .then_inc(k_done, 1)

                    def keep(u, j):
                        n = u * NA + j
                        dve.wait_ge(scored, b * U * NA + n + 2)
                        done = (u - 2) * NG + j // 2 + 1 if u >= 2 else 0
                        dve.wait_ge(pv_done, b * U * NG + done + 1)
                        for i in range(AG):
                            t = j * AG + i
                            ins = nc.vector.scalar_tensor_tensor(
                                out=st[:, u % 2, t, :].rearrange("p (h q) -> p h q", h=2),
                                in0=hidden[:, t, :].unsqueeze(1).to_broadcast([P, 2, P]), scalar=NEG,
                                in1=A[n % 3][:, i * PAIR:(i + 1) * PAIR].rearrange("p (h q) -> p h q", h=2),
                                op0=ALU.mult, op1=ALU.add)
                        ins.then_inc(kept, 1)

                    def reduce_half(u, half):
                        if half == 0:
                            dve.wait_ge(max_row, b * U + u + 1)
                        dve.wait_ge(kept, b * U * NA + u * NA + (half + 1) * NA // 2 + 1)
                        ts = slice(half * KT // 2, (half + 1) * KT // 2)
                        nc.vector.tensor_reduce(mxh[:, half, :], st[:, u % 2, ts, :].rearrange("p t q -> p q t"), AX.X, ALU.max) \
                            .then_inc(half_max, 1)

                    def max_of_row(u):
                        n = b * U + u
                        dve.wait_ge(max_turned, n + 1)
                        nc.vector.tensor_reduce(nmax[:], MT[:].rearrange("p (f h k) -> p h f k", f=2, h=2), AX.XY, ALU.max,
                                                negate=True).then_inc(max_row, 1)
                        dve.wait_ge(max_row, n + 2)
                        dve.wait_ge(max_spread, n + 1)
                        nc.vector.tensor_tensor(diag[:], k["ident"][:].unsqueeze(1).to_broadcast([P, 2, P]),
                                                nmax[:].unsqueeze(2).to_broadcast([P, 2, P]), ALU.mult).then_inc(diag_made, 1)

                    def subtract(u):
                        for g in dve_groups:
                            dve.wait_ge(nmB_ready, b * U + u + 2)
                            nc.vector.tensor_tensor(st[:, u % 2, g * GT:(g + 1) * GT, :], st[:, u % 2, g * GT:(g + 1) * GT, :],
                                                    nmB[:, u % 2, :].unsqueeze(1).to_broadcast([P, GT, PAIR]), ALU.add) \
                                .then_inc(sub_dve, 1)

                    def finish(u):
                        n = b * U + u
                        dve.wait_ge(o_turned, n + 2)
                        out = OT[:, 0:2 * ODD].rearrange("p (h d) -> p h d", h=2)
                        nc.vector.reciprocal(rden[:, u % 2, :], OT[:, HD:ODD + VW:ODD]).then_inc(rden_done, 1)
                        dve.wait_ge(rden_done, n + 2)
                        nc.vector.tensor_tensor(attn[:, bass.ds(b, 1), 2 * u * HD:(2 * u + 2) * HD]
                                                .rearrange("p o (h d) -> p (o h) d", h=2),
                                                out[:, :, 0:HD], rden[:, u % 2, :].unsqueeze(2).to_broadcast([P, 2, HD]),
                                                ALU.mult).then_inc(o_done, 1)

                    if masked:
                        for j in range(NA):
                            keep(0, j)
                    reduce_half(0, 0)
                    reduce_half(0, 1)
                    for u in range(U + 1):
                        for g in range(NG):
                            if masked and u + 1 < U:
                                keep(u + 1, 2 * g)
                                keep(u + 1, 2 * g + 1)
                            if g == 0:
                                if u < U:
                                    max_of_row(u)
                                if u >= 2:
                                    finish(u - 2)
                            if g == 1 and u < U:
                                if u + 1 < U:
                                    reduce_half(u + 1, 0)
                                subtract(u)
                            if g == 3 and u + 1 < U:
                                reduce_half(u + 1, 1)
                    finish(U - 1)

            @block.scalar
            def _(act):
                prime(act, v_done, nmB_ready, o_kept)
                if not masked:
                    prime(act, kept)
                act.wait_ge(bk_in, 16)
                act.wait_ge(cleared, 4)
                with act.Fori(0, NB) as b:
                    for ch in range(NKC):
                        act.wait_ge(raw_in, 16 * (b * NKC + ch) + 16)
                        if ch >= 2:
                            act.wait_ge(k_made, b * KG + (ch - 1) * C)
                        else:
                            act.wait_ge(v_done, b * VG + 1)
                        nc.scalar.copy(chi[:, ch % 2], raw[:]).then_inc(chi_ready, 1)
                        for i in range(C + KC // P):
                            if i % 3 == 2:
                                t = i // 3
                                act.wait_ge(v_made, b * VG + ch * 2 + t + 1)
                                nc.scalar.copy(v[:, ch * 2 + t, :, 0:HD], VB[t][:].rearrange("p (h d) -> p h d", h=HEADS)) \
                                    .then_inc(v_done, 1)
                            else:
                                o = i - i // 3
                                act.wait_ge(k_made, b * KG + ch * C + o + 1)
                                nc.scalar.activation(khi[:, o, ch * KC:(ch + 1) * KC], KB[o % 2][:, 0:KC], ACT.Identity,
                                                     bias=bkcol[:, o:o + 1]).then_inc(khi_done, 1)

                    def keep(u, j):
                        n = u * NA + j
                        act.wait_ge(scored, b * U * NA + n + 2)
                        done = (u - 2) * NG + j // 2 + 1 if u >= 2 else 0
                        act.wait_ge(pv_done, b * U * NG + done + 1)
                        nc.scalar.copy(st[:, u % 2, j * AG:(j + 1) * AG, :].rearrange("p t q -> p (t q)"), A[n % 3][:]) \
                            .then_inc(kept, 1)

                    def keep_max(u):
                        act.wait_ge(max_spread, b * U + u + 2)
                        nc.scalar.copy(nmB[:, u % 2, :], MB[:, 0:PAIR]).then_inc(nmB_ready, 1)

                    def exponent(u, g):
                        n = b * U + u
                        if g in pool_groups:
                            act.wait_ge(sub_pool, n * len(pool_groups) + pool_groups.index(g) + 2)
                        else:
                            act.wait_ge(sub_dve, n * len(dve_groups) + dve_groups.index(g) + 2)
                        part = st[:, u % 2, g * GT:(g + 1) * GT, :].rearrange("p t q -> p (t q)")
                        nc.scalar.activation(part, part, ACT.Exp).then_inc(exp_done, 1)

                    def keep_output(u):
                        act.wait_ge(pv_done, NG * (b * U + u) + NG + 1)
                        act.wait_ge(o_turned, b * U + max(u - 1, 0) + 1)
                        for i in range(2):
                            ins = nc.scalar.copy(oT[i * ODD:i * ODD + VW, u % 2, :], O[u % 2][i * ODD:i * ODD + VW, 0:P])
                        ins.then_inc(o_kept, 1)

                    if not masked:
                        for j in range(NA):
                            keep(0, j)
                    for u in range(U + 1):
                        for g in range(NG):
                            if u >= 1:
                                exponent(u - 1, g)
                            if not masked and u + 1 < U:
                                keep(u + 1, 2 * g)
                                keep(u + 1, 2 * g + 1)
                            if g == 1 and u < U:
                                keep_max(u)
                        if u >= 1:
                            keep_output(u - 1)


def stage_attention_output(nc, k, name, a, bv, wo, bo, gamma, beta, x_in, x_out):
    with ExitStack() as ctx:
        m = Mem(nc, ctx, name)
        ab = m.sb("ab", [P, NB, D])
        x = m.sb("x", [P, NB, D])
        y = m.sb("y", [P, NB, D])
        y2 = m.sb("y2", [P, NB, D])
        aT = m.sb("aT", [P, C, TOK])
        woT = m.sb("woT", [P, C, D])
        rows = m.sb("rows", [P, 4, D])
        stats, mv = m.sb("stats", [P, NB, 6]), m.sb("mv", [P, NB, 2])
        ve, std, rstd = m.sb("ve", [P, NB]), m.sb("std", [P, NB]), m.sb("rstd", [P, NB])
        w_in, x_sem, r_in = m.sem("w_in"), m.sem("x_in"), m.sem("r_in")
        dstep, ab_ready, turned, aT_ready, made = (m.sem(s) for s in ("dstep", "ab", "turned", "aT", "made"))
        var_ready, std_ready, done, stored = (m.sem(s) for s in ("var", "std", "done", "stored"))
        ps = k["ps"]
        row_list = [bv, bo] + ([gamma, beta] if gamma is not None else [])
        with nc.Block() as block:
            @block.sync
            def _(sp):
                for i, r in enumerate(row_list):
                    sp.dma_start(rows[:, i, :], r.partition_broadcast(P)).then_inc(r_in, 16)
                sp.dma_start(woT[:], wo).then_inc(w_in, 16)
                sp.dma_start(x[:], x_in.rearrange("b p d -> p b d")).then_inc(x_sem, 16)
                sp.wait_ge(done, NB)
                sp.dma_start(x_out.rearrange("b p d -> p b d"), x[:]).then_inc(stored, 16)
                sp.wait_ge(stored, 16)

            @block.tensor
            def _(pe):
                pe.wait_ge(ab_ready, NB)
                for c in range(C):
                    if c >= 2:
                        pe.wait_ge(aT_ready, c - 1)
                    for b in range(NB):
                        last = pe.transpose(ps[c % 2][:, b * P:(b + 1) * P], ab[:, b, c * P:(c + 1) * P], k["ident"][:])
                    last.then_inc(turned, 1)
                pe.wait_ge(aT_ready, C)
                pe.wait_ge(w_in, 16)
                for b in range(NB):
                    for c in range(C):
                        last = pe.matmul(ps[2 + b][:], aT[:, c, b * P:(b + 1) * P], woT[:, c, :],
                                         start=(c == 0), stop=(c == C - 1))
                    last.then_inc(made, 1)

            @block.scalar
            def _(act):
                for c in range(C):
                    act.wait_ge(turned, c + 1)
                    nc.scalar.copy(aT[:, c, :], ps[c % 2][:]).then_inc(aT_ready, 1)
                if gamma is not None:
                    act.wait_ge(var_ready, 1)
                    nc.scalar.sqrt(std[:], ve[:]).then_inc(std_ready, 1)

            @block.vector
            def _(dve):
                s = Steps(dve, dstep)
                dve.wait_ge(r_in, 16 * len(row_list))
                for b in range(NB):
                    nc.vector.tensor_tensor(ab[:, b, :], a[:, b, :], rows[:, 0, :], ALU.add).then_inc(ab_ready, 1)
                dve.wait_ge(x_sem, 16)
                for b in range(NB):
                    dve.wait_ge(made, b + 1)
                    s.mark(nc.vector.tensor_tensor(y[:, b, :], ps[2 + b][:], rows[:, 1, :], ALU.add))
                s.wait()
                last_y = y
                if gamma is not None:
                    for b in range(NB):
                        s.mark(nc.vector.bn_stats(stats[:, b, :], y[:, b, :]))
                    s.wait()
                    for b in range(NB):
                        s.mark(nc.vector.bn_aggr(mv[:, b, :], stats[:, b, :]))
                    s.wait()
                    nc.vector.tensor_scalar_add(ve[:], mv[:, :, 1], LN_EPS).then_inc(var_ready, 1)
                    dve.wait_ge(std_ready, 1)
                    s.then(nc.vector.reciprocal(rstd[:], std[:]))
                    for b in range(NB):
                        s.mark(nc.vector.tensor_scalar(y2[:, b, :], y[:, b, :], mv[:, b, 0:1], rstd[:, b:b + 1],
                                                       ALU.subtract, ALU.mult))
                    s.wait()
                    for b in range(NB):
                        s.mark(nc.vector.tensor_tensor(y[:, b, :], y2[:, b, :], rows[:, 2, :], ALU.mult))
                    s.wait()
                    for b in range(NB):
                        s.mark(nc.vector.tensor_tensor(y2[:, b, :], y[:, b, :], rows[:, 3, :], ALU.add))
                    s.wait()
                    last_y = y2
                for b in range(NB):
                    nc.vector.tensor_tensor(x[:, b, :], x[:, b, :], last_y[:, b, :], ALU.add).then_inc(done, 1)


def stage_retention(nc, k, t, x_in, x_out):
    QD, KD = QH * RD, KVH * RD
    WIDE = QD + 2 * KD + KVH
    ROT = QH + KVH
    with ExitStack() as ctx:
        m = Mem(nc, ctx, "ret")
        w = m.sb("w", [P, C, WIDE])
        wp = m.sb("wp", [P, 2 * C, D])
        rot = m.sb("rot", [P, 2, RD])
        lnw = m.sb("lnw", [P, RD])
        causal = m.sb("causal", [P, P])
        upto = m.sb("upto", [P, P])
        after = m.sb("after", [P, P])
        x, xn = m.sb("x", [P, D]), m.sb("xn", [P, D])
        xT = m.sb("xT", [P, C, P])
        qk = m.sb("qk", [P, ROT, RD])
        qkr = m.sb("qkr", [P, ROT, RD])
        qks = m.sb("qks", [P, ROT, RD])
        qr = m.sb("qr", [P, QH, RD])
        kr = m.sb("kr", [P, KVH, 2, RD])
        vx = m.sb("vx", [P, KVH, RD + 1])
        gate = m.sb("gate", [P, 6, KVH])
        cut = m.sb("cut", [P, KVH, P])
        decay = m.sb("decay", [P, KVH, P])
        qT, kT = m.sb("qT", [P, KVH, P]), m.sb("kT", [P, KVH, P])
        s_abs, u = m.sb("s_abs", [P, QH, P]), m.sb("u", [P, QH, P])
        um, ru = m.sb("um", [P, QH]), m.sb("ru", [P, QH])
        aT = m.sb("aT", [P, QH, P])
        y, yc, y2 = m.sb("y", [P, QH, RD]), m.sb("yc", [P, QH, RD]), m.sb("y2", [P, QH, RD])
        col = m.sb("col", [P, 6, QH])
        yT = m.sb("yT", [P, 2 * C, P])
        res = m.sb("res", [P, D])
        stats, mv, rs = m.sb("stats", [P, 6]), m.sb("mv", [P, 2]), m.sb("rs", [P, 3])
        pad = m.sb("pad", [P, 1])
        S = {}
        for n in ("const_in", "filled", "x_sem", "dstep", "astep", "pstep", "var", "std", "xn", "xturned", "xT", "proj", "proj_read",
                  "gate_in", "e_gate", "gate_1", "l_gate", "cut", "decay_made", "decay_exp", "rotated", "qk_turned", "qk_copied",
                  "scores", "abs", "r_ready", "squared", "a_turned", "a_copied", "num", "y_sum", "yvar", "ystd", "y_ready",
                  "y_turned", "y_copied", "out_made", "res", "stored"):
            S[n] = m.sem(n)
        ps, ps2 = k["ps"], k["ps2"]
        NPJ = WIDE // D + 1
        with nc.Block() as block:
            @block.sync
            def _(sp):
                sp.dma_start(rot[:], t["rotary"]).then_inc(S["const_in"], 16)
                sp.dma_start(lnw[:], t["L0_attn_ln_w"].partition_broadcast(P)).then_inc(S["const_in"], 16)
                sp.dma_start(w[:], t["L0_attn_w_attn"]).then_inc(S["const_in"], 16)
                sp.dma_start(wp[:], t["L0_attn_w_proj"]).then_inc(S["const_in"], 16)
                with sp.Fori(0, NB) as b:
                    sp.wait_ge(S["res"], b)
                    sp.dma_start(x[:], x_in[bass.ds(b, 1)].rearrange("o p d -> (o p) d")).then_inc(S["x_sem"], 16)
                    sp.wait_ge(S["res"], b + 1)
                    sp.dma_start(x_out[bass.ds(b, 1)].rearrange("o p d -> (o p) d"), res[:]).then_inc(S["stored"], 16)
                sp.wait_ge(S["stored"], 16 * NB)

            @block.gpsimd
            def _(pool):
                nc.gpsimd.memset(vx[:, :, RD:RD + 1], 1.0).then_inc(S["filled"], 1)
                nc.gpsimd.affine_select(out=causal[:], in_=k["ones"][:], compare_op=ALU.is_ge, fill=0.0, base=0,
                                        pattern=[[-1, P]], channel_multiplier=1).then_inc(S["filled"], 1)
                nc.gpsimd.affine_select(out=upto[:], in_=k["ones"][:], compare_op=ALU.is_ge, fill=0.0, base=0,
                                        pattern=[[1, P]], channel_multiplier=-1).then_inc(S["filled"], 1)
                nc.gpsimd.affine_select(out=after[:], in_=k["ones"][:], compare_op=ALU.is_gt, fill=0.0, base=0,
                                        pattern=[[-1, P]], channel_multiplier=1).then_inc(S["filled"], 1)

            @block.tensor
            def _(pe):
                pe.wait_ge(S["filled"], 4)
                pe.wait_ge(S["const_in"], 64)
                with pe.Fori(0, NB) as b:
                    pe.wait_ge(S["xn"], b + 1)
                    pe.wait_ge(S["out_made"], b)
                    for c in range(C):
                        last = pe.transpose(ps[4][:, c * P:(c + 1) * P], xn[:, c * P:(c + 1) * P], k["ident"][:])
                    last.then_inc(S["xturned"], 1)
                    pe.wait_ge(S["xT"], b + 1)
                    for g in range(NPJ):
                        n = min(D, WIDE - g * D)
                        if g >= 2:
                            pe.wait_ge(S["proj_read"], b * NPJ + g - 1)
                        for c in range(C):
                            last = pe.matmul(ps[5 + g % 2][:, 0:n], xT[:, c, :], w[:, c, g * D:g * D + n],
                                             start=(c == 0), stop=(c == C - 1))
                        last.then_inc(S["proj"], 1)
                    pe.wait_ge(S["cut"], b + 1)
                    for i in range(2):
                        last = pe.matmul(ps2[0][:, i * D:(i + 1) * D], upto[:],
                                         cut[:, i * 4:(i + 1) * 4, :].rearrange("p h s -> p (h s)"), start=True, stop=True)
                    last.then_inc(S["decay_made"], 1)
                    for i in range(4):
                        src = qr if i < 2 else kr
                        flat = src[:].rearrange("p h d -> p (h d)") if i < 2 else src[:].rearrange("p h r d -> p (h r d)")
                        if i == 0:
                            pe.wait_ge(S["rotated"], 2 * b + 1)
                        if i == 2:
                            pe.wait_ge(S["rotated"], 2 * b + 2)
                        if i >= 2:
                            pe.wait_ge(S["qk_copied"], 4 * b + i - 1)
                        for j in range(4):
                            at = ((i % 2) * 4 + j) * P
                            last = pe.transpose(ps[6 + i % 2][:, j * P:(j + 1) * P], flat[:, at:at + P], k["ident"][:])
                        last.then_inc(S["qk_turned"], 1)
                    pe.wait_ge(S["qk_copied"], 4 * b + 4)
                    pe.wait_ge(S["decay_exp"], b + 1)
                    for r in range(2):
                        for h in range(KVH):
                            last = pe.matmul(ps2[r][:, h * P:(h + 1) * P], qT[r * RD:(r + 1) * RD, h, :],
                                             kT[r * RD:(r + 1) * RD, h, :], start=True, stop=True)
                        last.then_inc(S["scores"], 1)
                    pe.wait_ge(S["squared"], b + 1)
                    for i in range(4):
                        if i >= 2:
                            pe.wait_ge(S["a_copied"], 4 * b + i - 1)
                        for j in range(4):
                            last = pe.transpose(ps[4 + i % 2][:, j * P:(j + 1) * P], s_abs[:, i * 4 + j, :], k["ident"][:])
                        last.then_inc(S["a_turned"], 1)
                    pe.wait_ge(S["a_copied"], 4 * b + 4)
                    for h in range(QH):
                        last = pe.matmul(ps[h // 4][:, (h % 4) * (RD + 1):(h % 4 + 1) * (RD + 1)], aT[:, h, :],
                                         vx[:, h // 2, :], start=True, stop=True)
                    last.then_inc(S["num"], 1)
                    pe.wait_ge(S["y_ready"], b + 1)
                    flat = y2[:].rearrange("p h d -> p (h d)")
                    for i in range(2):
                        for j in range(4):
                            last = pe.transpose(ps[4 + i][:, j * P:(j + 1) * P], flat[:, (i * 4 + j) * P:(i * 4 + j + 1) * P], k["ident"][:])
                        last.then_inc(S["y_turned"], 1)
                    pe.wait_ge(S["y_copied"], 2 * b + 2)
                    for c in range(2 * C):
                        last = pe.matmul(ps[6][:], yT[:, c, :], wp[:, c, :], start=(c == 0), stop=(c == 2 * C - 1))
                    last.then_inc(S["out_made"], 1)

            @block.scalar
            def _(act):
                with act.Fori(0, NB) as b:
                    act.wait_ge(S["var"], b + 1)
                    nc.scalar.sqrt(rs[:, 1:2], rs[:, 0:1]).then_inc(S["std"], 1)
                    act.wait_ge(S["xturned"], b + 1)
                    nc.scalar.copy(xT[:].rearrange("p c t -> p (c t)"), ps[4][:]).then_inc(S["xT"], 1)
                    for g in range(NPJ):
                        act.wait_ge(S["proj"], b * NPJ + g + 1)
                        src = ps[5 + g % 2]
                        if g < 3:
                            ins = nc.scalar.copy(qk[:, g * 8:(g + 1) * 8, :], src[:].rearrange("p (h d) -> p h d", d=RD))
                        elif g == 3:
                            ins = nc.scalar.copy(vx[:, :, 0:RD], src[:].rearrange("p (h d) -> p h d", d=RD))
                        else:
                            ins = nc.scalar.copy(gate[:, 0, :], src[:, 0:KVH])
                        ins.then_inc(S["proj_read"], 1)
                    act.wait_ge(S["gate_in"], b + 1)
                    nc.scalar.activation(gate[:, 2, :], gate[:, 1, :], ACT.Exp, scale=-1.0).then_inc(S["e_gate"], 1)
                    act.wait_ge(S["gate_1"], b + 1)
                    nc.scalar.activation(gate[:, 4, :], gate[:, 3, :], ACT.Ln).then_inc(S["l_gate"], 1)
                    act.wait_ge(S["decay_made"], b + 1)
                    nc.scalar.activation(decay[:].rearrange("p h s -> p (h s)"), ps2[0][:], ACT.Exp, scale=0.5) \
                        .then_inc(S["decay_exp"], 1)
                    for i in range(4):
                        act.wait_ge(S["qk_turned"], 4 * b + i + 1)
                        dst = (qT if i < 2 else kT)[:, (i % 2) * 4:(i % 2 + 1) * 4, :].rearrange("p h t -> p (h t)")
                        nc.scalar.copy(dst, ps[6 + i % 2][:]).then_inc(S["qk_copied"], 1)
                    for r in range(2):
                        act.wait_ge(S["scores"], 2 * b + r + 1)
                        nc.scalar.activation(s_abs[:, r:QH:2, :], ps2[r][:].rearrange("p (h s) -> p h s", s=P), ACT.Abs,
                                             scale=float(RD) ** -0.5).then_inc(S["abs"], 1)
                    act.wait_ge(S["r_ready"], b + 1)
                    nc.scalar.square(s_abs[:], u[:]).then_inc(S["squared"], 1)
                    for i in range(4):
                        act.wait_ge(S["a_turned"], 4 * b + i + 1)
                        nc.scalar.copy(aT[:, i * 4:(i + 1) * 4, :].rearrange("p h t -> p (h t)"), ps[4 + i % 2][:]) \
                            .then_inc(S["a_copied"], 1)
                    act.wait_ge(S["yvar"], b + 1)
                    nc.scalar.sqrt(col[:, 3, :], col[:, 2, :]).then_inc(S["ystd"], 1)
                    for i in range(2):
                        act.wait_ge(S["y_turned"], 2 * b + i + 1)
                        nc.scalar.copy(yT[:, i * 4:(i + 1) * 4, :].rearrange("p c t -> p (c t)"), ps[4 + i][:]) \
                            .then_inc(S["y_copied"], 1)

            @block.vector
            def _(dve):
                dve.wait_ge(S["filled"], 4)
                dve.wait_ge(S["const_in"], 64)
                with dve.Fori(0, NB) as b:
                    s = Steps(dve, S["dstep"], b, RET_STEPS)
                    dve.wait_ge(S["x_sem"], 16 * b + 16)
                    s.then(nc.vector.bn_stats(stats[:], x[:]))
                    nc.vector.memset(pad[:], 0.0)
                    s.then(nc.vector.bn_aggr(mv[:], stats[:]))
                    nc.vector.tensor_scalar_add(rs[:, 0:1], mv[:, 1:2], LN_EPS).then_inc(S["var"], 1)
                    dve.wait_ge(S["std"], b + 1)
                    s.then(nc.vector.reciprocal(rs[:, 2:3], rs[:, 1:2]))
                    nc.vector.tensor_scalar(xn[:], x[:], mv[:, 0:1], rs[:, 2:3], ALU.subtract, ALU.mult).then_inc(S["xn"], 1)
                    dve.wait_ge(S["proj_read"], b * NPJ + 3)
                    cos = rot[:, 0:1, :].to_broadcast([P, ROT, RD])
                    pairs = qk[:].rearrange("p h (i e) -> p h i e", e=2)
                    spairs = qks[:].rearrange("p h (i e) -> p h i e", e=2)
                    sinp = rot[:, 1, :].rearrange("p (i e) -> p i e", e=2)
                    s.mark(nc.vector.tensor_tensor(qkr[:], qk[:], cos, ALU.mult))
                    for e in range(2):
                        sin_e = sinp[:, :, e].unsqueeze(1).to_broadcast([P, ROT, RD // 2])
                        s.mark(nc.vector.tensor_tensor(spairs[:, :, :, e], pairs[:, :, :, 1 - e], sin_e, ALU.mult))
                    s.wait()
                    nc.vector.tensor_tensor(qr[:], qkr[:, 0:QH], qks[:, 0:QH], ALU.add).then_inc(S["rotated"], 1)
                    s.mark(nc.vector.tensor_tensor(kr[:, :, 0, :], qkr[:, QH:ROT], qks[:, QH:ROT], ALU.add))
                    nc.vector.tensor_tensor(kr[:, :, 1, :], qkr[:, QH:ROT], qks[:, QH:ROT], ALU.add).then_inc(S["rotated"], 1)
                    dve.wait_ge(S["proj_read"], b * NPJ + NPJ)
                    s.then(nc.vector.tensor_scalar_add(gate[:, 0, :], gate[:, 0, :], 6.906768))
                    nc.vector.scalar_tensor_tensor(out=gate[:, 1, :], in0=gate[:, 0, :], scalar=-1.0, in1=gate[:, 0, :],
                                                   op0=ALU.mult, op1=ALU.max).then_inc(S["gate_in"], 1)
                    dve.wait_ge(S["e_gate"], b + 1)
                    nc.vector.tensor_scalar_add(gate[:, 3, :], gate[:, 2, :], 1.0).then_inc(S["gate_1"], 1)
                    dve.wait_ge(S["l_gate"], b + 1)
                    s.then(nc.vector.scalar_tensor_tensor(out=gate[:, 5, :], in0=gate[:, 0, :], scalar=0.0, in1=gate[:, 4, :],
                                                          op0=ALU.min, op1=ALU.subtract))
                    nc.vector.tensor_tensor(cut[:], after[:].unsqueeze(1).to_broadcast([P, KVH, P]),
                                            gate[:, 5, :].unsqueeze(2).to_broadcast([P, KVH, P]), ALU.mult).then_inc(S["cut"], 1)
                    dve.wait_ge(S["decay_exp"], b + 1)
                    s.then(nc.vector.tensor_tensor(decay[:], decay[:], causal[:].unsqueeze(1).to_broadcast([P, KVH, P]), ALU.mult))
                    dve.wait_ge(S["abs"], 2 * b + 2)
                    for r in range(2):
                        s.mark(nc.vector.scalar_tensor_tensor(out=u[:, r:QH:2, :], in0=s_abs[:, r:QH:2, :], scalar=1e-30,
                                                              in1=decay[:], op0=ALU.add, op1=ALU.mult))
                    s.wait()
                    s.then(nc.vector.tensor_reduce(um[:], u[:], AX.X, ALU.max))
                    s.then(nc.vector.reciprocal(ru[:], um[:]))
                    nc.vector.tensor_tensor(u[:], u[:], ru[:].unsqueeze(2).to_broadcast([P, QH, P]), ALU.mult) \
                        .then_inc(S["r_ready"], 1)
                    dve.wait_ge(S["num"], b + 1)
                    for i in range(4):
                        at = ps[i][:, 0:4 * (RD + 1)].rearrange("p (h d) -> p h d", h=4)
                        s.then(nc.vector.tensor_scalar_add(col[:, 0, i * 4:(i + 1) * 4], at[:, :, RD], 1e-6))
                        s.then(nc.vector.reciprocal(col[:, 1, i * 4:(i + 1) * 4], col[:, 0, i * 4:(i + 1) * 4]))
                        s.mark(nc.vector.tensor_tensor(y[:, i * 4:(i + 1) * 4, :], at[:, :, 0:RD],
                                                       col[:, 1, i * 4:(i + 1) * 4].unsqueeze(2).to_broadcast([P, 4, RD]), ALU.mult))
                    s.wait()
                    s.then(nc.vector.reduce_sum(col[:, 4, :], y[:], AX.X))
                    s.then(nc.vector.tensor_scalar(col[:, 5, :], col[:, 4, :], 1.0 / RD, None, ALU.mult))
                    s.then(nc.vector.tensor_tensor(yc[:], y[:], col[:, 5, :].unsqueeze(2).to_broadcast([P, QH, RD]), ALU.subtract))
                    s.then(nc.vector.tensor_tensor(y[:], yc[:], yc[:], ALU.mult))
                    s.then(nc.vector.reduce_sum(col[:, 4, :], y[:], AX.X))
                    nc.vector.tensor_scalar(col[:, 2, :], col[:, 4, :], 1.0 / RD, 1e-9, ALU.mult, ALU.add).then_inc(S["yvar"], 1)
                    dve.wait_ge(S["ystd"], b + 1)
                    s.then(nc.vector.reciprocal(col[:, 5, :], col[:, 3, :]))
                    s.then(nc.vector.tensor_tensor(y[:], yc[:], col[:, 5, :].unsqueeze(2).to_broadcast([P, QH, RD]), ALU.mult))
                    nc.vector.tensor_tensor(y2[:], y[:], lnw[:].unsqueeze(1).to_broadcast([P, QH, RD]), ALU.mult) \
                        .then_inc(S["y_ready"], 1)
                    dve.wait_ge(S["out_made"], b + 1)
                    dve.wait_ge(S["stored"], 16 * b)
                    nc.vector.tensor_tensor(res[:], x[:], ps[6][:], ALU.add).then_inc(S["res"], 1)
                    assert s.n == RET_STEPS, s.n


RET_STEPS = 33


def stage_experts(nc, k, name, t, x_in, x_out, layer):
    HT = HID // P if layer == 0 else C
    GR = HT // C
    with ExitStack() as ctx:
        m = Mem(nc, ctx, name)
        x = m.sb("x", [P, NB, D])
        xhi, xlo = m.sb("xhi", [P, C, TOK], F32R), m.sb("xlo", [P, C, TOK], F32R)
        weT = m.sb("weT", [NE, TOK])
        weB = m.sb("weB", [P, NE, TOK])
        b2 = m.sb("b2", [NE, D])
        b1 = m.sb("b1", [P, NE * HT]) if layer == 0 else None
        prep_done = {n: m.sem(n) for n in ("x_in", "b_in", "xlo_ready", "weB_ready")}
        ps = k["ps"]
        Y = ps[0:4]
        with ExitStack() as prep:
            p = Mem(nc, prep, name + "p")
            xn = p.sb("xn", [P, NB, D])
            xT = p.sb("xT", [P, C, TOK])
            stats, mv = p.sb("stats", [P, NB, 6]), p.sb("mv", [P, NB, 2])
            ve, std, rstd = p.sb("ve", [P, NB]), p.sb("std", [P, NB]), p.sb("rstd", [P, NB])
            if layer == 0:
                rw1, rw2 = p.sb("rw1", [P, C, HID]), p.sb("rw2", [P, HT, NE])
                rb1, hr = p.sb("rb1", [P, HT]), p.sb("hr", [P, HT, TOK])
            else:
                rw2 = p.sb("rw2", [P, C, NE])
            rb2 = p.sb("rb2", [1, NE])
            logit = p.sb("logit", [P, NB, NE])
            best, bidx, bidf = p.sb("best", [P, NB, 8]), p.sb("bidx", [P, NB, 8], U32), p.sb("bidf", [P, NB, 8])
            gap, e2, e1 = p.sb("gap", [P, NB]), p.sb("e2", [P, NB]), p.sb("e1", [P, NB])
            prob = p.sb("prob", [P, NB, 2])
            number = p.sb("number", [P, NE])
            we, we2 = p.sb("we", [P, NB, NE]), p.sb("we2", [P, NB, NE])
            sel = p.sb("sel", [NE, NE, P])
            s_ = {n: p.sem(n) for n in ("w_in", "dstep", "var", "std", "xn", "turned", "xT", "xhi", "h_made", "h_read", "logits",
                                        "gap", "e2", "we", "we_turned", "weT", "weB_made", "filled", "selected")}
            with nc.Block() as block:
                @block.sync
                def _(sp):
                    sp.dma_start(x[:], x_in.rearrange("b p d -> p b d")).then_inc(prep_done["x_in"], 16)
                    if layer == 0:
                        sp.dma_start(rb1[:], t["L0_ffn_rb1"]).then_inc(s_["w_in"], 16)
                        sp.dma_start(rw1[:], t["L0_ffn_rw1"]).then_inc(s_["w_in"], 16)
                        sp.dma_start(rw2[:], t["L0_ffn_rw2"]).then_inc(s_["w_in"], 16)
                        sp.dma_start(rb2[:], t["L0_ffn_rb2"].rearrange("(o e) -> o e", o=1)).then_inc(s_["w_in"], 16)
                        sp.dma_start(b1[:], t["L0_ffn_b1"]).then_inc(prep_done["b_in"], 16)
                        sp.dma_start(b2[:], t["L0_ffn_b2"]).then_inc(prep_done["b_in"], 16)
                    else:
                        sp.dma_start(rw2[:], t["L1_ffn_router_w"]).then_inc(s_["w_in"], 16)
                        sp.dma_start(rb2[:], t["L1_ffn_router_b"].rearrange("(o e) -> o e", o=1)).then_inc(s_["w_in"], 16)

                @block.gpsimd
                def _(pool):
                    nc.gpsimd.memset(sel[:], 1.0).then_inc(s_["filled"], 1)
                    nc.gpsimd.iota(number[:], pattern=[[1, NE]], base=0, channel_multiplier=0,
                                   allow_small_or_imprecise_dtypes=True).then_inc(s_["filled"], 1)
                    pool.wait_ge(s_["filled"], 2)
                    nc.gpsimd.affine_select(out=sel[:], in_=sel[:], compare_op=ALU.is_equal, fill=0.0, base=0,
                                            pattern=[[-1, NE], [0, P]], channel_multiplier=1).then_inc(s_["selected"], 1)
                    if layer == 1:
                        nc.gpsimd.memset(b2[:], 0.0).then_inc(prep_done["b_in"], 16)

                @block.tensor
                def _(pe):
                    for c in range(C):
                        pe.wait_ge(s_["xn"], NB)
                        if c >= 2:
                            pe.wait_ge(s_["xT"], c - 1)
                        for b in range(NB):
                            last = pe.transpose(ps[4 + c % 2][:, b * P:(b + 1) * P], xn[:, b, c * P:(c + 1) * P], k["ident"][:])
                        last.then_inc(s_["turned"], 1)
                    pe.wait_ge(s_["xT"], C)
                    pe.wait_ge(s_["w_in"], 64 if layer == 0 else 32)
                    if layer == 0:
                        for j in range(HT):
                            if j >= 2:
                                pe.wait_ge(s_["h_read"], j - 1)
                            for c in range(C):
                                last = pe.matmul(ps[4 + j % 2][:], rw1[:, c, j * P:(j + 1) * P], xT[:, c, :],
                                                 start=(c == 0), stop=(c == C - 1))
                            last.then_inc(s_["h_made"], 1)
                        pe.wait_ge(s_["h_read"], HT)
                    rows, n = (hr, HT) if layer == 0 else (xT, C)
                    for b in range(NB):
                        pe.matmul(ps[6][:, b * NE:(b + 1) * NE], k["ones"][0:1, :], rb2[:], start=True, stop=False)
                        for j in range(n):
                            last = pe.matmul(ps[6][:, b * NE:(b + 1) * NE], rows[:, j, b * P:(b + 1) * P], rw2[:, j, :],
                                             start=False, stop=(j == n - 1))
                    last.then_inc(s_["logits"], 1)
                    pe.wait_ge(s_["we"], NB)
                    for b in range(NB):
                        last = pe.transpose(ps[7][0:NE, b * P:(b + 1) * P], we[:, b, :], k["ident"][:])
                    last.then_inc(s_["we_turned"], 1)
                    pe.wait_ge(s_["weT"], 1)
                    pe.wait_ge(s_["selected"], 1)
                    for e in range(NE):
                        if e >= 2:
                            pe.wait_ge(prep_done["weB_ready"], e - 1)
                        pe.matmul(ps[4 + e % 2][:], sel[:, e, :], weT[:], start=True, stop=True).then_inc(s_["weB_made"], 1)

                @block.scalar
                def _(act):
                    act.wait_ge(s_["var"], 1)
                    nc.scalar.sqrt(std[:], ve[:]).then_inc(s_["std"], 1)
                    for c in range(C):
                        act.wait_ge(s_["xT"], c + 1)
                        nc.scalar.copy(xhi[:, c, :], xT[:, c, :]).then_inc(s_["xhi"], 1)
                    if layer == 0:
                        act.wait_ge(s_["w_in"], 64)
                        for j in range(HT):
                            act.wait_ge(s_["h_made"], j + 1)
                            nc.scalar.activation(hr[:, j, :], ps[4 + j % 2][:], ACT.Silu, bias=rb1[:, j:j + 1]) \
                                .then_inc(s_["h_read"], 1)
                    act.wait_ge(s_["gap"], 1)
                    nc.scalar.activation(e2[:], gap[:], ACT.Exp).then_inc(s_["e2"], 1)
                    for e in range(NE):
                        act.wait_ge(s_["weB_made"], e + 1)
                        nc.scalar.copy(weB[:, e, :], ps[4 + e % 2][:]).then_inc(prep_done["weB_ready"], 1)

                @block.vector
                def _(dve):
                    s = Steps(dve, s_["dstep"])
                    dve.wait_ge(prep_done["x_in"], 16)
                    for b in range(NB):
                        s.mark(nc.vector.bn_stats(stats[:, b, :], x[:, b, :]))
                    s.wait()
                    for b in range(NB):
                        s.mark(nc.vector.bn_aggr(mv[:, b, :], stats[:, b, :]))
                    s.wait()
                    nc.vector.tensor_scalar_add(ve[:], mv[:, :, 1], LN_EPS).then_inc(s_["var"], 1)
                    dve.wait_ge(s_["std"], 1)
                    s.then(nc.vector.reciprocal(rstd[:], std[:]))
                    for b in range(NB):
                        nc.vector.tensor_scalar(xn[:, b, :], x[:, b, :], mv[:, b, 0:1], rstd[:, b:b + 1],
                                                ALU.subtract, ALU.mult).then_inc(s_["xn"], 1)
                    for c in range(C):
                        dve.wait_ge(s_["turned"], c + 1)
                        nc.vector.tensor_copy(xT[:, c, :], ps[4 + c % 2][:]).then_inc(s_["xT"], 1)
                    for c in range(C):
                        dve.wait_ge(s_["xhi"], c + 1)
                        nc.vector.tensor_tensor(xlo[:, c, :], xT[:, c, :], f32(xhi[:, c, :]), ALU.subtract) \
                            .then_inc(prep_done["xlo_ready"], 1)
                    dve.wait_ge(s_["logits"], 1)
                    s.then(nc.vector.tensor_copy(logit[:].rearrange("p b e -> p (b e)"), ps[6][:, 0:NB * NE]))
                    for b in range(NB):
                        s.mark(nc.vector.max(best[:, b, :], logit[:, b, :]))
                    s.wait()
                    for b in range(NB):
                        s.mark(nc.vector.max_index(bidx[:, b, :], best[:, b, :], logit[:, b, :]))
                    s.wait()
                    s.mark(nc.vector.tensor_copy(bidf[:], bidx[:]))
                    nc.vector.tensor_tensor(gap[:], best[:, :, 1], best[:, :, 0], ALU.subtract).then_inc(s_["gap"], 1)
                    dve.wait_ge(s_["e2"], 1)
                    s.then(nc.vector.tensor_scalar_add(e1[:], e2[:], 1.0))
                    s.then(nc.vector.reciprocal(prob[:, :, 0], e1[:]))
                    s.then(nc.vector.tensor_tensor(prob[:, :, 1], e2[:], prob[:, :, 0], ALU.mult))
                    dve.wait_ge(s_["filled"], 2)
                    for b in range(NB):
                        s.mark(nc.vector.tensor_scalar(we2[:, b, :], number[:], bidf[:, b, 1:2], prob[:, b, 1:2], ALU.is_equal, ALU.mult))
                        s.mark(nc.vector.tensor_scalar(we[:, b, :], number[:], bidf[:, b, 0:1], prob[:, b, 0:1], ALU.is_equal, ALU.mult))
                    s.wait()
                    for b in range(NB):
                        nc.vector.tensor_tensor(we[:, b, :], we[:, b, :], we2[:, b, :], ALU.add).then_inc(s_["we"], 1)
                    dve.wait_ge(s_["we_turned"], 1)
                    nc.vector.tensor_copy(weT[:], ps[7][0:NE, :]).then_inc(s_["weT"], 1)
        NW = 2 if layer == 0 else 3
        wraw = [m.sb(f"wraw{i}", [P, C * D]) for i in range(NW)]
        whi = [m.sb(f"whi{i}", [P, 2, C * D], F32R) for i in range(NW)]
        wlo = [m.sb(f"wlo{i}", [P, 2, C * D], F32R) for i in range(NW)]
        act_h, wh = m.sb("act_h", [P, 2, TOK]), m.sb("wh", [P, 2, TOK])
        hhi, hlo = m.sb("hhi", [P, 2, TOK], F32R), m.sb("hlo", [P, 2, TOK], F32R)
        names = ("L0_ffn_w1", "L0_ffn_w2") if layer == 0 else ("L1_ffn_we_gate", "L1_ffn_we_up", "L1_ffn_we_down")
        s_ = {n: m.sem("x" + n) for n in ("w_in", "whi", "wlo", "primed", "h_made", "h_read", "silu", "dstep", "wh", "hhi", "hlo",
                                          "y_tile", "y_made", "out", "stored")}
        up = 1 if layer == 1 else 0
        with nc.Block() as block:
            @block.sync
            def _(sp):
                with sp.Fori(0, NE) as e:
                    for g in range(GR):
                        if g:
                            sp.wait_ge(s_["wlo"], NW * (e * GR + g))
                        else:
                            sp.wait_ge(s_["wlo"], e * (NW * GR))
                        for i in range(NW):
                            sp.dma_start(wraw[i][:], t[names[i]][bass.ds(e * GR + g, 1)].rearrange("o p n -> (o p) n")) \
                                .then_inc(s_["w_in"], 16)
                sp.wait_ge(s_["out"], NB)
                sp.dma_start(x_out.rearrange("b p d -> p b d"), x[:]).then_inc(s_["stored"], 16)
                sp.wait_ge(s_["stored"], 16)

            PAR = 2 if GR > 1 else 1

            @block.gpsimd
            def _(pool):
                with pool.Fori(0, NE) as e:
                    for g in range(GR):
                        for i in range(NW):
                            pool.wait_ge(s_["whi"], e * (NW * GR) + NW * g + i + 1)
                            nc.gpsimd.tensor_tensor(wlo[i][:, g % PAR, :], wraw[i][:], f32(whi[i][:, g % PAR, :]), ALU.subtract) \
                                .then_inc(s_["wlo"], 1)

            @block.tensor
            def _(pe):
                pe.wait_ge(prep_done["b_in"], 32 if layer == 0 else 16)
                for b in range(NB):
                    pe.matmul(Y[b][:], weT[:, b * P:(b + 1) * P], b2[:], start=True, stop=False, skip_group_check=True)
                with pe.Fori(0, NE) as e:
                    def hidden(j):
                        g, r = j // C, j % C
                        if r == 0:
                            pe.wait_ge(s_["wlo"], e * (NW * GR) + NW * (g + 1))
                        pe.wait_ge(s_["h_read"] if up else s_["silu"], e * HT + max(j - 1, 0))
                        for i in range(1 + up):
                            bank = ps[4 + (j % 2) * (1 + up) + i]
                            for c in range(C):
                                at = c * D + r * P
                                last = three_products(pe, bank[:], whi[i][:, g % PAR, at:at + P], wlo[i][:, g % PAR, at:at + P],
                                                      xhi[:, c, :], xlo[:, c, :], c == 0, c == C - 1)
                        last.then_inc(s_["h_made"], 1)

                    def output(j):
                        g, r = j // C, j % C
                        pe.wait_ge(s_["hlo"], e * HT + j + 1)
                        for b in range(NB):
                            last = three_products(pe, Y[b][:], hhi[:, j % 2, b * P:(b + 1) * P], hlo[:, j % 2, b * P:(b + 1) * P],
                                                  whi[-1][:, g % PAR, r * D:(r + 1) * D], wlo[-1][:, g % PAR, r * D:(r + 1) * D],
                                                  False, j == HT - 1, check=False)
                        last.then_inc(s_["y_tile"], 1)

                    hidden(0)
                    for j in range(HT):
                        if j + 1 < HT:
                            hidden(j + 1)
                        output(j)

            @block.scalar
            def _(act):
                with act.Fori(0, NE) as e:
                    def split(g):
                        act.wait_ge(s_["w_in"], e * (16 * NW * GR) + 16 * NW * (g + 1))
                        act.wait_ge(s_["y_tile"], e * HT + max(0, g - PAR + 1) * C)
                        for i in range(NW):
                            nc.scalar.copy(whi[i][:, g % PAR, :], wraw[i][:]).then_inc(s_["whi"], 1)

                    split(0)
                    for j in range(HT):
                        if j % C == 1 and j // C + 1 < GR:
                            split(j // C + 1)
                        act.wait_ge(s_["h_made"], e * HT + j + 1)
                        if j >= 2:
                            act.wait_ge(s_["wh"], e * HT + j - 1)
                        else:
                            act.wait_ge(s_["wh"], e * HT)
                        bank = ps[4 + (j % 2) * (1 + up)]
                        if layer == 0:
                            nc.scalar.activation(act_h[:, j % 2, :], bank[:], ACT.Silu, bias=b1[:, bass.ds(e * HT + j, 1)]) \
                                .then_inc(s_["silu"], 1)
                        else:
                            nc.scalar.activation(act_h[:, j % 2, :], bank[:], ACT.Silu).then_inc(s_["silu"], 1)
                        act.wait_ge(s_["wh"], e * HT + j + 1)
                        if j >= 2:
                            act.wait_ge(s_["y_tile"], e * HT + j - 1)
                        else:
                            act.wait_ge(s_["y_tile"], e * HT)
                        nc.scalar.copy(hhi[:, j % 2, :], wh[:, j % 2, :]).then_inc(s_["hhi"], 1)

            @block.vector
            def _(dve):
                with dve.Fori(0, NE) as e:
                    for j in range(HT):
                        weight = weB[:, bass.ds(e, 1), :].rearrange("p o t -> p (o t)")
                        dve.wait_ge(s_["silu"], e * HT + j + 1)
                        bank = ps[4 + (j % 2) * (1 + up)]
                        if layer == 0:
                            nc.vector.tensor_tensor(wh[:, j % 2, :], act_h[:, j % 2, :], weight, ALU.mult).then_inc(s_["wh"], 1)
                        else:
                            nc.vector.tensor_tensor(act_h[:, j % 2, :], act_h[:, j % 2, :], ps[4 + (j % 2) * 2 + 1][:], ALU.mult) \
                                .then_inc(s_["h_read"], 1)
                            dve.wait_ge(s_["h_read"], e * HT + j + 1)
                            nc.vector.tensor_tensor(wh[:, j % 2, :], act_h[:, j % 2, :], weight, ALU.mult).then_inc(s_["wh"], 1)
                        dve.wait_ge(s_["hhi"], e * HT + j + 1)
                        nc.vector.tensor_tensor(hlo[:, j % 2, :], wh[:, j % 2, :], f32(hhi[:, j % 2, :]), ALU.subtract) \
                            .then_inc(s_["hlo"], 1)
                dve.wait_ge(s_["y_tile"], NE * HT)
                for b in range(NB):
                    nc.vector.tensor_tensor(x[:, b, :], x[:, b, :], Y[b][:], ALU.add).then_inc(s_["out"], 1)


def stage_rwkv(nc, k, t, x_in, x_out):
    with ExitStack() as ctx:
        m = Mem(nc, ctx, "rwkv")
        x, z, zn = m.sb("x", [P, NB, D]), m.sb("z", [P, NB, D]), m.sb("zn", [P, NB, D])
        zT = m.sb("zT", [P, C, NB, P])
        prev = m.sb("prev", [P, C, NB, P])
        mixed = [m.sb(f"mixed{i}", [P, C, NB, P]) for i in range(3)]
        w = [m.sb(f"w{i}", [P, C, D]) for i in range(4)]
        cols = m.sb("cols", [P, 6, C])
        one_minus = m.sb("one_minus", [P, 3, C])
        decay = m.sb("decay", [P, C])
        vT = m.sb("vT", [P, C, TOK])
        kv = m.sb("kv", [P, C, NB, P])
        state = m.sb("state", [P, C, NB, P])
        rate = m.sb("rate", [P, C, P])
        r = m.sb("r", [P, NB, D])
        stats, mv = m.sb("stats", [P, NB, 6]), m.sb("mv", [P, NB, 2])
        ve, std, rstd = m.sb("ve", [P, 2, NB]), m.sb("std", [P, 2, NB]), m.sb("rstd", [P, 2, NB])
        names = ("ln_w", "ln_b", "tmk", "tmv", "tmr", "decay_w")
        s_ = {n: m.sem(n) for n in ("x_in", "c_in", "w_in", "dstep", "var", "std", "zn", "turned", "zT", "decay", "mixed", "v_made",
                                    "vT", "k_made", "kv", "state", "r_made", "r", "o_made", "rate", "done", "stored")}
        ps = k["ps"]
        with nc.Block() as block:
            @block.sync
            def _(sp):
                sp.dma_start(x[:], x_in.rearrange("b p d -> p b d")).then_inc(s_["x_in"], 16)
                for i, n in enumerate(names):
                    sp.dma_start(cols[:, i, :], t["L1_attn_" + n]).then_inc(s_["c_in"], 16)
                for i, n in enumerate(("Wv", "Wk", "Wr", "Wo")):
                    sp.dma_start(w[i][:], t["L1_attn_" + n]).then_inc(s_["w_in"], 16)
                sp.wait_ge(s_["done"], NB)
                sp.dma_start(x_out.rearrange("b p d -> p b d"), x[:]).then_inc(s_["stored"], 16)
                sp.wait_ge(s_["stored"], 16)

            @block.tensor
            def _(pe):
                for c in range(C):
                    pe.wait_ge(s_["zn"], NB)
                    if c >= 2:
                        pe.wait_ge(s_["zT"], c - 1)
                    for b in range(NB):
                        last = pe.transpose(ps[c % 2][:, b * P:(b + 1) * P], zn[:, b, c * P:(c + 1) * P], k["ident"][:])
                    last.then_inc(s_["turned"], 1)
                pe.wait_ge(s_["w_in"], 64)
                flat = [x_[:].rearrange("p c b t -> p c (b t)") for x_ in mixed]
                pe.wait_ge(s_["zT"], C)
                for i, (src, made, banks) in enumerate(((1, "v_made", (2, 3, 4, 5)), (0, "k_made", (6, 7, 0, 1)))):
                    pe.wait_ge(s_["mixed"], C * (i + 1))
                    for o in range(C):
                        for c in range(C):
                            last = pe.matmul(ps[banks[o]][:], w[i][:, c, o * P:(o + 1) * P], flat[src][:, c, :],
                                             start=(c == 0), stop=(c == C - 1))
                        last.then_inc(s_[made], 1)
                pe.wait_ge(s_["vT"], C)
                pe.wait_ge(s_["mixed"], 3 * C)
                for b in range(NB):
                    for c in range(C):
                        last = pe.matmul(ps[2 + b][:], mixed[2][:, c, b, :], w[2][:, c, :], start=(c == 0), stop=(c == C - 1))
                    last.then_inc(s_["r_made"], 1)
                pe.wait_ge(s_["state"], C * NB)
                for b in range(NB):
                    for c in range(C):
                        last = pe.matmul(ps[(6 + b) % 8][:], state[:, c, b, :], w[3][:, c, :], start=(c == 0), stop=(c == C - 1))
                    last.then_inc(s_["o_made"], 1)

            @block.scalar
            def _(act):
                for i in range(2):
                    act.wait_ge(s_["var"], i + 1)
                    nc.scalar.sqrt(std[:, i, :], ve[:, i, :]).then_inc(s_["std"], 1)
                act.wait_ge(s_["c_in"], 16 * len(names))
                nc.scalar.activation(decay[:], cols[:, 5, :], ACT.Sigmoid).then_inc(s_["decay"], 1)
                for o in range(C):
                    act.wait_ge(s_["v_made"], o + 1)
                    nc.scalar.copy(vT[:, o, :], ps[2 + o][:]).then_inc(s_["vT"], 1)
                for b in range(NB):
                    act.wait_ge(s_["r_made"], b + 1)
                    nc.scalar.activation(r[:, b, :], ps[2 + b][:], ACT.Sigmoid).then_inc(s_["r"], 1)

            @block.gpsimd
            def _(pool):
                nc.gpsimd.memset(prev[:, :, :, 0:1], 0.0).then_inc(s_["rate"], 1)
                pool.wait_ge(s_["decay"], 1)
                nc.gpsimd.tensor_copy(rate[:], decay[:].unsqueeze(2).to_broadcast([P, C, P])).then_inc(s_["rate"], 1)

            @block.vector
            def _(dve):
                s = Steps(dve, s_["dstep"])
                dve.wait_ge(s_["x_in"], 16)
                for i, (src, dst) in enumerate(((x, z), (z, zn))):
                    for b in range(NB):
                        s.mark(nc.vector.bn_stats(stats[:, b, :], src[:, b, :]))
                    s.wait()
                    for b in range(NB):
                        s.mark(nc.vector.bn_aggr(mv[:, b, :], stats[:, b, :]))
                    s.wait()
                    nc.vector.tensor_scalar_add(ve[:, i, :], mv[:, :, 1], LN_EPS).then_inc(s_["var"], 1)
                    dve.wait_ge(s_["std"], i + 1)
                    s.then(nc.vector.reciprocal(rstd[:, i, :], std[:, i, :]))
                    for b in range(NB):
                        ins = nc.vector.tensor_scalar(dst[:, b, :], src[:, b, :], mv[:, b, 0:1], rstd[:, i, b:b + 1],
                                                      ALU.subtract, ALU.mult)
                        if i:
                            ins.then_inc(s_["zn"], 1)
                        else:
                            s.mark(ins)
                    if not i:
                        s.wait()
                dve.wait_ge(s_["c_in"], 16 * len(names))
                s.mark(nc.vector.tensor_scalar(one_minus[:], cols[:, 2:5, :], -1.0, 1.0, ALU.mult, ALU.add))
                for c in range(C):
                    dve.wait_ge(s_["turned"], c + 1)
                    nc.vector.tensor_scalar(zT[:, c].rearrange("p b t -> p (b t)"), ps[c % 2][:], cols[:, 0, c:c + 1],
                                            cols[:, 1, c:c + 1], ALU.mult, ALU.add).then_inc(s_["zT"], 1)
                dve.wait_ge(s_["zT"], C)
                dve.wait_ge(s_["rate"], 1)
                for i in (1, 0, 2):
                    for c in range(C):
                        s.mark(nc.vector.tensor_scalar(prev[:, c, :, 1:P], zT[:, c, :, 0:P - 1], one_minus[:, i, c:c + 1],
                                                       None, ALU.mult))
                    s.wait()
                    for c in range(C):
                        nc.vector.scalar_tensor_tensor(out=mixed[i][:, c], in0=zT[:, c], scalar=cols[:, 2 + i, c:c + 1],
                                                       in1=prev[:, c], op0=ALU.mult, op1=ALU.add).then_inc(s_["mixed"], 1)
                    dve.wait_ge(s_["mixed"], C * {1: 1, 0: 2, 2: 3}[i])
                for o in range(C):
                    dve.wait_ge(s_["k_made"], o + 1)
                    dve.wait_ge(s_["vT"], o + 1)
                    nc.vector.tensor_tensor(kv[:, o].rearrange("p b t -> p (b t)"), vT[:, o, :], ps[(6 + o) % 8][:], ALU.mult) \
                        .then_inc(s_["kv"], 1)
                dve.wait_ge(s_["rate"], 2)
                dve.wait_ge(s_["kv"], C)
                for o in range(C):
                    for b in range(NB):
                        nc.vector.tensor_tensor_scan(state[:, o, b, :], rate[:, o, :], kv[:, o, b, :], 0.0, ALU.mult, ALU.add) \
                            .then_inc(s_["state"], 1)
                for b in range(NB):
                    s.mark(nc.vector.tensor_tensor(x[:, b, :], x[:, b, :], z[:, b, :], ALU.add))
                for b in range(NB):
                    dve.wait_ge(s_["o_made"], b + 1)
                    dve.wait_ge(s_["r"], b + 1)
                    s.mark(nc.vector.tensor_tensor(r[:, b, :], r[:, b, :], ps[(6 + b) % 8][:], ALU.mult))
                s.wait()
                for b in range(NB):
                    nc.vector.tensor_tensor(x[:, b, :], x[:, b, :], r[:, b, :], ALU.add).then_inc(s_["done"], 1)




def build(nc, t, out, stages=99):
    def dram(name, shape, dt=F32):
        return nc.dram_tensor(name, shape, dt, kind="Internal").ap()

    xs = [t["x"]] + [dram(f"x_{i}", (NB, P, D)) for i in range(1, 6)] + [out]
    q_hi, q_lo = dram("q_hi", (NB, P, C, P)), dram("q_lo", (NB, P, C, P))
    with ExitStack() as ctx:
        k = {
            "ident": ctx.enter_context(nc.sbuf_tensor("ident", [P, P], F32)),
            "ones": ctx.enter_context(nc.sbuf_tensor("ones", [P, P], F32)),
        }
        k["ps2"] = [ctx.enter_context(nc.psum_tensor(f"wide{i}", [P, 2 * 512], F32)) for i in range(2)]
        one = [ctx.enter_context(nc.psum_tensor(f"bank{i}", [P, 512], F32)) for i in range(4, 8)]
        k["ps"] = [k["ps2"][0][:, 0:512], k["ps2"][0][:, 512:1024], k["ps2"][1][:, 0:512], k["ps2"][1][:, 512:1024]] \
            + [x[:, :] for x in one]
        stage_constants(nc, k)

        def cross(layer, x_in, x_out, mask):
            L = f"L{layer}_xattn_"
            with ExitStack() as outer:
                attn = outer.enter_context(nc.sbuf_tensor(f"{L}attn", [P, NB, D], F32))
                with ExitStack() as inner:
                    weights = [tuple(inner.enter_context(nc.sbuf_tensor(f"{L}{w}_{p}", [P, C * D], F32R))
                                     for p in ("hi", "lo")) for w in ("wk", "wv")]
                    stage_project_q(nc, k, f"q{layer}", x_in, t[L + "Wq"], t[L + "bq"], t[L + "Wk"], t[L + "Wv"], weights,
                                    q_hi, q_lo, mask)
                    stage_attention(nc, k, f"a{layer}", t["ctx_1024"], weights, t[L + "bk"], q_hi, q_lo, attn,
                                    t["mask_turned"] if mask is not None else None)
                norm = layer == 1
                stage_attention_output(nc, k, f"o{layer}", attn, t[L + "bv"], t[L + "Wo"], t[L + "bo"],
                                       t[L + "gamma"] if norm else None, t[L + "beta"] if norm else None, x_in, x_out)

        def last(i):
            return out if stages == i else xs[i]

        cross(0, xs[0], last(1), t["mask_1x1xSxS2_bk0"])
        if stages >= 2:
            stage_retention(nc, k, t, xs[1], last(2))
        if stages >= 3:
            stage_experts(nc, k, "moe0", t, xs[2], last(3), 0)
        if stages >= 4:
            cross(1, xs[3], last(4), None)
        if stages >= 5:
            stage_rwkv(nc, k, t, xs[4], last(5))
        if stages >= 6:
            stage_experts(nc, k, "moe1", t, xs[5], out, 1)


def _tiles(a):
    return a.reshape(-1, P, a.shape[-1]).transpose(1, 0, 2)


def _columns(a):
    return a.reshape(-1, P).T


def _layout(name, a):
    if name == "ctx_1024":
        return a.reshape(NB, KEYS // CH, CH, C, P).transpose(0, 1, 4, 3, 2).reshape(NB * KEYS // CH, P, C * CH)
    if name == "mask_turned":
        return a.reshape(P, KT, P).transpose(2, 1, 0).reshape(P, KEYS)
    if name == "mask_1x1xSxS2_bk0":
        return a.reshape(P, KEYS)
    if "_xattn_W" in name or name in ("L1_attn_Wk", "L1_attn_Wv", "L1_attn_Wr", "L1_attn_Wo"):
        w = _tiles(a.T)
        return w.reshape(P, C * D) if name.endswith(("_Wk", "_Wv")) and "xattn" in name else w
    if name in ("L0_attn_w_attn", "L0_attn_w_proj", "L0_ffn_rw1", "L0_ffn_rw2", "L1_ffn_router_w"):
        return _tiles(a)
    if name == "L0_ffn_w1":
        return a.reshape(NE, C, P, C, D).transpose(0, 3, 2, 1, 4).reshape(NE * C, P, C * D)
    if name == "L0_ffn_w2":
        return a.reshape(NE, C, C, P, D).transpose(0, 1, 3, 2, 4).reshape(NE * C, P, C * D)
    if name in ("L1_ffn_we_gate", "L1_ffn_we_up", "L1_ffn_we_down"):
        return a.reshape(NE, C, P, D).transpose(0, 2, 1, 3).reshape(NE, P, C * D)
    if name == "L0_ffn_b1":
        return a.reshape(NE, HID // P, P).transpose(2, 0, 1).reshape(P, NE * HID // P)
    if name in ("L0_xattn_bq", "L0_xattn_bk", "L1_xattn_bq", "L1_xattn_bk", "L0_ffn_rb1", "L1_attn_ln_w", "L1_attn_ln_b",
                "L1_attn_tmk", "L1_attn_tmv", "L1_attn_tmr", "L1_attn_decay_w"):
        return _columns(a)
    return a


def _rotary():
    div = (2.0 * np.pi / float(P) ** (np.arange(0, RD, 2, dtype=np.float32) / RD)).astype(np.float32)
    ang = (np.arange(P, dtype=np.float32)[:, None] * div[None, :]).astype(np.float32)
    cos = np.repeat(np.cos(ang), 2, axis=-1)
    sin = np.repeat(np.sin(ang), 2, axis=-1)
    sin[:, 0::2] *= -1.0
    return np.stack([cos, sin], 1).astype(np.float32)


def kernel(**inputs):
    import concourse.bacc as _bacc
    from concourse import mybir as _mybir
    from concourse.bass_utils import run_bass_kernel_spmd as _run

    nc = _bacc.Bacc("TRN2", target_bir_lowering=False, num_devices=1)
    arrays, t = {}, {}
    inputs = dict(inputs, rotary=_rotary(), mask_turned=inputs["mask_1x1xSxS2_bk0"])
    for name, a in inputs.items():
        a = np.ascontiguousarray(_layout(name, np.asarray(a)))
        arrays[f"in_{name}"] = a
        t[name] = nc.dram_tensor(f"in_{name}", a.shape, _mybir.dt.from_np(a.dtype), kind="ExternalInput").ap()
    out = nc.dram_tensor("out_x", (NB, P, D), _mybir.dt.float32, kind="ExternalOutput").ap()
    build(nc, t, out, STAGES)
    r = _run(nc, [arrays], core_ids=[0])
    return r.results[0]["out_x"]


STAGES = 99
```

```python
from contextlib import ExitStack

import numpy as np

import concourse.bass as bass
from concourse import mybir
from concourse.alu_op_type import AluOpType as ALU

ACT = mybir.ActivationFunctionType
AX = mybir.AxisListType
F32 = mybir.dt.float32
F32R = mybir.dt.float32r
U8 = mybir.dt.uint8
U32 = mybir.dt.uint32

P = 128
D = 512
C = D // P
NB = 4
TOK = NB * P
KEYS = 2048
HEADS = 16
HD = D // HEADS
HPT = P // HD
CH = 256
KT = KEYS // P
QH, KVH, RD = 16, 8, 64
NE = 8
HID = 2048
LN_EPS = 1e-5
NEG = -1e9


class Mem:

    def __init__(self, nc, ctx, stage):
        self.nc, self.ctx, self.stage = nc, ctx, stage
        self.sems = []
        ctx.callback(self.clear)

    def sb(self, name, shape, dt=F32):
        return self.ctx.enter_context(self.nc.sbuf_tensor(f"{self.stage}_{name}", shape, dt))

    def sem(self, name):
        self.sems.append(self.nc.alloc_semaphore(f"{self.stage}_{name}"))
        return self.sems[-1]

    def clear(self):
        if self.sems:
            self.nc.clear_and_free_semaphores(self.sems)
            self.nc.all_engine_barrier()


class Steps:

    def __init__(self, engine, sem, turn=0, per_turn=0):
        self.engine, self.sem, self.base, self.n = engine, sem, turn * per_turn, 0

    def then(self, ins):
        self.mark(ins)
        self.engine.wait_ge(self.sem, self.base + self.n)

    def mark(self, ins):
        ins.then_inc(self.sem, 1)
        self.n += 1

    def wait(self):
        self.engine.wait_ge(self.sem, self.base + self.n)


def f32(ap):
    return ap.bitcast(F32)


def three_products(pe, out, w_hi, w_lo, m_hi, m_lo, start, stop, check=True):
    pe.matmul(out, w_hi, m_hi, start=start, stop=False, skip_group_check=not check)
    pe.matmul(out, w_hi, m_lo, start=False, stop=False, skip_group_check=not check)
    return pe.matmul(out, w_lo, m_hi, start=False, stop=stop, skip_group_check=not check)


def stage_constants(nc, k):
    with ExitStack() as ctx:
        m = Mem(nc, ctx, "const")
        filled, cut = m.sem("filled"), m.sem("cut")
        with nc.Block() as block:
            @block.gpsimd
            def _(pool):
                nc.gpsimd.memset(k["ident"][:], 0.0).then_inc(filled, 1)
                nc.gpsimd.memset(k["ones"][:], 1.0).then_inc(filled, 1)
                pool.wait_ge(filled, 2)
                nc.gpsimd.affine_select(out=k["ident"][:], in_=k["ident"][:], compare_op=ALU.not_equal, fill=1.0,
                                        base=0, pattern=[[-1, P]], channel_multiplier=1).then_inc(cut, 1)


def stage_project_q(nc, k, name, x_rows, x_in, wq, bq, wk, wv, weights, q_hi_out, q_lo_out, mask):
    with ExitStack() as ctx:
        m = Mem(nc, ctx, name)
        x = x_rows if x_in is None else m.sb("x", [P, NB, D])
        xn = m.sb("xn", [P, NB, D])
        xT = m.sb("xT", [P, C, TOK])
        wqT = m.sb("wqT", [P, C, D])
        wraw = m.sb("wraw", [P, 2, C * D])
        bcol = m.sb("bcol", [P, C])
        qf = m.sb("qf", [P, C, TOK])
        qhi = m.sb("qhi", [P, C, TOK], F32R)
        qlo = m.sb("qlo", [P, C, TOK], F32R)
        stats = m.sb("stats", [P, NB, 6])
        mv = m.sb("mv", [P, NB, 2])
        ve = m.sb("ve", [P, NB])
        std = m.sb("std", [P, NB])
        rstd = m.sb("rstd", [P, NB])
        x_in_sem, w_in, wq_in, b_in = m.sem("x_in"), m.sem("w_in"), m.sem("wq_in"), m.sem("b_in")
        dstep, var_ready, std_ready, xn_ready = m.sem("dstep"), m.sem("var"), m.sem("std"), m.sem("xn")
        turned, xT_ready, q_made = m.sem("turned"), m.sem("xT"), m.sem("q_made")
        lo_ready, whi_ready, wlo_ready, q_out = (m.sem(s) for s in ("lo", "whi", "wlo", "q_out"))
        if mask is not None:
            mraw = m.sb("mraw", [P, KEYS], U8)
            many = m.sb("many", [P, 1])
            manyr = m.sb("manyr", [P, P])
            manyT = m.sb("manyT", [P, P])
            m_in, any_ready, any_turned = m.sem("m_in"), m.sem("any_ready"), m.sem("any_turned")
        ps = k["ps"]
        with nc.Block() as block:
            @block.sync
            def _(sp):
                if x_in is not None:
                    sp.dma_start(x[:], x_in.rearrange("b p d -> p b d")).then_inc(x_in_sem, 16)
                sp.dma_start(wqT[:], wq).then_inc(wq_in, 16)
                sp.dma_start(bcol[:], bq).then_inc(b_in, 16)
                if mask is not None:
                    sp.dma_start(mraw[:], mask).then_inc(m_in, 16)
                sp.dma_start(wraw[:, 0, :], wk).then_inc(w_in, 16)
                sp.dma_start(wraw[:, 1, :], wv).then_inc(w_in, 16)
                for c in range(C):
                    sp.wait_ge(lo_ready, c + 1)
                    for dst, part in ((q_hi_out, qhi), (q_lo_out, qlo)):
                        sp.dma_start(dst[:, :, c, :].rearrange("b p t -> p b t"),
                                     f32(part[:, c, :]).rearrange("p (b t) -> p b t", b=NB)).then_inc(q_out, 16)
                sp.wait_ge(q_out, 32 * C)

            @block.vector
            def _(dve):
                s = Steps(dve, dstep)
                if x_in is not None:
                    dve.wait_ge(x_in_sem, 16)
                for b in range(NB):
                    s.mark(nc.vector.bn_stats(stats[:, b, :], x[:, b, :]))
                s.wait()
                for b in range(NB):
                    s.mark(nc.vector.bn_aggr(mv[:, b, :], stats[:, b, :]))
                s.wait()
                nc.vector.tensor_scalar_add(ve[:], mv[:, :, 1], LN_EPS).then_inc(var_ready, 1)
                dve.wait_ge(std_ready, 1)
                s.then(nc.vector.reciprocal(rstd[:], std[:]))
                for b in range(NB):
                    nc.vector.tensor_scalar(xn[:, b, :], x[:, b, :], mv[:, b, 0:1], rstd[:, b:b + 1],
                                            ALU.subtract, ALU.mult).then_inc(xn_ready, 1)
                if mask is not None:
                    dve.wait_ge(m_in, 16)
                    s.then(nc.vector.reduce_max(many[:], mraw[:], AX.X))
                    nc.vector.tensor_scalar(manyr[:], k["ones"][:], many[:, 0:1], None, ALU.mult).then_inc(any_ready, 1)
                    dve.wait_ge(any_turned, 1)
                    s.mark(nc.vector.tensor_copy(manyT[:], ps[7][:, 0:P]))
                for c in range(C):
                    dve.wait_ge(turned, c + 1)
                    nc.vector.tensor_copy(xT[:, c, :], ps[c % 2][:]).then_inc(xT_ready, 1)
                if mask is not None:
                    s.wait()
                dve.wait_ge(w_in, 32)
                for i, (hi, lo) in enumerate(weights):
                    dve.wait_ge(whi_ready, i + 1)
                    nc.vector.tensor_tensor(lo[:], wraw[:, i, :], f32(hi[:]), ALU.subtract).then_inc(wlo_ready, 1)
                dve.wait_ge(b_in, 16)
                for c in range(C):
                    dve.wait_ge(q_made, c + 1)
                    s.then(nc.vector.tensor_scalar(qf[:, c, :], ps[2 + c][:], bcol[:, c:c + 1], float(HD) ** -0.5,
                                                   ALU.add, ALU.mult))
                    if mask is not None:
                        for b in range(NB):
                            s.mark(nc.vector.tensor_tensor(qf[:, c, b * P:(b + 1) * P], qf[:, c, b * P:(b + 1) * P],
                                                           manyT[:], ALU.mult))
                        s.wait()
                    s.then(nc.vector.tensor_copy(qhi[:, c, :], qf[:, c, :]))
                    nc.vector.tensor_tensor(qlo[:, c, :], qf[:, c, :], f32(qhi[:, c, :]), ALU.subtract).then_inc(lo_ready, 1)

            @block.scalar
            def _(act):
                act.wait_ge(var_ready, 1)
                nc.scalar.sqrt(std[:], ve[:]).then_inc(std_ready, 1)
                act.wait_ge(w_in, 32)
                for i, (hi, lo) in enumerate(weights):
                    nc.scalar.copy(hi[:], wraw[:, i, :]).then_inc(whi_ready, 1)

            @block.tensor
            def _(pe):
                if mask is not None:
                    pe.wait_ge(any_ready, 1)
                    pe.transpose(ps[7][:, 0:P], manyr[:], k["ident"][:]).then_inc(any_turned, 1)
                for c in range(C):
                    pe.wait_ge(xn_ready, NB)
                    if c >= 2:
                        pe.wait_ge(xT_ready, c - 1)
                    for b in range(NB):
                        last = pe.transpose(ps[c % 2][:, b * P:(b + 1) * P], xn[:, b, c * P:(c + 1) * P], k["ident"][:])
                    last.then_inc(turned, 1)
                pe.wait_ge(xT_ready, C)
                pe.wait_ge(wq_in, 16)
                for o in range(C):
                    for c in range(C):
                        last = pe.matmul(ps[2 + o][:], wqT[:, c, o * P:(o + 1) * P], xT[:, c, :],
                                         start=(c == 0), stop=(c == C - 1))
                    last.then_inc(q_made, 1)


def prime(engine, *sems):
    for s in sems:
        engine.sem_inc(s, 1)


def turns(engine, n, body):
    with engine.Fori(0, n - 1) as i:
        body(i, True)
    body(n - 1, False)


def stage_attention(nc, k, name, ctxT, weights, bk, q_hi_in, q_lo_in, attn, mask):
    (wk_hi, wk_lo), (wv_hi, wv_lo) = weights
    masked = mask is not None
    KC = CH
    NKC = KEYS // KC
    KG, VG = NKC * C, KT
    PAIR = 2 * P
    U = HEADS // 2
    AG = 2
    NA = KT // AG
    NG, GT = 4, KT // 4
    AHEAD = 1
    VW = HD + 1
    HALF = P // 2
    ODD = HALF
    pool_groups = (0, 1, 2, 3) if masked else (1, 3)
    dve_groups = tuple(g for g in range(NG) if g not in pool_groups)
    with ExitStack() as ctx:
        m = Mem(nc, ctx, name)
        raw = m.sb("raw", [P, C, KC])
        chi, clo = m.sb("chi", [P, 2, C, KC], F32R), m.sb("clo", [P, 2, C, KC], F32R)
        kk = m.sb("kk", [P, U, KEYS], F32R)
        v = m.sb("v", [P, KT, HEADS, VW])
        q_hi, q_lo = m.sb("q_hi", [P, 2, PAIR], F32R), m.sb("q_lo", [P, 2, PAIR], F32R)
        st = m.sb("st", [P, 2, KT, PAIR])
        mxh = m.sb("mxh", [P, 2, PAIR])
        nmax = m.sb("nmax", [P, 2])
        diag = m.sb("diag", [P, 2, P])
        nmB = m.sb("nmB", [P, 2, PAIR])
        oT = m.sb("oT", [P, 2, P])
        rden = m.sb("rden", [P, 2, 2])
        bkcol = m.sb("bkcol", [P, C])
        sem = m.sem
        bk_in, raw_in, chi_ready, clo_ready, cleared = (sem(s) for s in ("bk_in", "raw_in", "chi", "clo", "cleared"))
        k_made, khi_done, k_done, v_made, v_done = (sem(s) for s in ("k_made", "khi_done", "k_done", "v_made", "v_done"))
        q_in = [sem(f"q_in_{i}") for i in range(2)]
        scored, kept, half_max, max_turned = (sem(s) for s in ("scored", "kept", "half_max", "max_turned"))
        max_row, diag_made, max_spread, nmB_ready = (sem(s) for s in ("max_row", "diag", "max_spread", "nmB"))
        sub_pool, sub_dve, exp_done, pv_done = (sem(s) for s in ("sub_pool", "sub_dve", "exp", "pv"))
        o_kept, o_turned, rden_done, o_done = (sem(s) for s in ("o_kept", "o_turned", "rden", "o_done"))
        ps = k["ps"]
        A = ps[0:3]
        MT, MB = ps[3], ps[4]
        O = ps[5:7]
        OT = ps[7]
        KB, VB = ps[0:3], ps[3:5]
        if masked:
            hidden = m.sb("hidden", [P, KT, 2, P], U8)
            mraw = st[:, 0].rearrange("p t q -> p (t q)").bitcast(U8)[:, 0:KEYS]
            m_in, hidden_ready = sem("m_in"), sem("hidden")

        with nc.Block() as block:
            @block.sync
            def _(sp):
                sp.dma_start(bkcol[:], bk).then_inc(bk_in, 16)
                if masked:
                    sp.dma_start(mraw, mask).then_inc(m_in, 16)
                sp.wait_ge(cleared, 4)
                def load_q(b, u):
                    sp.wait_ge(scored, b * U * NA + max(u - 1, 0) * NA + 1)
                    for part, src in ((q_hi, q_hi_in), (q_lo, q_lo_in)):
                        for i in range(2):
                            r = ((2 * u + i) % HPT) * HD
                            for half in range(2):
                                at = half * HALF + i * HD
                                sp.dma_start(f32(part[at:at + HD, u % 2, i * P:(i + 1) * P]),
                                             src[bass.ds(b, 1), r:r + HD, u // 2, :].rearrange("o p t -> (o p) t")) \
                                    .then_inc(q_in[u % 2], 16)

                def load_chunk(b, ch):
                    sp.wait_ge(clo_ready, b * NKC + ch + 1)
                    sp.dma_start(raw[:].rearrange("p c n -> p (c n)"),
                                 ctxT[bass.ds(b * NKC + ch, 1)].rearrange("o p n -> (o p) n")).then_inc(raw_in, 16)

                def body(b, more):
                    for ch in range(1, NKC):
                        load_chunk(b, ch)
                        if ch <= 2:
                            load_q(b, ch - 1)
                    for u in range(2, U):
                        load_q(b, u)
                    if more:
                        load_chunk(b + 1, 0)

                load_chunk(0, 0)
                turns(sp, NB, body)

            @block.gpsimd
            def _(pool):
                nc.gpsimd.memset(f32(q_hi[:]), 0.0).then_inc(cleared, 1)
                nc.gpsimd.memset(f32(q_lo[:]), 0.0).then_inc(cleared, 1)
                nc.gpsimd.memset(oT[:], 0.0).then_inc(cleared, 1)
                nc.gpsimd.memset(v[:, :, :, HD:VW], 1.0).then_inc(cleared, 1)
                prime(pool, sub_pool)
                with pool.Fori(0, NB) as b:
                    for u in range(U):
                        for i, g in enumerate(pool_groups):
                            pool.wait_ge(nmB_ready, b * U + u + 2)
                            nc.gpsimd.tensor_tensor(st[:, u % 2, g * GT:(g + 1) * GT, :], st[:, u % 2, g * GT:(g + 1) * GT, :],
                                                    nmB[:, u % 2, :].unsqueeze(1).to_broadcast([P, GT, PAIR]), ALU.add) \
                                .then_inc(sub_pool, 1)

            @block.tensor
            def _(pe):
                prime(pe, scored, pv_done, o_turned, max_spread)

                def project_k(b, ch, o):
                    if o == 0:
                        pe.wait_ge(clo_ready, b * NKC + ch + 2)
                    g = ch * C + o
                    if g < 3:
                        pe.wait_ge(kept, b * U * NA + 1)
                    pe.wait_ge(k_done, b * KG + max(g - 2, 0) + 1)
                    for c in range(C):
                        at = c * D + o * P
                        last = three_products(pe, KB[g % 3][:, 0:KC], wk_hi[:, at:at + P], wk_lo[:, at:at + P],
                                              chi[:, ch % 2, c, :], clo[:, ch % 2, c, :], c == 0, c == C - 1)
                    last.then_inc(k_made, 1)

                def project_v(b, ch, t):
                    g = ch * 2 + t
                    if g == 0:
                        pe.wait_ge(max_row, b * U + 1)
                    if g == 1:
                        pe.wait_ge(nmB_ready, b * U + 1)
                    pe.wait_ge(v_done, b * VG + max(g - 1, 0) + 1)
                    for c in range(C):
                        last = three_products(pe, VB[t][:], chi[:, ch % 2, c, t * P:(t + 1) * P],
                                              clo[:, ch % 2, c, t * P:(t + 1) * P],
                                              wv_hi[:, c * D:(c + 1) * D], wv_lo[:, c * D:(c + 1) * D],
                                              c == 0, c == C - 1)
                    last.then_inc(v_made, 1)

                def body(b, more):
                    project_v(b, 0, 0)
                    project_v(b, 0, 1)
                    for ch in range(1, NKC):
                        for i in range(C + KC // P):
                            if i % 3 == 2:
                                project_v(b, ch, i // 3)
                            else:
                                project_k(b, ch, i - i // 3)
                    pe.wait_ge(k_done, b * KG + KG + 1)
                    pe.wait_ge(v_done, b * VG + VG + 1)

                    def scores(u, j):
                        n = u * NA + j
                        if j == 0:
                            pe.wait_ge(q_in[u % 2], 128 * (b * (U // 2) + u // 2) + 128)
                        pe.wait_ge(kept, b * U * NA + max(n - 2, 0) + 1)
                        for i in range(AG):
                            t = j * AG + i
                            for part in (q_hi, q_lo):
                                last = pe.matmul(A[n % 3][:, i * PAIR:(i + 1) * PAIR], kk[:, u, t * P:(t + 1) * P],
                                                 part[:, u % 2, :], start=(part is q_hi), stop=(part is q_lo))
                        last.then_inc(scored, 1)

                    def turn_max(u):
                        pe.wait_ge(half_max, 2 * (b * U + u) + 3)
                        for half in range(2):
                            for i in range(2):
                                last = pe.transpose(MT[:, (2 * half + i) * P:(2 * half + i + 1) * P],
                                                    mxh[:, half, i * P:(i + 1) * P], k["ident"][:])
                        last.then_inc(max_turned, 1)

                    def spread_max(u):
                        pe.wait_ge(diag_made, b * U + u + 2)
                        pe.wait_ge(nmB_ready, b * U + u + 1)
                        pe.matmul(MB[:, 0:PAIR], k["ones"][:], diag[:].rearrange("p h q -> p (h q)"),
                                  start=True, stop=True).then_inc(max_spread, 1)

                    def outputs(u, g):
                        pe.wait_ge(exp_done, NG * (b * U + u) + g + 1)
                        if g == 0:
                            pe.wait_ge(o_kept, b * U + max(u - 1, 0) + 1)
                        for t in range(g * GT, (g + 1) * GT):
                            for i in range(2):
                                last = pe.matmul(O[u % 2][i * ODD:i * ODD + VW, 0:P], v[:, t, 2 * u + i, :],
                                                 st[:, u % 2, t, i * P:(i + 1) * P], start=(t == 0), stop=(t == KT - 1))
                        last.then_inc(pv_done, 1)

                    def turn_output(u):
                        pe.wait_ge(o_kept, b * U + u + 2)
                        pe.wait_ge(o_done, b * U + u + 1)
                        pe.transpose(OT[:, 0:ODD + VW], oT[0:ODD + VW, u % 2, :], k["ident"][0:ODD + VW, 0:ODD + VW]) \
                            .then_inc(o_turned, 1)

                    for j in range(NA):
                        scores(0, j)
                    for u in range(U + 1):
                        for g in range(NG):
                            if u >= 1:
                                outputs(u - 1, g)
                            if u + 1 < U:
                                scores(u + 1, 2 * g)
                                scores(u + 1, 2 * g + 1)
                            if g == 0:
                                if u < U:
                                    turn_max(u)
                                if u >= 2:
                                    turn_output(u - 2)
                            if g == 1 and u < U:
                                spread_max(u)
                            if more and u == U and g:
                                project_k(b + 1, 0, g - 1)
                    if more:
                        project_k(b + 1, 0, C - 1)
                    turn_output(U - 1)

                for o in range(C):
                    project_k(0, 0, o)
                turns(pe, NB, body)

            @block.vector
            def _(dve):
                prime(dve, clo_ready, k_done, half_max, max_row, diag_made, sub_dve, rden_done, o_done)
                if masked:
                    prime(dve, kept)
                    dve.wait_ge(m_in, 16)
                    for i in range(2):
                        nc.vector.tensor_scalar(hidden[:, :, i, :], mraw.rearrange("p (t q) -> p t q", t=KT), -1.0, 1.0,
                                                ALU.mult, ALU.add).then_inc(hidden_ready, 1)
                    dve.wait_ge(hidden_ready, 2)
                dve.wait_ge(bk_in, 16)

                def low_part(b, ch):
                    dve.wait_ge(chi_ready, b * NKC + ch + 1)
                    nc.vector.tensor_tensor(clo[:, ch % 2], raw[:], f32(chi[:, ch % 2]), ALU.subtract).then_inc(clo_ready, 1)

                def low_k(b, ch, o):
                    at = slice(ch * KC, (ch + 1) * KC)
                    g = ch * C + o
                    for half in range(2):
                        dve.wait_ge(khi_done, 2 * (b * KG + g) + half + 1)
                        rows, other = (slice(h * HALF, (h + 1) * HALF) for h in (half, 1 - half))
                        ins = nc.vector.scalar_tensor_tensor(
                            out=kk[other, 2 * o + half, at], in0=KB[g % 3][rows, 0:KC], scalar=bkcol[rows, o:o + 1],
                            in1=f32(kk[rows, 2 * o + half, at]), op0=ALU.add, op1=ALU.subtract)
                    ins.then_inc(k_done, 1)

                def body(b, more):
                    low_part(b, 1)
                    for ch in range(1, NKC):
                        for o in range(C):
                            low_k(b, ch, o)
                            if o == 1 and ch + 1 < NKC:
                                low_part(b, ch + 1)

                    def keep(u, j):
                        n = u * NA + j
                        dve.wait_ge(scored, b * U * NA + n + 2)
                        done = (u - 2) * NG + j // 2 + 1 if u >= 2 else 0
                        dve.wait_ge(pv_done, b * U * NG + done + 1)
                        ts = slice(j * AG, (j + 1) * AG)
                        nc.vector.scalar_tensor_tensor(
                            out=st[:, u % 2, ts, :].rearrange("p t q -> p (t q)"), in0=hidden[:, ts].rearrange("p t h q -> p (t h q)"),
                            scalar=NEG, in1=A[n % 3][:], op0=ALU.mult, op1=ALU.add).then_inc(kept, 1)

                    def reduce_half(u, half):
                        if half == 0:
                            dve.wait_ge(max_row, b * U + u + 1)
                        dve.wait_ge(kept, b * U * NA + u * NA + (half + 1) * NA // 2 + 1)
                        ts = slice(half * KT // 2, (half + 1) * KT // 2)
                        nc.vector.tensor_reduce(mxh[:, half, :], st[:, u % 2, ts, :].rearrange("p t q -> p q t"), AX.X, ALU.max) \
                            .then_inc(half_max, 1)

                    def max_of_row(u):
                        n = b * U + u
                        dve.wait_ge(max_turned, n + 1)
                        nc.vector.tensor_reduce(nmax[:], MT[:].rearrange("p (f h k) -> p h f k", f=2, h=2), AX.XY, ALU.max,
                                                negate=True).then_inc(max_row, 1)
                        dve.wait_ge(max_row, n + 2)
                        dve.wait_ge(max_spread, n + 1)
                        nc.vector.tensor_tensor(diag[:], k["ident"][:].unsqueeze(1).to_broadcast([P, 2, P]),
                                                nmax[:].unsqueeze(2).to_broadcast([P, 2, P]), ALU.mult).then_inc(diag_made, 1)

                    def subtract(u):
                        for g in dve_groups:
                            dve.wait_ge(nmB_ready, b * U + u + 2)
                            nc.vector.tensor_tensor(st[:, u % 2, g * GT:(g + 1) * GT, :], st[:, u % 2, g * GT:(g + 1) * GT, :],
                                                    nmB[:, u % 2, :].unsqueeze(1).to_broadcast([P, GT, PAIR]), ALU.add) \
                                .then_inc(sub_dve, 1)

                    def finish(u):
                        n = b * U + u
                        dve.wait_ge(o_turned, n + 2)
                        out = OT[:, 0:2 * ODD].rearrange("p (h d) -> p h d", h=2)
                        nc.vector.reciprocal(rden[:, u % 2, :], OT[:, HD:ODD + VW:ODD]).then_inc(rden_done, 1)
                        dve.wait_ge(rden_done, n + 2)
                        nc.vector.tensor_tensor(attn[:, bass.ds(b, 1), 2 * u * HD:(2 * u + 2) * HD]
                                                .rearrange("p o (h d) -> p (o h) d", h=2),
                                                out[:, :, 0:HD], rden[:, u % 2, :].unsqueeze(2).to_broadcast([P, 2, HD]),
                                                ALU.mult).then_inc(o_done, 1)

                    if masked:
                        for j in range(NA):
                            keep(0, j)
                    reduce_half(0, 0)
                    reduce_half(0, 1)
                    for u in range(U + 1):
                        for g in range(NG):
                            if masked and u + 1 < U:
                                keep(u + 1, 2 * g)
                                keep(u + 1, 2 * g + 1)
                            if g == 0:
                                if u < U:
                                    max_of_row(u)
                                if u >= 2:
                                    finish(u - 2)
                                if more and u == U:
                                    low_part(b + 1, 0)
                            if g == 1 and u < U:
                                subtract(u)
                                if u + 1 < U:
                                    reduce_half(u + 1, 0)
                            if g == 3 and u + 1 < U:
                                reduce_half(u + 1, 1)
                            if more and u == U and g:
                                low_k(b + 1, 0, g - 1)
                    if more:
                        low_k(b + 1, 0, C - 1)
                    finish(U - 1)

                low_part(0, 0)
                for o in range(C):
                    low_k(0, 0, o)
                turns(dve, NB, body)

            @block.scalar
            def _(act):
                prime(act, v_done, nmB_ready, o_kept)
                if not masked:
                    prime(act, kept)
                act.wait_ge(bk_in, 16)
                act.wait_ge(cleared, 4)

                def high_part(b, ch):
                    act.wait_ge(raw_in, 16 * (b * NKC + ch) + 16)
                    act.wait_ge(v_done, b * VG + max(ch - 1, 0) * (KC // P) + 1)
                    nc.scalar.copy(chi[:, ch % 2], raw[:]).then_inc(chi_ready, 1)

                def high_k(b, ch, o):
                    at = slice(ch * KC, (ch + 1) * KC)
                    act.wait_ge(k_made, b * KG + ch * C + o + 1)
                    for half in range(2):
                        rows = slice(half * HALF, (half + 1) * HALF)
                        nc.scalar.activation(kk[rows, 2 * o + half, at], KB[(ch * C + o) % 3][rows, 0:KC],
                                             ACT.Identity, bias=bkcol[rows, o:o + 1]).then_inc(khi_done, 1)

                def keep_v(b, ch, t):
                    act.wait_ge(v_made, b * VG + ch * 2 + t + 1)
                    nc.scalar.copy(v[:, ch * 2 + t, :, 0:HD], VB[t][:].rearrange("p (h d) -> p h d", h=HEADS)) \
                        .then_inc(v_done, 1)

                def body(b, more):
                    high_part(b, 1)
                    keep_v(b, 0, 0)
                    keep_v(b, 0, 1)
                    for ch in range(1, NKC):
                        for i in range(C + KC // P):
                            if i % 3 == 2:
                                keep_v(b, ch, i // 3)
                            else:
                                o = i - i // 3
                                high_k(b, ch, o)
                                if o == 1 and ch + 1 < NKC:
                                    high_part(b, ch + 1)

                    def keep(u, j):
                        n = u * NA + j
                        act.wait_ge(scored, b * U * NA + n + 2)
                        done = (u - 2) * NG + j // 2 + 1 if u >= 2 else 0
                        act.wait_ge(pv_done, b * U * NG + done + 1)
                        nc.scalar.copy(st[:, u % 2, j * AG:(j + 1) * AG, :].rearrange("p t q -> p (t q)"), A[n % 3][:]) \
                            .then_inc(kept, 1)

                    def keep_max(u):
                        act.wait_ge(max_spread, b * U + u + 2)
                        nc.scalar.copy(nmB[:, u % 2, :], MB[:, 0:PAIR]).then_inc(nmB_ready, 1)

                    def exponent(u, g):
                        n = b * U + u
                        if g in pool_groups:
                            act.wait_ge(sub_pool, n * len(pool_groups) + pool_groups.index(g) + 2)
                        else:
                            act.wait_ge(sub_dve, n * len(dve_groups) + dve_groups.index(g) + 2)
                        part = st[:, u % 2, g * GT:(g + 1) * GT, :].rearrange("p t q -> p (t q)")
                        nc.scalar.activation(part, part, ACT.Exp).then_inc(exp_done, 1)

                    def keep_output(u):
                        act.wait_ge(pv_done, NG * (b * U + u) + NG + 1)
                        act.wait_ge(o_turned, b * U + max(u - 1, 0) + 1)
                        for i in range(2):
                            ins = nc.scalar.copy(oT[i * ODD:i * ODD + VW, u % 2, :], O[u % 2][i * ODD:i * ODD + VW, 0:P])
                        ins.then_inc(o_kept, 1)

                    if not masked:
                        for j in range(NA):
                            keep(0, j)
                    for u in range(U + 1):
                        for g in range(NG):
                            n = u * NG + g - NG + AHEAD
                            if 0 <= n < U * NG:
                                exponent(n // NG, n % NG)
                            if not masked and u + 1 < U:
                                keep(u + 1, 2 * g)
                                keep(u + 1, 2 * g + 1)
                            if g == 1 and u < U:
                                keep_max(u)
                            if more and u == U - 1 and g == NG - 1:
                                high_part(b + 1, 0)
                            if more and u == U and g:
                                high_k(b + 1, 0, g - 1)
                        if u >= 1:
                            keep_output(u - 1)
                    if more:
                        high_k(b + 1, 0, C - 1)

                high_part(0, 0)
                for o in range(C):
                    high_k(0, 0, o)
                turns(act, NB, body)


def stage_attention_output(nc, k, name, a, bv, wo, bo, gamma, beta, x_in, x_out):
    with ExitStack() as ctx:
        m = Mem(nc, ctx, name)
        ab = m.sb("ab", [P, NB, D])
        x = m.sb("x", [P, NB, D])
        y = m.sb("y", [P, NB, D])
        y2 = m.sb("y2", [P, NB, D])
        aT = m.sb("aT", [P, C, TOK])
        woT = m.sb("woT", [P, C, D])
        rows = m.sb("rows", [P, 4, D])
        stats, mv = m.sb("stats", [P, NB, 6]), m.sb("mv", [P, NB, 2])
        ve, std, rstd = m.sb("ve", [P, NB]), m.sb("std", [P, NB]), m.sb("rstd", [P, NB])
        w_in, x_sem, r_in = m.sem("w_in"), m.sem("x_in"), m.sem("r_in")
        dstep, ab_ready, turned, aT_ready, made = (m.sem(s) for s in ("dstep", "ab", "turned", "aT", "made"))
        var_ready, std_ready, done, stored = (m.sem(s) for s in ("var", "std", "done", "stored"))
        ps = k["ps"]
        row_list = [bv, bo] + ([gamma, beta] if gamma is not None else [])
        with nc.Block() as block:
            @block.sync
            def _(sp):
                for i, r in enumerate(row_list):
                    sp.dma_start(rows[:, i, :], r.partition_broadcast(P)).then_inc(r_in, 16)
                sp.dma_start(woT[:], wo).then_inc(w_in, 16)
                sp.dma_start(x[:], x_in.rearrange("b p d -> p b d")).then_inc(x_sem, 16)
                if x_out is not None:
                    sp.wait_ge(done, NB)
                    sp.dma_start(x_out.rearrange("b p d -> p b d"), a[:]).then_inc(stored, 16)
                    sp.wait_ge(stored, 16)

            @block.tensor
            def _(pe):
                pe.wait_ge(ab_ready, NB)
                for c in range(C):
                    if c >= 2:
                        pe.wait_ge(aT_ready, c - 1)
                    for b in range(NB):
                        last = pe.transpose(ps[c % 2][:, b * P:(b + 1) * P], ab[:, b, c * P:(c + 1) * P], k["ident"][:])
                    last.then_inc(turned, 1)
                pe.wait_ge(aT_ready, C)
                pe.wait_ge(w_in, 16)
                for b in range(NB):
                    for c in range(C):
                        last = pe.matmul(ps[2 + b][:], aT[:, c, b * P:(b + 1) * P], woT[:, c, :],
                                         start=(c == 0), stop=(c == C - 1))
                    last.then_inc(made, 1)

            @block.scalar
            def _(act):
                for c in range(C):
                    act.wait_ge(turned, c + 1)
                    nc.scalar.copy(aT[:, c, :], ps[c % 2][:]).then_inc(aT_ready, 1)
                if gamma is not None:
                    act.wait_ge(var_ready, 1)
                    nc.scalar.sqrt(std[:], ve[:]).then_inc(std_ready, 1)

            @block.vector
            def _(dve):
                s = Steps(dve, dstep)
                dve.wait_ge(r_in, 16 * len(row_list))
                for b in range(NB):
                    nc.vector.tensor_tensor(ab[:, b, :], a[:, b, :], rows[:, 0, :], ALU.add).then_inc(ab_ready, 1)
                dve.wait_ge(x_sem, 16)
                for b in range(NB):
                    dve.wait_ge(made, b + 1)
                    s.mark(nc.vector.tensor_tensor(y[:, b, :], ps[2 + b][:], rows[:, 1, :], ALU.add))
                s.wait()
                last_y = y
                if gamma is not None:
                    for b in range(NB):
                        s.mark(nc.vector.bn_stats(stats[:, b, :], y[:, b, :]))
                    s.wait()
                    for b in range(NB):
                        s.mark(nc.vector.bn_aggr(mv[:, b, :], stats[:, b, :]))
                    s.wait()
                    nc.vector.tensor_scalar_add(ve[:], mv[:, :, 1], LN_EPS).then_inc(var_ready, 1)
                    dve.wait_ge(std_ready, 1)
                    s.then(nc.vector.reciprocal(rstd[:], std[:]))
                    for b in range(NB):
                        s.mark(nc.vector.tensor_scalar(y2[:, b, :], y[:, b, :], mv[:, b, 0:1], rstd[:, b:b + 1],
                                                       ALU.subtract, ALU.mult))
                    s.wait()
                    for b in range(NB):
                        s.mark(nc.vector.tensor_tensor(y[:, b, :], y2[:, b, :], rows[:, 2, :], ALU.mult))
                    s.wait()
                    for b in range(NB):
                        s.mark(nc.vector.tensor_tensor(y2[:, b, :], y[:, b, :], rows[:, 3, :], ALU.add))
                    s.wait()
                    last_y = y2
                for b in range(NB):
                    nc.vector.tensor_tensor(a[:, b, :], x[:, b, :], last_y[:, b, :], ALU.add).then_inc(done, 1)


def stage_retention(nc, k, t, x, x_out):
    QD, KD = QH * RD, KVH * RD
    WIDE = QD + 2 * KD + KVH
    ROT = QH + KVH
    NPJ = WIDE // D + 1
    with ExitStack() as ctx:
        m = Mem(nc, ctx, "ret")
        w = m.sb("w", [P, C, WIDE])
        wp = m.sb("wp", [P, 2 * C, D])
        rot = m.sb("rot", [P, 2, RD])
        lnw = m.sb("lnw", [P, RD])
        causal = m.sb("causal", [P, P])
        upto = m.sb("upto", [P, P])
        after = m.sb("after", [P, P])
        xn = m.sb("xn", [P, D])
        xT = m.sb("xT", [P, C, P])
        qk = m.sb("qk", [P, ROT, RD])
        qkr = m.sb("qkr", [P, ROT, RD])
        qks = m.sb("qks", [P, ROT, RD])
        qr = m.sb("qr", [P, QH, RD])
        kr = m.sb("kr", [P, KVH, 2, RD])
        vx = m.sb("vx", [P, NB, KVH, RD + 1])
        gate = m.sb("gate", [P, 6, KVH])
        cut = m.sb("cut", [P, KVH, P])
        decay = m.sb("decay", [P, KVH, P])
        qT, kT = m.sb("qT", [P, KVH, P]), m.sb("kT", [P, KVH, P])
        s_abs, u = m.sb("s_abs", [P, QH, P]), m.sb("u", [P, QH, P])
        um, ru = m.sb("um", [P, QH]), m.sb("ru", [P, QH])
        aT = m.sb("aT", [P, QH, P])
        y, yc, y2 = m.sb("y", [P, QH, RD]), m.sb("yc", [P, QH, RD]), m.sb("y2", [P, QH, RD])
        col = m.sb("col", [P, 6, QH])
        yT = m.sb("yT", [P, 2 * C, P])
        stats, mv = m.sb("stats", [P, NB, 6]), m.sb("mv", [P, NB, 2])
        ve, std, rstd = m.sb("ve", [P, NB]), m.sb("std", [P, NB]), m.sb("rstd", [P, NB])
        S = {}
        for n in ("const_in", "w_in", "wp_in", "filled", "lstep", "fstep", "bstep", "var", "std", "xn", "xturned", "xT", "proj", "proj_read",
                  "gate_in", "e_gate", "gate_1", "l_gate", "cut", "decay_made", "decay_exp", "rotated", "qk_turned", "qk_copied",
                  "scores", "abs", "r_ready", "squared", "a_turned", "a_copied", "num", "yvar", "ystd", "y_ready",
                  "y_turned", "y_copied", "out_made", "res", "stored"):
            S[n] = m.sem(n)
        ps, ps2 = k["ps"], k["ps2"]

        with nc.Block() as block:
            @block.sync
            def _(sp):
                sp.dma_start(w[:], t["L0_attn_w_attn"]).then_inc(S["w_in"], 16)
                sp.dma_start(rot[:], t["rotary"]).then_inc(S["const_in"], 16)
                sp.dma_start(lnw[:], t["L0_attn_ln_w"].partition_broadcast(P)).then_inc(S["const_in"], 16)
                sp.dma_start(wp[:], t["L0_attn_w_proj"]).then_inc(S["wp_in"], 16)
                if x_out is not None:
                    for b in range(NB):
                        sp.wait_ge(S["res"], b + 2)
                        sp.dma_start(x_out[b], x[:, b, :]).then_inc(S["stored"], 16)
                    sp.wait_ge(S["stored"], 16 * NB)

            @block.gpsimd
            def _(pool):
                nc.gpsimd.memset(vx[:, :, :, RD:RD + 1], 1.0).then_inc(S["filled"], 1)
                nc.gpsimd.affine_select(out=causal[:], in_=k["ones"][:], compare_op=ALU.is_ge, fill=0.0, base=0,
                                        pattern=[[-1, P]], channel_multiplier=1).then_inc(S["filled"], 1)
                nc.gpsimd.affine_select(out=upto[:], in_=k["ones"][:], compare_op=ALU.is_ge, fill=0.0, base=0,
                                        pattern=[[1, P]], channel_multiplier=-1).then_inc(S["filled"], 1)
                nc.gpsimd.affine_select(out=after[:], in_=k["ones"][:], compare_op=ALU.is_gt, fill=0.0, base=0,
                                        pattern=[[-1, P]], channel_multiplier=1).then_inc(S["filled"], 1)

            @block.tensor
            def _(pe):
                def turn_x(b):
                    pe.wait_ge(S["xn"], b + 1)
                    for c in range(C):
                        last = pe.transpose(ps[4][:, c * P:(c + 1) * P], xn[:, c * P:(c + 1) * P], k["ident"][:])
                    last.then_inc(S["xturned"], 1)

                def project(b, first):
                    pe.wait_ge(S["xT"], b + 1)
                    if first:
                        pe.wait_ge(S["w_in"], 16)
                    for g in range(NPJ):
                        n = min(D, WIDE - g * D)
                        if g == 1 and not first:
                            pe.wait_ge(S["res"], b)
                        if g >= 2:
                            pe.wait_ge(S["proj_read"], b * NPJ + g - 1)
                        for c in range(C):
                            last = pe.matmul(ps[5 + g % 2][:, 0:n], xT[:, c, :], w[:, c, g * D:g * D + n],
                                             start=(c == 0), stop=(c == C - 1))
                        last.then_inc(S["proj"], 1)

                def decay_and_turns(b):
                    pe.wait_ge(S["cut"], b + 1)
                    for i in range(2):
                        pe.matmul(ps[6 + i][:], upto[:], cut[:, i * 4:(i + 1) * 4, :].rearrange("p h s -> p (h s)"),
                                  start=True, stop=True).then_inc(S["decay_made"], 1)
                    for i in range(4):
                        src = qr if i < 2 else kr
                        flat = src[:].rearrange("p h d -> p (h d)") if i < 2 else src[:].rearrange("p h r d -> p (h r d)")
                        if i % 2 == 0:
                            pe.wait_ge(S["rotated"], 2 * b + i // 2 + 2)
                        if i >= 2:
                            pe.wait_ge(S["qk_copied"], 4 * b + i - 1)
                        for j in range(4):
                            at = ((i % 2) * 4 + j) * P
                            last = pe.transpose(ps[4 + i % 2][:, j * P:(j + 1) * P], flat[:, at:at + P], k["ident"][:])
                        last.then_inc(S["qk_turned"], 1)

                def front(b):
                    turn_x(b)
                    project(b, True)
                    decay_and_turns(b)
                    pe.wait_ge(S["wp_in"], 16)

                def turn(b, more):
                    pe.wait_ge(S["qk_copied"], 4 * b + 4)
                    if more:
                        turn_x(b + 1)
                    for r in range(2):
                        for h in range(KVH):
                            last = pe.matmul(ps2[r][:, h * P:(h + 1) * P], qT[r * RD:(r + 1) * RD, h, :],
                                             kT[r * RD:(r + 1) * RD, h, :], start=True, stop=True)
                        last.then_inc(S["scores"], 1)
                    if more:
                        project(b + 1, False)
                    pe.wait_ge(S["squared"], b + 1)
                    for i in range(4):
                        if i == 1 and more:
                            pe.wait_ge(S["proj_read"], (b + 2) * NPJ)
                        if i >= 2:
                            pe.wait_ge(S["a_copied"], 4 * b + i - 1)
                        for j in range(4):
                            last = pe.transpose(ps[4 + i % 2][:, j * P:(j + 1) * P], s_abs[:, i * 4 + j, :], k["ident"][:])
                        last.then_inc(S["a_turned"], 1)
                    for i in range(4):
                        pe.wait_ge(S["a_copied"], 4 * b + i + 1)
                        for h in range(4 * i, 4 * i + 4):
                            last = pe.matmul(ps[i][:, (h % 4) * (RD + 1):(h % 4 + 1) * (RD + 1)], aT[:, h, :],
                                             vx[:, bass.ds(b, 1), h // 2, :].rearrange("p o d -> p (o d)"), start=True, stop=True)
                        last.then_inc(S["num"], 1)
                    if more:
                        decay_and_turns(b + 1)
                    pe.wait_ge(S["y_ready"], b + 1)
                    pe.wait_ge(S["qk_copied"], 4 * (b + 2) if more else 4 * (b + 1))
                    flat = y2[:].rearrange("p h d -> p (h d)")
                    for i in range(2):
                        for j in range(4):
                            last = pe.transpose(ps[4 + i][:, j * P:(j + 1) * P], flat[:, (i * 4 + j) * P:(i * 4 + j + 1) * P], k["ident"][:])
                        last.then_inc(S["y_turned"], 1)
                    if more:
                        pe.wait_ge(S["decay_exp"], 2 * (b + 2))
                    for c in range(2 * C):
                        if c % 4 == 0:
                            pe.wait_ge(S["y_copied"], 2 * b + c // 4 + 1)
                        last = pe.matmul(ps[6][:], yT[:, c, :], wp[:, c, :], start=(c == 0), stop=(c == 2 * C - 1))
                    last.then_inc(S["out_made"], 1)

                pe.wait_ge(S["filled"], 4)
                prime(pe, S["xturned"])
                front(0)
                turns(pe, NB, turn)

            @block.scalar
            def _(act):
                def keep_xT(b):
                    act.wait_ge(S["xturned"], b + 2)
                    nc.scalar.copy(xT[:].rearrange("p c t -> p (c t)"), ps[4][:]).then_inc(S["xT"], 1)

                def keep_projection(b, g):
                    act.wait_ge(S["proj"], b * NPJ + g + 1)
                    if g == 0:
                        act.wait_ge(S["rotated"], 2 * b + 1)
                    src = ps[5 + g % 2]
                    if g < 3:
                        ins = nc.scalar.copy(qk[:, g * 8:(g + 1) * 8, :], src[:].rearrange("p (h d) -> p h d", d=RD))
                    elif g == 3:
                        ins = nc.scalar.copy(vx[:, bass.ds(b, 1), :, 0:RD].rearrange("p o h d -> p (o h) d"),
                                             src[:].rearrange("p (h d) -> p h d", d=RD))
                    else:
                        ins = nc.scalar.copy(gate[:, 0, :], src[:, 0:KVH])
                    ins.then_inc(S["proj_read"], 1)

                def gates(b):
                    act.wait_ge(S["gate_in"], b + 1)
                    nc.scalar.activation(gate[:, 2, :], gate[:, 1, :], ACT.Exp, scale=-1.0).then_inc(S["e_gate"], 1)
                    act.wait_ge(S["gate_1"], b + 1)
                    nc.scalar.activation(gate[:, 4, :], gate[:, 3, :], ACT.Ln).then_inc(S["l_gate"], 1)

                def decay_and_turns(b):
                    for i in range(2):
                        act.wait_ge(S["decay_made"], 2 * b + i + 1)
                        nc.scalar.activation(decay[:, i * 4:(i + 1) * 4, :].rearrange("p h s -> p (h s)"), ps[6 + i][:],
                                             ACT.Exp, scale=0.5).then_inc(S["decay_exp"], 1)
                    for i in range(4):
                        act.wait_ge(S["qk_turned"], 4 * b + i + 1)
                        dst = (qT if i < 2 else kT)[:, (i % 2) * 4:(i % 2 + 1) * 4, :].rearrange("p h t -> p (h t)")
                        nc.scalar.copy(dst, ps[4 + i % 2][:]).then_inc(S["qk_copied"], 1)

                def front(b):
                    keep_xT(b)
                    for g in range(NPJ):
                        keep_projection(b, g)
                    gates(b)
                    decay_and_turns(b)

                def turn(b, more):
                    if more:
                        keep_xT(b + 1)
                    for r in range(2):
                        act.wait_ge(S["scores"], 2 * b + r + 1)
                        nc.scalar.activation(s_abs[:, r:QH:2, :], ps2[r][:].rearrange("p (h s) -> p h s", s=P), ACT.Abs,
                                             scale=float(RD) ** -0.5).then_inc(S["abs"], 1)
                    if more:
                        for g in range(NPJ):
                            keep_projection(b + 1, g)
                    act.wait_ge(S["r_ready"], b + 1)
                    nc.scalar.square(s_abs[:], u[:]).then_inc(S["squared"], 1)
                    for i in range(4):
                        act.wait_ge(S["a_turned"], 4 * b + i + 1)
                        nc.scalar.copy(aT[:, i * 4:(i + 1) * 4, :].rearrange("p h t -> p (h t)"), ps[4 + i % 2][:]) \
                            .then_inc(S["a_copied"], 1)
                    if more:
                        gates(b + 1)
                        decay_and_turns(b + 1)
                    act.wait_ge(S["yvar"], b + 1)
                    nc.scalar.sqrt(col[:, 3, :], col[:, 2, :]).then_inc(S["ystd"], 1)
                    for i in range(2):
                        act.wait_ge(S["y_turned"], 2 * b + i + 1)
                        nc.scalar.copy(yT[:, i * 4:(i + 1) * 4, :].rearrange("p c t -> p (c t)"), ps[4 + i][:]) \
                            .then_inc(S["y_copied"], 1)

                act.wait_ge(S["var"], 1)
                nc.scalar.sqrt(std[:], ve[:]).then_inc(S["std"], 1)
                front(0)
                turns(act, NB, turn)

            @block.vector
            def _(dve):
                def normalise(b):
                    dve.wait_ge(S["xturned"], b + 1)
                    nc.vector.tensor_scalar(xn[:], x[:, bass.ds(b, 1), :].rearrange("p o d -> p (o d)"),
                                            mv[:, bass.ds(b, 1), 0:1].rearrange("p o e -> p (o e)"), rstd[:, bass.ds(b, 1)],
                                            ALU.subtract, ALU.mult).then_inc(S["xn"], 1)

                def rotate(b):
                    s = Steps(dve, S["fstep"], b, RET_FRONT_STEPS)
                    dve.wait_ge(S["proj_read"], b * NPJ + NPJ)
                    s.then(nc.vector.tensor_scalar_add(gate[:, 0, :], gate[:, 0, :], 6.906768))
                    nc.vector.scalar_tensor_tensor(out=gate[:, 1, :], in0=gate[:, 0, :], scalar=-1.0, in1=gate[:, 0, :],
                                                   op0=ALU.mult, op1=ALU.max).then_inc(S["gate_in"], 1)
                    cos = rot[:, 0:1, :].to_broadcast([P, ROT, RD])
                    pairs = qk[:].rearrange("p h (i e) -> p h i e", e=2)
                    spairs = qks[:].rearrange("p h (i e) -> p h i e", e=2)
                    sinp = rot[:, 1, :].rearrange("p (i e) -> p i e", e=2)
                    s.mark(nc.vector.tensor_tensor(qkr[:], qk[:], cos, ALU.mult))
                    dve.wait_ge(S["e_gate"], b + 1)
                    nc.vector.tensor_scalar_add(gate[:, 3, :], gate[:, 2, :], 1.0).then_inc(S["gate_1"], 1)
                    for e in range(2):
                        sin_e = sinp[:, :, e].unsqueeze(1).to_broadcast([P, ROT, RD // 2])
                        s.mark(nc.vector.tensor_tensor(spairs[:, :, :, e], pairs[:, :, :, 1 - e], sin_e, ALU.mult))
                    dve.wait_ge(S["l_gate"], b + 1)
                    s.then(nc.vector.scalar_tensor_tensor(out=gate[:, 5, :], in0=gate[:, 0, :], scalar=0.0, in1=gate[:, 4, :],
                                                          op0=ALU.min, op1=ALU.subtract))
                    nc.vector.tensor_tensor(cut[:], after[:].unsqueeze(1).to_broadcast([P, KVH, P]),
                                            gate[:, 5, :].unsqueeze(2).to_broadcast([P, KVH, P]), ALU.mult).then_inc(S["cut"], 1)
                    nc.vector.tensor_tensor(qr[:], qkr[:, 0:QH], qks[:, 0:QH], ALU.add).then_inc(S["rotated"], 1)
                    s.mark(nc.vector.tensor_tensor(kr[:, :, 0, :], qkr[:, QH:ROT], qks[:, QH:ROT], ALU.add))
                    nc.vector.tensor_tensor(kr[:, :, 1, :], qkr[:, QH:ROT], qks[:, QH:ROT], ALU.add).then_inc(S["rotated"], 1)
                    assert s.n == RET_FRONT_STEPS, s.n

                def front(b):
                    normalise(b)
                    dve.wait_ge(S["const_in"], 32)
                    rotate(b)

                def turn(b, more):
                    if more:
                        normalise(b + 1)
                    s = Steps(dve, S["bstep"], b, RET_BACK_STEPS)
                    dve.wait_ge(S["decay_exp"], 2 * b + 2)
                    s.then(nc.vector.tensor_tensor(decay[:], decay[:], causal[:].unsqueeze(1).to_broadcast([P, KVH, P]), ALU.mult))
                    for r in range(2):
                        dve.wait_ge(S["abs"], 2 * b + r + 1)
                        s.mark(nc.vector.scalar_tensor_tensor(out=u[:, r:QH:2, :], in0=s_abs[:, r:QH:2, :], scalar=1e-30,
                                                              in1=decay[:], op0=ALU.add, op1=ALU.mult))
                    s.wait()
                    s.then(nc.vector.tensor_reduce(um[:], u[:], AX.X, ALU.max))
                    s.then(nc.vector.reciprocal(ru[:], um[:]))
                    nc.vector.tensor_tensor(u[:], u[:], ru[:].unsqueeze(2).to_broadcast([P, QH, P]), ALU.mult) \
                        .then_inc(S["r_ready"], 1)
                    if more:
                        rotate(b + 1)
                    for i in range(4):
                        dve.wait_ge(S["num"], 4 * b + i + 1)
                        at = ps[i][:, 0:4 * (RD + 1)].rearrange("p (h d) -> p h d", h=4)
                        s.then(nc.vector.tensor_scalar_add(col[:, 0, i * 4:(i + 1) * 4], at[:, :, RD], 1e-6))
                        s.then(nc.vector.reciprocal(col[:, 1, i * 4:(i + 1) * 4], col[:, 0, i * 4:(i + 1) * 4]))
                        s.mark(nc.vector.tensor_tensor(y[:, i * 4:(i + 1) * 4, :], at[:, :, 0:RD],
                                                       col[:, 1, i * 4:(i + 1) * 4].unsqueeze(2).to_broadcast([P, 4, RD]), ALU.mult))
                    s.wait()
                    s.then(nc.vector.reduce_sum(col[:, 4, :], y[:], AX.X))
                    s.then(nc.vector.tensor_scalar(col[:, 5, :], col[:, 4, :], 1.0 / RD, None, ALU.mult))
                    s.then(nc.vector.tensor_tensor(yc[:], y[:], col[:, 5, :].unsqueeze(2).to_broadcast([P, QH, RD]), ALU.subtract))
                    s.then(nc.vector.tensor_tensor(y[:], yc[:], yc[:], ALU.mult))
                    s.then(nc.vector.reduce_sum(col[:, 4, :], y[:], AX.X))
                    nc.vector.tensor_scalar(col[:, 2, :], col[:, 4, :], 1.0 / RD, 1e-9, ALU.mult, ALU.add).then_inc(S["yvar"], 1)
                    dve.wait_ge(S["ystd"], b + 1)
                    s.then(nc.vector.reciprocal(col[:, 5, :], col[:, 3, :]))
                    s.then(nc.vector.tensor_tensor(y[:], yc[:], col[:, 5, :].unsqueeze(2).to_broadcast([P, QH, RD]), ALU.mult))
                    nc.vector.tensor_tensor(y2[:], y[:], lnw[:].unsqueeze(1).to_broadcast([P, QH, RD]), ALU.mult) \
                        .then_inc(S["y_ready"], 1)
                    dve.wait_ge(S["out_made"], b + 1)
                    row = x[:, bass.ds(b, 1), :].rearrange("p o d -> p (o d)")
                    nc.vector.tensor_tensor(row, row, ps[6][:], ALU.add).then_inc(S["res"], 1)
                    assert s.n == RET_BACK_STEPS, s.n

                s = Steps(dve, S["lstep"])
                for b in range(NB):
                    s.mark(nc.vector.bn_stats(stats[:, b, :], x[:, b, :]))
                s.wait()
                for b in range(NB):
                    s.mark(nc.vector.bn_aggr(mv[:, b, :], stats[:, b, :]))
                s.wait()
                nc.vector.tensor_scalar_add(ve[:], mv[:, :, 1], LN_EPS).then_inc(S["var"], 1)
                dve.wait_ge(S["std"], 1)
                s.then(nc.vector.reciprocal(rstd[:], std[:]))
                dve.wait_ge(S["filled"], 4)
                prime(dve, S["rotated"], S["res"])
                front(0)
                turns(dve, NB, turn)


RET_FRONT_STEPS = 6
RET_BACK_STEPS = 24


def stage_experts(nc, k, name, t, x, x_out, layer):
    HT = HID // P if layer == 0 else C
    GR = HT // C
    with ExitStack() as ctx:
        m = Mem(nc, ctx, name)
        xhi, xlo = m.sb("xhi", [P, C, TOK], F32R), m.sb("xlo", [P, C, TOK], F32R)
        weT = m.sb("weT", [NE, TOK])
        weB = m.sb("weB", [P, NE, TOK])
        b2 = m.sb("b2", [NE, D])
        b1 = m.sb("b1", [P, NE * HT]) if layer == 0 else None
        names = ("L0_ffn_w1", "L0_ffn_w2") if layer == 0 else ("L1_ffn_we_gate", "L1_ffn_we_up", "L1_ffn_we_down")
        wraw = [m.sb(f"wraw{i}", [P, C * D]) for i in range(len(names))]
        w_in = [m.sem(f"w{i}_in") for i in range(len(names))]
        NW = len(names)
        whi = [m.sb(f"whi{i}", [P, 2, C * D], F32R) for i in range(NW)]
        wlo = [m.sb(f"wlo{i}", [P, 2, C * D], F32R) for i in range(NW)]
        whi_ready, wlo_ready = m.sem("whi"), m.sem("wlo")
        prep_done = {n: m.sem(n) for n in ("b_in", "xlo_ready", "weB_ready")}
        ps = k["ps"]
        Y = ps[0:4]
        with ExitStack() as prep:
            p = Mem(nc, prep, name + "p")
            xT = p.sb("xT", [P, C, TOK])
            stats, mv = p.sb("stats", [P, NB, 6]), p.sb("mv", [P, NB, 2])
            ve, std, rstd = p.sb("ve", [P, NB]), p.sb("std", [P, NB]), p.sb("rstd", [P, NB])
            if layer == 0:
                rw1, rw2 = p.sb("rw1", [P, C, HID]), p.sb("rw2", [P, HT, NE])
                rb1, hr = p.sb("rb1", [P, HT]), p.sb("hr", [P, HT, TOK])
                xn = hr[:, 0:NB, :]
            else:
                rw2 = p.sb("rw2", [P, C, NE])
                xn = p.sb("xn", [P, NB, D])
            rb2 = p.sb("rb2", [NE, 1])
            logitT = p.sb("logitT", [NE, TOK])
            logit = p.sb("logit", [P, NB, NE])
            best, bidx, bidf = p.sb("best", [P, NB, 8]), p.sb("bidx", [P, NB, 8], U32), p.sb("bidf", [P, NB, 8])
            gap, e2, e1 = p.sb("gap", [P, NB]), p.sb("e2", [P, NB]), p.sb("e1", [P, NB])
            prob = p.sb("prob", [P, NB, 2])
            number = p.sb("number", [P, NE])
            we, we2 = p.sb("we", [P, NB, NE]), p.sb("we2", [P, NB, NE])
            sel = p.sb("sel", [NE, NE, P])
            s_ = {n: p.sem(n) for n in ("w_in", "dstep", "var", "std", "xn", "turned", "xT", "xhi", "h_made", "h_read", "logits_made", "logits_kept", "logits",
                                        "gap", "e2", "we", "we_turned", "weT", "weB_made", "filled", "selected")}
            with nc.Block() as block:
                @block.sync
                def _(sp):
                    if layer == 0:
                        sp.dma_start(rb1[:], t["L0_ffn_rb1"]).then_inc(s_["w_in"], 16)
                        sp.dma_start(rw1[:], t["L0_ffn_rw1"]).then_inc(s_["w_in"], 16)
                        sp.dma_start(rw2[:], t["L0_ffn_rw2"]).then_inc(s_["w_in"], 16)
                        sp.dma_start(rb2[:], t["L0_ffn_rb2"].rearrange("(e o) -> e o", o=1)).then_inc(s_["w_in"], 16)
                        sp.dma_start(b1[:], t["L0_ffn_b1"]).then_inc(prep_done["b_in"], 16)
                        sp.dma_start(b2[:], t["L0_ffn_b2"]).then_inc(prep_done["b_in"], 16)
                    else:
                        sp.dma_start(rw2[:], t["L1_ffn_router_w"]).then_inc(s_["w_in"], 16)
                        sp.dma_start(rb2[:], t["L1_ffn_router_b"].rearrange("(e o) -> e o", o=1)).then_inc(s_["w_in"], 16)
                    for i, w in enumerate(names):
                        sp.dma_start(wraw[i][:], t[w][0]).then_inc(w_in[i], 16)
                    for i, w in enumerate(names):
                        sp.wait_ge(wlo_ready, i + 2)
                        sp.dma_start(wraw[i][:], t[w][1]).then_inc(w_in[i], 16)

                @block.gpsimd
                def _(pool):
                    nc.gpsimd.memset(sel[:], 1.0).then_inc(s_["filled"], 1)
                    nc.gpsimd.iota(number[:], pattern=[[1, NE]], base=0, channel_multiplier=0,
                                   allow_small_or_imprecise_dtypes=True).then_inc(s_["filled"], 1)
                    pool.wait_ge(s_["filled"], 2)
                    nc.gpsimd.affine_select(out=sel[:], in_=sel[:], compare_op=ALU.is_equal, fill=0.0, base=0,
                                            pattern=[[-1, NE], [0, P]], channel_multiplier=1).then_inc(s_["selected"], 1)
                    if layer == 1:
                        nc.gpsimd.memset(b2[:], 0.0).then_inc(prep_done["b_in"], 16)
                    prime(pool, wlo_ready)
                    for i in range(NW):
                        pool.wait_ge(whi_ready, i + 1)
                        nc.gpsimd.tensor_tensor(wlo[i][:, 0, :], wraw[i][:], f32(whi[i][:, 0, :]), ALU.subtract) \
                            .then_inc(wlo_ready, 1)

                @block.tensor
                def _(pe):
                    for c in range(C):
                        pe.wait_ge(s_["xn"], NB)
                        if c >= 2:
                            pe.wait_ge(s_["xT"], c - 1)
                        for b in range(NB):
                            last = pe.transpose(ps[4 + c % 2][:, b * P:(b + 1) * P], xn[:, b, c * P:(c + 1) * P], k["ident"][:])
                        last.then_inc(s_["turned"], 1)
                    pe.wait_ge(s_["xT"], C)
                    pe.wait_ge(s_["w_in"], 64 if layer == 0 else 32)
                    if layer == 0:
                        for j in range(HT):
                            if j >= 2:
                                pe.wait_ge(s_["h_read"], j - 1)
                            for c in range(C):
                                last = pe.matmul(ps[4 + j % 2][:], rw1[:, c, j * P:(j + 1) * P], xT[:, c, :],
                                                 start=(c == 0), stop=(c == C - 1))
                            last.then_inc(s_["h_made"], 1)
                        pe.wait_ge(s_["h_read"], HT)
                    rows, n = (hr, HT) if layer == 0 else (xT, C)
                    for j in range(n):
                        last = pe.matmul(ps[6][0:NE, :], rw2[:, j, :], rows[:, j, :], start=(j == 0), stop=(j == n - 1))
                    last.then_inc(s_["logits_made"], 1)
                    pe.wait_ge(s_["logits_kept"], 1)
                    for b in range(NB):
                        last = pe.transpose(ps[7][:, b * NE:(b + 1) * NE], logitT[:, b * P:(b + 1) * P], k["ident"][0:NE, 0:NE])
                    last.then_inc(s_["logits"], 1)
                    pe.wait_ge(s_["we"], NB)
                    for b in range(NB):
                        last = pe.transpose(ps[7][0:NE, b * P:(b + 1) * P], we[:, b, :], k["ident"][:])
                    last.then_inc(s_["we_turned"], 1)
                    pe.wait_ge(s_["weT"], 1)
                    pe.wait_ge(s_["selected"], 1)
                    for e in range(NE):
                        if e >= 2:
                            pe.wait_ge(prep_done["weB_ready"], e - 1)
                        pe.matmul(ps[4 + e % 2][:], sel[:, e, :], weT[:], start=True, stop=True).then_inc(s_["weB_made"], 1)

                @block.scalar
                def _(act):
                    act.wait_ge(s_["var"], 1)
                    nc.scalar.sqrt(std[:], ve[:]).then_inc(s_["std"], 1)
                    for c in range(C):
                        act.wait_ge(s_["xT"], c + 1)
                        nc.scalar.copy(xhi[:, c, :], xT[:, c, :]).then_inc(s_["xhi"], 1)
                    for i in range(NW):
                        act.wait_ge(w_in[i], 16)
                        nc.scalar.copy(whi[i][:, 0, :], wraw[i][:]).then_inc(whi_ready, 1)
                    if layer == 0:
                        act.wait_ge(s_["w_in"], 64)
                        for j in range(HT):
                            act.wait_ge(s_["h_made"], j + 1)
                            nc.scalar.activation(hr[:, j, :], ps[4 + j % 2][:], ACT.Silu, bias=rb1[:, j:j + 1]) \
                                .then_inc(s_["h_read"], 1)
                    act.wait_ge(s_["gap"], 1)
                    nc.scalar.activation(e2[:], gap[:], ACT.Exp).then_inc(s_["e2"], 1)
                    for e in range(NE):
                        act.wait_ge(s_["weB_made"], e + 1)
                        nc.scalar.copy(weB[:, e, :], ps[4 + e % 2][:]).then_inc(prep_done["weB_ready"], 1)

                @block.vector
                def _(dve):
                    s = Steps(dve, s_["dstep"])
                    for b in range(NB):
                        s.mark(nc.vector.bn_stats(stats[:, b, :], x[:, b, :]))
                    s.wait()
                    for b in range(NB):
                        s.mark(nc.vector.bn_aggr(mv[:, b, :], stats[:, b, :]))
                    s.wait()
                    nc.vector.tensor_scalar_add(ve[:], mv[:, :, 1], LN_EPS).then_inc(s_["var"], 1)
                    dve.wait_ge(s_["std"], 1)
                    s.then(nc.vector.reciprocal(rstd[:], std[:]))
                    for b in range(NB):
                        nc.vector.tensor_scalar(xn[:, b, :], x[:, b, :], mv[:, b, 0:1], rstd[:, b:b + 1],
                                                ALU.subtract, ALU.mult).then_inc(s_["xn"], 1)
                    for c in range(C):
                        dve.wait_ge(s_["turned"], c + 1)
                        nc.vector.tensor_copy(xT[:, c, :], ps[4 + c % 2][:]).then_inc(s_["xT"], 1)
                    for c in range(C):
                        dve.wait_ge(s_["xhi"], c + 1)
                        nc.vector.tensor_tensor(xlo[:, c, :], xT[:, c, :], f32(xhi[:, c, :]), ALU.subtract) \
                            .then_inc(prep_done["xlo_ready"], 1)
                    dve.wait_ge(s_["w_in"], 64 if layer == 0 else 32)
                    dve.wait_ge(s_["logits_made"], 1)
                    nc.vector.tensor_scalar(logitT[:], ps[6][0:NE, :], rb2[:, 0:1], None, ALU.add).then_inc(s_["logits_kept"], 1)
                    dve.wait_ge(s_["logits"], 1)
                    s.then(nc.vector.tensor_copy(logit[:].rearrange("p b e -> p (b e)"), ps[7][:, 0:NB * NE]))
                    for b in range(NB):
                        s.mark(nc.vector.max(best[:, b, :], logit[:, b, :]))
                    s.wait()
                    for b in range(NB):
                        s.mark(nc.vector.max_index(bidx[:, b, :], best[:, b, :], logit[:, b, :]))
                    s.wait()
                    s.mark(nc.vector.tensor_copy(bidf[:], bidx[:]))
                    nc.vector.tensor_tensor(gap[:], best[:, :, 1], best[:, :, 0], ALU.subtract).then_inc(s_["gap"], 1)
                    dve.wait_ge(s_["e2"], 1)
                    s.then(nc.vector.tensor_scalar_add(e1[:], e2[:], 1.0))
                    s.then(nc.vector.reciprocal(prob[:, :, 0], e1[:]))
                    s.then(nc.vector.tensor_tensor(prob[:, :, 1], e2[:], prob[:, :, 0], ALU.mult))
                    dve.wait_ge(s_["filled"], 2)
                    for b in range(NB):
                        s.mark(nc.vector.tensor_scalar(we2[:, b, :], number[:], bidf[:, b, 1:2], prob[:, b, 1:2], ALU.is_equal, ALU.mult))
                        s.mark(nc.vector.tensor_scalar(we[:, b, :], number[:], bidf[:, b, 0:1], prob[:, b, 0:1], ALU.is_equal, ALU.mult))
                    s.wait()
                    for b in range(NB):
                        nc.vector.tensor_tensor(we[:, b, :], we[:, b, :], we2[:, b, :], ALU.add).then_inc(s_["we"], 1)
                    dve.wait_ge(s_["we_turned"], 1)
                    nc.vector.tensor_copy(weT[:], ps[7][0:NE, :]).then_inc(s_["weT"], 1)
        STEP = 1 if layer == 0 else 2
        G = STEP * GR
        TS = G * C
        NS = NE // STEP
        act_h, wh = m.sb("act_h", [P, 2, TOK]), m.sb("wh", [P, 2, TOK])
        hhi, hlo = m.sb("hhi", [P, 2, TOK], F32R), m.sb("hlo", [P, 2, TOK], F32R)
        s_ = {n: m.sem("x" + n) for n in ("h_made", "h_read", "silu", "wh", "hhi", "hlo", "y_tile", "out", "stored")}
        up = 1 if layer == 1 else 0

        with nc.Block() as block:
            @block.sync
            def _(sp):
                def body(e, more):
                    for g in range(2, G + 2 if more else G):
                        for i in range(NW):
                            sp.wait_ge(wlo_ready, NW * (e * G + g - 1) + i + 2)
                            sp.dma_start(wraw[i][:], t[names[i]][bass.ds(e * G + g, 1)].rearrange("o p n -> (o p) n")) \
                                .then_inc(w_in[i], 16)

                turns(sp, NS, body)
                for b in range(NB):
                    sp.wait_ge(s_["out"], b + 1)
                    sp.dma_start(x_out[b], x[:, b, :]).then_inc(s_["stored"], 16)
                sp.wait_ge(s_["stored"], 16 * NB)

            @block.gpsimd
            def _(pool):
                def body(e, more):
                    for g in range(1, G + 1 if more else G):
                        for i in range(NW):
                            pool.wait_ge(whi_ready, NW * (e * G + g) + i + 1)
                            nc.gpsimd.tensor_tensor(wlo[i][:, g % 2, :], wraw[i][:], f32(whi[i][:, g % 2, :]), ALU.subtract) \
                                .then_inc(wlo_ready, 1)

                turns(pool, NS, body)

            @block.tensor
            def _(pe):
                pe.wait_ge(prep_done["b_in"], 32 if layer == 0 else 16)
                for b in range(NB):
                    pe.matmul(Y[b][:], weT[:, b * P:(b + 1) * P], b2[:], start=True, stop=False, skip_group_check=True)
                prime(pe, s_["y_tile"])

                def hidden(e, j):
                    g, r = j // C, j % C
                    if r == 0:
                        pe.wait_ge(wlo_ready, NW * (e * G + g) + NW)
                    pe.wait_ge(s_["h_read"] if up else s_["silu"], e * TS + max(j, 1))
                    for i in range(1 + up):
                        bank = ps[4 + (j % 2) * (1 + up) + i]
                        for c in range(C):
                            at = c * D + r * P
                            ins = three_products(pe, bank[:], whi[i][:, g % 2, at:at + P], wlo[i][:, g % 2, at:at + P],
                                                 xhi[:, c, :], xlo[:, c, :], c == 0, c == C - 1)
                    ins.then_inc(s_["h_made"], 1)

                def output(e, j, closes):
                    g, r = j // C, j % C
                    if r == 0:
                        pe.wait_ge(wlo_ready, NW * (e * G + g) + NW + 1)
                    pe.wait_ge(s_["hlo"], e * TS + j + 1)
                    for b in range(NB):
                        ins = three_products(pe, Y[b][:], hhi[:, j % 2, b * P:(b + 1) * P], hlo[:, j % 2, b * P:(b + 1) * P],
                                             whi[-1][:, g % 2, r * D:(r + 1) * D], wlo[-1][:, g % 2, r * D:(r + 1) * D],
                                             False, closes, check=False)
                    ins.then_inc(s_["y_tile"], 1)

                def body(e, more):
                    for j in range(TS):
                        if j + 1 < TS:
                            hidden(e, j + 1)
                        elif more:
                            hidden(e + 1, 0)
                        output(e, j, not more and j == TS - 1)

                hidden(0, 0)
                turns(pe, NS, body)

            @block.scalar
            def _(act):
                prime(act, s_["silu"])

                def split(e, g, i):
                    act.wait_ge(w_in[i], 16 * (e * G + g) + 16)
                    if i == NW - 1:
                        act.wait_ge(s_["y_tile"], (e * G + g - 1) * C + 1)
                    nc.scalar.copy(whi[i][:, g % 2, :], wraw[i][:]).then_inc(whi_ready, 1)

                def body(e, more):
                    for j in range(TS):
                        g, r = j // C, j % C
                        act.wait_ge(s_["h_made"], e * TS + j + 1)
                        act.wait_ge(s_["wh"], e * TS + max(j, 1))
                        bank = ps[4 + (j % 2) * (1 + up)]
                        if layer == 0:
                            nc.scalar.activation(act_h[:, j % 2, :], bank[:], ACT.Silu, bias=b1[:, bass.ds(e * HT + j, 1)]) \
                                .then_inc(s_["silu"], 1)
                        else:
                            nc.scalar.activation(act_h[:, j % 2, :], bank[:], ACT.Silu).then_inc(s_["silu"], 1)
                        act.wait_ge(s_["wh"], e * TS + j + 2)
                        act.wait_ge(s_["y_tile"], e * TS + max(j, 1))
                        nc.scalar.copy(hhi[:, j % 2, :], wh[:, j % 2, :]).then_inc(s_["hhi"], 1)
                        if r < NW and (more or g < G - 1):
                            if g + 1 < G:
                                split(e, g + 1, r)
                            else:
                                split(e + 1, 0, r)

                turns(act, NS, body)

            @block.vector
            def _(dve):
                prime(dve, s_["wh"], s_["h_read"])

                def body(e, more):
                    for j in range(TS):
                        g = j // C
                        weight = weB[:, bass.ds(e * STEP + (g if layer else 0), 1), :].rearrange("p o t -> p (o t)")
                        dve.wait_ge(s_["silu"], e * TS + j + 2)
                        if layer == 0:
                            nc.vector.tensor_tensor(wh[:, j % 2, :], act_h[:, j % 2, :], weight, ALU.mult).then_inc(s_["wh"], 1)
                        else:
                            nc.vector.tensor_tensor(act_h[:, j % 2, :], act_h[:, j % 2, :], ps[4 + (j % 2) * 2 + 1][:], ALU.mult) \
                                .then_inc(s_["h_read"], 1)
                            dve.wait_ge(s_["h_read"], e * TS + j + 2)
                            nc.vector.tensor_tensor(wh[:, j % 2, :], act_h[:, j % 2, :], weight, ALU.mult).then_inc(s_["wh"], 1)
                        dve.wait_ge(s_["hhi"], e * TS + j + 1)
                        nc.vector.tensor_tensor(hlo[:, j % 2, :], wh[:, j % 2, :], f32(hhi[:, j % 2, :]), ALU.subtract) \
                            .then_inc(s_["hlo"], 1)

                turns(dve, NS, body)
                dve.wait_ge(s_["y_tile"], NE * HT + 1)
                for b in range(NB):
                    nc.vector.tensor_tensor(x[:, b, :], x[:, b, :], Y[b][:], ALU.add).then_inc(s_["out"], 1)


def stage_rwkv(nc, k, t, x, x_out):
    with ExitStack() as ctx:
        m = Mem(nc, ctx, "rwkv")
        z, zn = m.sb("z", [P, NB, D]), m.sb("zn", [P, NB, D])
        zT = m.sb("zT", [P, C, NB, P])
        prev = m.sb("prev", [P, C, NB, P])
        mixed = [m.sb(f"mixed{i}", [P, C, NB, P]) for i in range(3)]
        w = [m.sb(f"w{i}", [P, C, D]) for i in range(4)]
        cols = m.sb("cols", [P, 6, C])
        one_minus = m.sb("one_minus", [P, 3, C])
        decay = m.sb("decay", [P, C])
        vT = m.sb("vT", [P, C, TOK])
        kv = m.sb("kv", [P, C, NB, P])
        state = m.sb("state", [P, C, NB, P])
        rate = m.sb("rate", [P, C, P])
        r = m.sb("r", [P, NB, D])
        stats, mv = m.sb("stats", [P, NB, 6]), m.sb("mv", [P, NB, 2])
        ve, std, rstd = m.sb("ve", [P, 2, NB]), m.sb("std", [P, 2, NB]), m.sb("rstd", [P, 2, NB])
        names = ("ln_w", "ln_b", "tmk", "tmv", "tmr", "decay_w")
        s_ = {n: m.sem(n) for n in ("c_in", "w_in", "dstep", "var", "std", "zn", "turned", "zT", "decay", "mixed", "v_made",
                                    "vT", "k_made", "kv", "state", "r_made", "r", "o_made", "rate", "done", "stored")}
        ps = k["ps"]
        with nc.Block() as block:
            @block.sync
            def _(sp):
                for i, n in enumerate(names):
                    sp.dma_start(cols[:, i, :], t["L1_attn_" + n]).then_inc(s_["c_in"], 16)
                for i, n in enumerate(("Wv", "Wk", "Wr", "Wo")):
                    sp.dma_start(w[i][:], t["L1_attn_" + n]).then_inc(s_["w_in"], 16)
                if x_out is not None:
                    sp.wait_ge(s_["done"], NB)
                    sp.dma_start(x_out.rearrange("b p d -> p b d"), x[:]).then_inc(s_["stored"], 16)
                    sp.wait_ge(s_["stored"], 16)

            @block.tensor
            def _(pe):
                for c in range(C):
                    pe.wait_ge(s_["zn"], NB)
                    if c >= 2:
                        pe.wait_ge(s_["zT"], c - 1)
                    for b in range(NB):
                        last = pe.transpose(ps[c % 2][:, b * P:(b + 1) * P], zn[:, b, c * P:(c + 1) * P], k["ident"][:])
                    last.then_inc(s_["turned"], 1)
                pe.wait_ge(s_["w_in"], 64)
                flat = [x_[:].rearrange("p c b t -> p c (b t)") for x_ in mixed]
                pe.wait_ge(s_["zT"], C)
                for i, (src, made, banks) in enumerate(((1, "v_made", (2, 3, 4, 5)), (0, "k_made", (6, 7, 0, 1)))):
                    pe.wait_ge(s_["mixed"], C * (i + 1))
                    for o in range(C):
                        for c in range(C):
                            last = pe.matmul(ps[banks[o]][:], w[i][:, c, o * P:(o + 1) * P], flat[src][:, c, :],
                                             start=(c == 0), stop=(c == C - 1))
                        last.then_inc(s_[made], 1)
                pe.wait_ge(s_["vT"], C)
                pe.wait_ge(s_["mixed"], 3 * C)
                for b in range(NB):
                    for c in range(C):
                        last = pe.matmul(ps[2 + b][:], mixed[2][:, c, b, :], w[2][:, c, :], start=(c == 0), stop=(c == C - 1))
                    last.then_inc(s_["r_made"], 1)
                pe.wait_ge(s_["state"], C * NB)
                for b in range(NB):
                    for c in range(C):
                        last = pe.matmul(ps[(6 + b) % 8][:], state[:, c, b, :], w[3][:, c, :], start=(c == 0), stop=(c == C - 1))
                    last.then_inc(s_["o_made"], 1)

            @block.scalar
            def _(act):
                for i in range(2):
                    act.wait_ge(s_["var"], i + 1)
                    nc.scalar.sqrt(std[:, i, :], ve[:, i, :]).then_inc(s_["std"], 1)
                act.wait_ge(s_["c_in"], 16 * len(names))
                nc.scalar.activation(decay[:], cols[:, 5, :], ACT.Sigmoid).then_inc(s_["decay"], 1)
                for o in range(C):
                    act.wait_ge(s_["v_made"], o + 1)
                    nc.scalar.copy(vT[:, o, :], ps[2 + o][:]).then_inc(s_["vT"], 1)
                for b in range(NB):
                    act.wait_ge(s_["r_made"], b + 1)
                    nc.scalar.activation(r[:, b, :], ps[2 + b][:], ACT.Sigmoid).then_inc(s_["r"], 1)

            @block.gpsimd
            def _(pool):
                nc.gpsimd.memset(prev[:, :, :, 0:1], 0.0).then_inc(s_["rate"], 1)
                pool.wait_ge(s_["decay"], 1)
                nc.gpsimd.tensor_copy(rate[:], decay[:].unsqueeze(2).to_broadcast([P, C, P])).then_inc(s_["rate"], 1)

            @block.vector
            def _(dve):
                s = Steps(dve, s_["dstep"])
                for i, (src, dst) in enumerate(((x, z), (z, zn))):
                    for b in range(NB):
                        s.mark(nc.vector.bn_stats(stats[:, b, :], src[:, b, :]))
                    s.wait()
                    for b in range(NB):
                        s.mark(nc.vector.bn_aggr(mv[:, b, :], stats[:, b, :]))
                    s.wait()
                    nc.vector.tensor_scalar_add(ve[:, i, :], mv[:, :, 1], LN_EPS).then_inc(s_["var"], 1)
                    dve.wait_ge(s_["std"], i + 1)
                    s.then(nc.vector.reciprocal(rstd[:, i, :], std[:, i, :]))
                    for b in range(NB):
                        ins = nc.vector.tensor_scalar(dst[:, b, :], src[:, b, :], mv[:, b, 0:1], rstd[:, i, b:b + 1],
                                                      ALU.subtract, ALU.mult)
                        if i:
                            ins.then_inc(s_["zn"], 1)
                        else:
                            s.mark(ins)
                    if not i:
                        s.wait()
                dve.wait_ge(s_["c_in"], 16 * len(names))
                s.mark(nc.vector.tensor_scalar(one_minus[:], cols[:, 2:5, :], -1.0, 1.0, ALU.mult, ALU.add))
                for c in range(C):
                    dve.wait_ge(s_["turned"], c + 1)
                    nc.vector.tensor_scalar(zT[:, c].rearrange("p b t -> p (b t)"), ps[c % 2][:], cols[:, 0, c:c + 1],
                                            cols[:, 1, c:c + 1], ALU.mult, ALU.add).then_inc(s_["zT"], 1)
                dve.wait_ge(s_["zT"], C)
                dve.wait_ge(s_["rate"], 1)
                for i in (1, 0, 2):
                    for c in range(C):
                        s.mark(nc.vector.tensor_scalar(prev[:, c, :, 1:P], zT[:, c, :, 0:P - 1], one_minus[:, i, c:c + 1],
                                                       None, ALU.mult))
                    s.wait()
                    for c in range(C):
                        nc.vector.scalar_tensor_tensor(out=mixed[i][:, c], in0=zT[:, c], scalar=cols[:, 2 + i, c:c + 1],
                                                       in1=prev[:, c], op0=ALU.mult, op1=ALU.add).then_inc(s_["mixed"], 1)
                    dve.wait_ge(s_["mixed"], C * {1: 1, 0: 2, 2: 3}[i])
                for o in range(C):
                    dve.wait_ge(s_["k_made"], o + 1)
                    dve.wait_ge(s_["vT"], o + 1)
                    nc.vector.tensor_tensor(kv[:, o].rearrange("p b t -> p (b t)"), vT[:, o, :], ps[(6 + o) % 8][:], ALU.mult) \
                        .then_inc(s_["kv"], 1)
                dve.wait_ge(s_["rate"], 2)
                dve.wait_ge(s_["kv"], C)
                for o in range(C):
                    for b in range(NB):
                        nc.vector.tensor_tensor_scan(state[:, o, b, :], rate[:, o, :], kv[:, o, b, :], 0.0, ALU.mult, ALU.add) \
                            .then_inc(s_["state"], 1)
                for b in range(NB):
                    s.mark(nc.vector.tensor_tensor(x[:, b, :], x[:, b, :], z[:, b, :], ALU.add))
                for b in range(NB):
                    dve.wait_ge(s_["o_made"], b + 1)
                    dve.wait_ge(s_["r"], b + 1)
                    s.mark(nc.vector.tensor_tensor(r[:, b, :], r[:, b, :], ps[(6 + b) % 8][:], ALU.mult))
                s.wait()
                for b in range(NB):
                    nc.vector.tensor_tensor(x[:, b, :], x[:, b, :], r[:, b, :], ALU.add).then_inc(s_["done"], 1)




def build(nc, t, out, stages=99):
    def dram(name, shape, dt=F32):
        return nc.dram_tensor(name, shape, dt, kind="Internal").ap()

    x_mid = dram("x_mid", (NB, P, D))
    q_hi, q_lo = dram("q_hi", (NB, P, C, P)), dram("q_lo", (NB, P, C, P))
    with ExitStack() as ctx:
        k = {
            "ident": ctx.enter_context(nc.sbuf_tensor("ident", [P, P], F32)),
            "ones": ctx.enter_context(nc.sbuf_tensor("ones", [P, P], F32)),
        }
        k["ps2"] = [ctx.enter_context(nc.psum_tensor(f"wide{i}", [P, 2 * 512], F32)) for i in range(2)]
        one = [ctx.enter_context(nc.psum_tensor(f"bank{i}", [P, 512], F32)) for i in range(4, 8)]
        k["ps"] = [k["ps2"][0][:, 0:512], k["ps2"][0][:, 512:1024], k["ps2"][1][:, 0:512], k["ps2"][1][:, 512:1024]] \
            + [x[:, :] for x in one]
        stage_constants(nc, k)

        rows = ctx.enter_context(nc.sbuf_tensor("rows", [P, NB, D], F32))

        def cross(layer, x_saved, rows_hold_x, x_out, mask):
            L = f"L{layer}_xattn_"
            with ExitStack() as inner:
                weights = [tuple(inner.enter_context(nc.sbuf_tensor(f"{L}{w}_{p}", [P, C * D], F32R))
                                 for p in ("hi", "lo")) for w in ("wk", "wv")]
                stage_project_q(nc, k, f"q{layer}", rows, None if rows_hold_x else x_saved, t[L + "Wq"], t[L + "bq"],
                                t[L + "Wk"], t[L + "Wv"], weights, q_hi, q_lo, mask)
                stage_attention(nc, k, f"a{layer}", t["ctx_1024"], weights, t[L + "bk"], q_hi, q_lo, rows,
                                t["mask_turned"] if mask is not None else None)
            norm = layer == 1
            stage_attention_output(nc, k, f"o{layer}", rows, t[L + "bv"], t[L + "Wo"], t[L + "bo"],
                                   t[L + "gamma"] if norm else None, t[L + "beta"] if norm else None, x_saved, x_out)

        def last(i):
            return out if stages == i else None

        cross(0, t["x"], False, last(1), t["mask_1x1xSxS2_bk0"])
        if stages >= 2:
            stage_retention(nc, k, t, rows, last(2))
        if stages >= 3:
            stage_experts(nc, k, "moe0", t, rows, last(3) if stages == 3 else x_mid, 0)
        if stages >= 4:
            cross(1, x_mid, True, last(4), None)
        if stages >= 5:
            stage_rwkv(nc, k, t, rows, last(5))
        if stages >= 6:
            stage_experts(nc, k, "moe1", t, rows, out, 1)


def _tiles(a):
    return a.reshape(-1, P, a.shape[-1]).transpose(1, 0, 2)


def _columns(a):
    return a.reshape(-1, P).T


def _layout(name, a):
    if name == "ctx_1024":
        return a.reshape(NB, KEYS // CH, CH, C, P).transpose(0, 1, 4, 3, 2).reshape(NB * KEYS // CH, P, C * CH)
    if name == "mask_turned":
        return a.reshape(P, KT, P).transpose(2, 1, 0).reshape(P, KEYS)
    if name == "mask_1x1xSxS2_bk0":
        return a.reshape(P, KEYS)
    if "_xattn_W" in name or name in ("L1_attn_Wk", "L1_attn_Wv", "L1_attn_Wr", "L1_attn_Wo"):
        w = _tiles(a.T)
        return w.reshape(P, C * D) if name.endswith(("_Wk", "_Wv")) and "xattn" in name else w
    if name in ("L0_attn_w_attn", "L0_attn_w_proj", "L0_ffn_rw1", "L0_ffn_rw2", "L1_ffn_router_w"):
        return _tiles(a)
    if name == "L0_ffn_w1":
        return a.reshape(NE, C, P, C, D).transpose(0, 3, 2, 1, 4).reshape(NE * C, P, C * D)
    if name == "L0_ffn_w2":
        return a.reshape(NE, C, C, P, D).transpose(0, 1, 3, 2, 4).reshape(NE * C, P, C * D)
    if name in ("L1_ffn_we_gate", "L1_ffn_we_up", "L1_ffn_we_down"):
        return a.reshape(NE, C, P, D).transpose(0, 2, 1, 3).reshape(NE, P, C * D)
    if name == "L0_ffn_b1":
        return a.reshape(NE, HID // P, P).transpose(2, 0, 1).reshape(P, NE * HID // P)
    if name in ("L0_xattn_bq", "L0_xattn_bk", "L1_xattn_bq", "L1_xattn_bk", "L0_ffn_rb1", "L1_attn_ln_w", "L1_attn_ln_b",
                "L1_attn_tmk", "L1_attn_tmv", "L1_attn_tmr", "L1_attn_decay_w"):
        return _columns(a)
    return a


def _rotary():
    div = (2.0 * np.pi / float(P) ** (np.arange(0, RD, 2, dtype=np.float32) / RD)).astype(np.float32)
    ang = (np.arange(P, dtype=np.float32)[:, None] * div[None, :]).astype(np.float32)
    cos = np.repeat(np.cos(ang), 2, axis=-1)
    sin = np.repeat(np.sin(ang), 2, axis=-1)
    sin[:, 0::2] *= -1.0
    return np.stack([cos, sin], 1).astype(np.float32)


def kernel(**inputs):
    import concourse.bacc as _bacc
    from concourse import mybir as _mybir
    from concourse.bass_utils import run_bass_kernel_spmd as _run

    nc = _bacc.Bacc("TRN2", target_bir_lowering=False, num_devices=1)
    arrays, t = {}, {}
    inputs = dict(inputs, rotary=_rotary(), mask_turned=inputs["mask_1x1xSxS2_bk0"])
    for name, a in inputs.items():
        a = np.ascontiguousarray(_layout(name, np.asarray(a)))
        arrays[f"in_{name}"] = a
        t[name] = nc.dram_tensor(f"in_{name}", a.shape, _mybir.dt.from_np(a.dtype), kind="ExternalInput").ap()
    out = nc.dram_tensor("out_x", (NB, P, D), _mybir.dt.float32, kind="ExternalOutput").ap()
    build(nc, t, out, STAGES)
    r = _run(nc, [arrays], core_ids=[0])
    return r.results[0]["out_x"]


STAGES = 99
```
